# Optimizing a Trainium2 kernel written in Bass

```python
import numpy as np
import jax
import jax.numpy as jnp

def _softmax(x, axis=-1):
    return jax.nn.softmax(x, axis=axis)

def _gelu(x):
    return jax.nn.gelu(x, approximate=True)

def _silu(x):
    return jax.nn.silu(x)

def _sigmoid(x):
    return jax.nn.sigmoid(x)

def _layernorm(x, axis=-1, eps=1e-05):
    m = jnp.mean(x, axis=axis, keepdims=True)
    v = jnp.var(x, axis=axis, keepdims=True)
    return (x - m) / jnp.sqrt(v + eps)

def _scatter_add(tgt, idx, src, axis=0):
    return tgt.at[idx].add(src)

def _segment_sum(src, seg, n):
    return jax.ops.segment_sum(src, seg, n)
kernel_name = 'mk_sandwich_d2_jaxref_r8_501cb5'

def setup_inputs(seed: int=0):
    np.random.seed(seed)
    _w = jnp.asarray

    def _L0_attn_setup():
        import jax, jax.numpy as jnp
        import numpy as np
        H, DK, DV = (16, 64, 64)
        LN_EPS = 1e-05
        key = jax.random.key(seed)
        ks = jax.random.split(key, 5)
        B, N, D = (4, 512, 128)
        s = 1.0 / np.sqrt(D)
        return {'inputs': jax.random.normal(ks[0], (B, N, D), dtype=jnp.float32), 'W_Q': jax.random.normal(ks[1], (D, H * DK), dtype=jnp.float32) * s, 'W_K': jax.random.normal(ks[2], (D, H * DK), dtype=jnp.float32) * s, 'W_V': jax.random.normal(ks[3], (D, H * DV), dtype=jnp.float32) * s, 'W_fc': jax.random.normal(ks[4], (H * DV, D), dtype=jnp.float32) * s, 'gamma': jnp.ones((D,), dtype=jnp.float32), 'beta': jnp.zeros((D,), dtype=jnp.float32)}
    _L0_attn_in = _L0_attn_setup()

    def _L0_ffn_setup():
        import jax, jax.numpy as jnp
        import numpy as np
        D_IN, D_HID = (128, 512)

        def _ternary(key, shape):
            return jax.random.randint(key, shape, -1, 2).astype(jnp.float32)

        def _tlin(x, w, s):
            return jnp.einsum('bsi,oi->bso', x, w) * s
        key = jax.random.key(seed)
        ks = jax.random.split(key, 12)
        inv = lambda fan: 1.0 / np.sqrt(fan).astype(np.float32)
        return {'x': jax.random.normal(ks[0], (4, 256, D_IN), dtype=jnp.float32), 'w1_w': _ternary(ks[1], (D_HID, D_IN)), 'w1_s': jax.random.uniform(ks[2], (D_HID,), dtype=jnp.float32) * inv(D_IN), 'w2_w': _ternary(ks[3], (D_HID, D_IN)), 'w2_s': jax.random.uniform(ks[4], (D_HID,), dtype=jnp.float32) * inv(D_IN), 'h1_w': _ternary(ks[5], (D_HID, D_HID)), 'h1_s': jax.random.uniform(ks[6], (D_HID,), dtype=jnp.float32) * inv(D_HID), 'h2_w': _ternary(ks[7], (D_HID, D_HID)), 'h2_s': jax.random.uniform(ks[8], (D_HID,), dtype=jnp.float32) * inv(D_HID), 'w3_w': _ternary(ks[9], (D_IN, D_HID)), 'w3_s': jax.random.uniform(ks[10], (D_IN,), dtype=jnp.float32) * inv(D_HID)}
    _L0_ffn_in = _L0_ffn_setup()

    def _L1_attn_setup():
        import jax, jax.numpy as jnp
        import numpy as np
        import math
        _DENSE_LOCAL_W = 64
        _DYADIC = [96, 128, 192, 32, 48, 64, 96, 128, 192]
        OFFSETS = sorted(set(range(0, _DENSE_LOCAL_W + 1)) | set(_DYADIC))
        B, N, D, H = (1, 256, 128, 16)
        HD = D // H
        key = jax.random.key(seed)
        ks = jax.random.split(key, 8)
        s = 1.0 / math.sqrt(D)
        x = jax.random.normal(ks[0], (B, N, D), dtype=jnp.float32)
        Wqkv = jax.random.uniform(ks[1], (3 * D, D), jnp.float32, -s, s)
        bqkv = jax.random.uniform(ks[2], (3 * D,), jnp.float32, -s, s)
        Wgate = jax.random.uniform(ks[3], (D, D), jnp.float32, -s, s)
        bgate = jax.random.uniform(ks[4], (D,), jnp.float32, -s, s)
        Wout = jax.random.uniform(ks[5], (D, D), jnp.float32, -s, s)
        bout = jax.random.uniform(ks[6], (D,), jnp.float32, -s, s)
        alphas = jnp.linspace(0.2, 2.0, H)
        deltas = jnp.array([math.log(1.0 + d) for d in OFFSETS], dtype=jnp.float32)
        pos_bias = -deltas[:, None] * alphas[None, :]
        offsets = jnp.array(OFFSETS, dtype=jnp.int32)
        return {'x': x, 'Wqkv': Wqkv, 'bqkv': bqkv, 'Wgate': Wgate, 'bgate': bgate, 'Wout': Wout, 'bout': bout, 'pos_bias': pos_bias, 'offsets': offsets}
    _L1_attn_in = _L1_attn_setup()

    def _L1_ffn_setup():
        import jax, jax.numpy as jnp
        import numpy as np
        D_IN, D_HID = (128, 512)

        def _ternary(key, shape):
            return jax.random.randint(key, shape, -1, 2).astype(jnp.float32)

        def _tlin(x, w, s):
            return jnp.einsum('bsi,oi->bso', x, w) * s
        key = jax.random.key(seed)
        ks = jax.random.split(key, 12)
        inv = lambda fan: 1.0 / np.sqrt(fan).astype(np.float32)
        return {'x': jax.random.normal(ks[0], (4, 256, D_IN), dtype=jnp.float32), 'w1_w': _ternary(ks[1], (D_HID, D_IN)), 'w1_s': jax.random.uniform(ks[2], (D_HID,), dtype=jnp.float32) * inv(D_IN), 'w2_w': _ternary(ks[3], (D_HID, D_IN)), 'w2_s': jax.random.uniform(ks[4], (D_HID,), dtype=jnp.float32) * inv(D_IN), 'h1_w': _ternary(ks[5], (D_HID, D_HID)), 'h1_s': jax.random.uniform(ks[6], (D_HID,), dtype=jnp.float32) * inv(D_HID), 'h2_w': _ternary(ks[7], (D_HID, D_HID)), 'h2_s': jax.random.uniform(ks[8], (D_HID,), dtype=jnp.float32) * inv(D_HID), 'w3_w': _ternary(ks[9], (D_IN, D_HID)), 'w3_s': jax.random.uniform(ks[10], (D_IN,), dtype=jnp.float32) * inv(D_HID)}
    _L1_ffn_in = _L1_ffn_setup()
    _d = {'L0_attn_inputs': _L0_attn_in['inputs'], 'L0_attn_W_Q': _L0_attn_in['W_Q'], 'L0_attn_W_K': _L0_attn_in['W_K'], 'L0_attn_W_V': _L0_attn_in['W_V'], 'L0_attn_W_fc': _L0_attn_in['W_fc'], 'L0_attn_gamma': _L0_attn_in['gamma'], 'L0_attn_beta': _L0_attn_in['beta'], 'L0_ffn_w1_w': _L0_ffn_in['w1_w'], 'L0_ffn_w1_s': _L0_ffn_in['w1_s'], 'L0_ffn_w2_w': _L0_ffn_in['w2_w'], 'L0_ffn_w2_s': _L0_ffn_in['w2_s'], 'L0_ffn_h1_w': _L0_ffn_in['h1_w'], 'L0_ffn_h1_s': _L0_ffn_in['h1_s'], 'L0_ffn_h2_w': _L0_ffn_in['h2_w'], 'L0_ffn_h2_s': _L0_ffn_in['h2_s'], 'L0_ffn_w3_w': _L0_ffn_in['w3_w'], 'L0_ffn_w3_s': _L0_ffn_in['w3_s'], 'L1_attn_Wqkv': _L1_attn_in['Wqkv'], 'L1_attn_bqkv': _L1_attn_in['bqkv'], 'L1_attn_Wgate': _L1_attn_in['Wgate'], 'L1_attn_bgate': _L1_attn_in['bgate'], 'L1_attn_Wout': _L1_attn_in['Wout'], 'L1_attn_bout': _L1_attn_in['bout'], 'L1_attn_pos_bias': _L1_attn_in['pos_bias'], 'L1_attn_offsets': _L1_attn_in['offsets'], 'L1_ffn_w1_w': _L1_ffn_in['w1_w'], 'L1_ffn_w1_s': _L1_ffn_in['w1_s'], 'L1_ffn_w2_w': _L1_ffn_in['w2_w'], 'L1_ffn_w2_s': _L1_ffn_in['w2_s'], 'L1_ffn_h1_w': _L1_ffn_in['h1_w'], 'L1_ffn_h1_s': _L1_ffn_in['h1_s'], 'L1_ffn_h2_w': _L1_ffn_in['h2_w'], 'L1_ffn_h2_s': _L1_ffn_in['h2_s'], 'L1_ffn_w3_w': _L1_ffn_in['w3_w'], 'L1_ffn_w3_s': _L1_ffn_in['w3_s']}
    _x0 = _d['L0_attn_inputs']
    _d['L0_attn_inputs'] = jax.random.normal(jax.random.fold_in(jax.random.key(seed), 1), (8, 1024, 128), dtype=_x0.dtype)
    del _x0
    return _d

def reference(L0_attn_inputs, L0_attn_W_Q, L0_attn_W_K, L0_attn_W_V, L0_attn_W_fc, L0_attn_gamma, L0_attn_beta, L0_ffn_w1_w, L0_ffn_w1_s, L0_ffn_w2_w, L0_ffn_w2_s, L0_ffn_h1_w, L0_ffn_h1_s, L0_ffn_h2_w, L0_ffn_h2_s, L0_ffn_w3_w, L0_ffn_w3_s, L1_attn_Wqkv, L1_attn_bqkv, L1_attn_Wgate, L1_attn_bgate, L1_attn_Wout, L1_attn_bout, L1_attn_pos_bias, L1_attn_offsets, L1_ffn_w1_w, L1_ffn_w1_s, L1_ffn_w2_w, L1_ffn_w2_s, L1_ffn_h1_w, L1_ffn_h1_s, L1_ffn_h2_w, L1_ffn_h2_s, L1_ffn_w3_w, L1_ffn_w3_s):

    def _L0_attn_ref(inputs, W_Q, W_K, W_V, W_fc, gamma, beta):
        import jax, jax.numpy as jnp
        import numpy as np
        H, DK, DV = (16, 64, 64)
        LN_EPS = 1e-05
        B, N, D = inputs.shape
        Q = jax.nn.sigmoid((inputs @ W_Q).reshape(B, N, H, DK))
        K = jax.nn.sigmoid((inputs @ W_K).reshape(B, N, H, DK))
        V = (inputs @ W_V).reshape(B, N, H, DV)
        KV = jnp.einsum('bnhk,bnhv->bhkv', K, V)
        num = jnp.einsum('bnhk,bhkv->bnhv', Q, KV)
        k_sum = K.sum(axis=1)
        den = jnp.einsum('bnhk,bhk->bnh', Q, k_sum)[..., None] + 1e-08
        out = (num / den).reshape(B, N, H * DV) @ W_fc
        x = out + inputs
        mu = x.mean(axis=-1, keepdims=True)
        var = jnp.mean((x - mu) ** 2, axis=-1, keepdims=True)
        return (x - mu) * jax.lax.rsqrt(var + LN_EPS) * gamma + beta

    def _L0_ffn_ref(x, w1_w, w1_s, w2_w, w2_s, h1_w, h1_s, h2_w, h2_s, w3_w, w3_s):
        import jax, jax.numpy as jnp
        import numpy as np
        D_IN, D_HID = (128, 512)

        def _ternary(key, shape):
            return jax.random.randint(key, shape, -1, 2).astype(jnp.float32)

        def _tlin(x, w, s):
            return jnp.einsum('bsi,oi->bso', x, w) * s
        h = jax.nn.silu(_tlin(x, w1_w, w1_s)) * _tlin(x, w2_w, w2_s)
        h = jax.nn.gelu(_tlin(h, h1_w, h1_s), approximate=False)
        h = jax.nn.gelu(_tlin(h, h2_w, h2_s), approximate=False)
        return _tlin(h, w3_w, w3_s)

    def _L1_attn_ref(x, Wqkv, bqkv, Wgate, bgate, Wout, bout, pos_bias, offsets):
        import jax, jax.numpy as jnp
        import numpy as np
        import math
        _DENSE_LOCAL_W = 64
        _DYADIC = [96, 128, 192, 32, 48, 64, 96, 128, 192]
        OFFSETS = sorted(set(range(0, _DENSE_LOCAL_W + 1)) | set(_DYADIC))
        B, N, D, H = (1, 256, 128, 16)
        HD = D // H
        Bx, Nx, Dx = x.shape
        qkv = x @ Wqkv.T + bqkv
        q, k, v = jnp.split(qkv, 3, axis=-1)
        q = q.reshape(Bx, Nx, H, HD).transpose(0, 2, 1, 3)
        k = k.reshape(Bx, Nx, H, HD).transpose(0, 2, 1, 3)
        v = v.reshape(Bx, Nx, H, HD).transpose(0, 2, 1, 3)
        scale = HD ** (-0.5)
        n_idx = jnp.arange(Nx, dtype=jnp.int32)[:, None]
        idx = n_idx - offsets[None, :]
        valid = idx >= 0
        idx_c = jnp.clip(idx, 0, Nx - 1)
        K_all = k[:, :, idx_c, :]
        V_all = v[:, :, idx_c, :]
        scores = jnp.einsum('bhnd,bhnod->bhno', q, K_all) * scale
        scores = scores + pos_bias.T[None, :, None, :]
        scores = jnp.where(valid[None, None], scores, -jnp.inf)
        alpha = jax.nn.softmax(scores, axis=-1)
        out = jnp.einsum('bhno,bhnod->bhnd', alpha, V_all)
        flat = out.transpose(0, 2, 1, 3).reshape(Bx, Nx, Dx)
        gate = jax.nn.sigmoid(x @ Wgate.T + bgate)
        return flat * gate @ Wout.T + bout

    def _L1_ffn_ref(x, w1_w, w1_s, w2_w, w2_s, h1_w, h1_s, h2_w, h2_s, w3_w, w3_s):
        import jax, jax.numpy as jnp
        import numpy as np
        D_IN, D_HID = (128, 512)

        def _ternary(key, shape):
            return jax.random.randint(key, shape, -1, 2).astype(jnp.float32)

        def _tlin(x, w, s):
            return jnp.einsum('bsi,oi->bso', x, w) * s
        h = jax.nn.silu(_tlin(x, w1_w, w1_s)) * _tlin(x, w2_w, w2_s)
        h = jax.nn.gelu(_tlin(h, h1_w, h1_s), approximate=False)
        h = jax.nn.gelu(_tlin(h, h2_w, h2_s), approximate=False)
        return _tlin(h, w3_w, w3_s)
    x = L0_attn_inputs
    x = x + _layernorm(_L0_attn_ref(_layernorm(x, axis=-1), L0_attn_W_Q, L0_attn_W_K, L0_attn_W_V, L0_attn_W_fc, L0_attn_gamma, L0_attn_beta), axis=-1)
    x = x + _layernorm(_L0_ffn_ref(_layernorm(x, axis=-1), L0_ffn_w1_w, L0_ffn_w1_s, L0_ffn_w2_w, L0_ffn_w2_s, L0_ffn_h1_w, L0_ffn_h1_s, L0_ffn_h2_w, L0_ffn_h2_s, L0_ffn_w3_w, L0_ffn_w3_s), axis=-1)
    x = x + _layernorm(_L1_attn_ref(_layernorm(x, axis=-1), L1_attn_Wqkv, L1_attn_bqkv, L1_attn_Wgate, L1_attn_bgate, L1_attn_Wout, L1_attn_bout, L1_attn_pos_bias, L1_attn_offsets), axis=-1)
    x = x + _layernorm(_L1_ffn_ref(_layernorm(x, axis=-1), L1_ffn_w1_w, L1_ffn_w1_s, L1_ffn_w2_w, L1_ffn_w2_s, L1_ffn_h1_w, L1_ffn_h1_s, L1_ffn_h2_w, L1_ffn_h2_s, L1_ffn_w3_w, L1_ffn_w3_s), axis=-1)
    return x

_drawn_inputs = setup_inputs


def setup_inputs(seed=0):
    import zlib

    import numpy as np

    out = dict(_drawn_inputs(seed))
    spreads = {'L0_attn_gamma': (1.0, 0.2), 'L0_attn_beta': (0.0, 0.1)}
    factors = {'L0_attn_W_Q': 34.072, 'L0_attn_W_K': 19.335, 'L1_attn_bgate': 7.339}
    for name, (base, spread) in spreads.items():
        noise = np.random.default_rng([zlib.crc32(name.encode()), seed]).standard_normal(out[name].shape)
        drawn = base * np.exp(spread * noise) if base else spread * noise
        out[name] = jnp.asarray(drawn.astype(out[name].dtype))
    for name, factor in factors.items():
        out[name] = (out[name] * factor).astype(out[name].dtype)
    return out
```

```python
import numpy as np
from contextlib import ExitStack

import concourse.bass as bass
from concourse import mybir

F32 = mybir.dt.float32
F32R = mybir.dt.float32r
I32 = mybir.dt.int32
ALU = mybir.AluOpType
ACT = mybir.ActivationFunctionType
AX = mybir.AxisListType

P = 128
B, N, D = 8, 1024, 128
NT = N // P
CH = 512
NC = N // CH
H0, DK = 16, 64
NF = H0 * DK // P
HID = 512
NB = HID // P
H1, HD = 16, 8
NG, GH = 4, 4
NOFF = 68
REACH = 192
WIN = P + REACH
TAB = P + WIN
EPS = 1e-5
DEN_EPS = 1e-8
FAR = 1e30


def f32(ap):
    return ap.bitcast(F32)


class Norm:

    def __init__(self, nc, sb, sem, tag, times):
        self.nc = nc
        self.stats = sb(f"{tag}_stats", [P, NT, 6])
        self.mean_var = [sb(f"{tag}_mean_var{k}", [P, NT, 2]) for k in range(times)]
        self.var_eps = sb(f"{tag}_var_eps", [P, NT])
        self.rstd = [sb(f"{tag}_rstd{k}", [P, NT]) for k in range(times)]
        self.stats_done = sem(f"{tag}_stats_done")
        self.moments_done = sem(f"{tag}_moments_done")
        self.eps_added = sem(f"{tag}_eps_added")
        self.rstd_ready = sem(f"{tag}_rstd_ready")

    def moments(self, dve, src, k):
        for t in range(NT):
            self.nc.vector.bn_stats(self.stats[:, t, :], src(t)).then_inc(self.stats_done, 1)
        dve.wait_ge(self.stats_done, NT * (k + 1))
        for t in range(NT):
            self.nc.vector.bn_aggr(self.mean_var[k][:, t, :], self.stats[:, t, :]).then_inc(self.moments_done, 1)

    def root(self, pool, minus_half, k):
        pool.wait_ge(self.moments_done, NT * (k + 1))
        self.nc.gpsimd.tensor_scalar(self.var_eps[:, :], self.mean_var[k][:, :, 1], EPS, None,
                                     ALU.add).then_inc(self.eps_added, 1)
        pool.wait_ge(self.eps_added, k + 1)
        self.nc.gpsimd.tensor_tensor(self.rstd[k][:, :], self.var_eps[:, :], minus_half,
                                     ALU.pow).then_inc(self.rstd_ready, 1)

    def apply(self, dve, out, src, k, done):
        dve.wait_ge(self.moments_done, NT * (k + 1))
        dve.wait_ge(self.rstd_ready, k + 1)
        for t in range(NT):
            self.nc.vector.tensor_scalar(out(t), src(t), self.mean_var[k][:, t, 0:1], self.rstd[k][:, t:t + 1],
                                         ALU.subtract, ALU.mult).then_inc(done, 1)


def split(nc, eng, hi, lo, x, done, base):
    nc.vector.tensor_copy(hi, x).then_inc(done, 1)
    eng.wait_ge(done, base + 1)
    nc.vector.tensor_tensor(lo, x, f32(hi), ALU.subtract).then_inc(done, 1)


def clear(nc, sems):
    with nc.Block() as block:
        @block.sync
        def _(sp):
            for s in sems:
                sp.sem_clear(s)


def linear_attention(nc, x_in, x_out, W_Q, W_K, W_VT, W_fc, gamma, beta, c_ident, c_headcol, c_headsel):
    with ExitStack() as ctx:
        def sb(name, shape, dt=F32):
            return ctx.enter_context(nc.sbuf_tensor("la_" + name, shape, dt))

        sems = []

        def sem(name):
            s = ctx.enter_context(nc.semaphore("la_" + name))
            sems.append(s)
            return s

        ps = ctx.enter_context(nc.psum_tensor("la_ps", [P, 8, CH], F32))

        ident = sb("ident", [P, P])
        wq_hi, wq_lo = sb("wq_hi", [P, H0 * DK], F32R), sb("wq_lo", [P, H0 * DK], F32R)
        wk_hi, wk_lo = sb("wk_hi", [P, H0 * DK], F32R), sb("wk_lo", [P, H0 * DK], F32R)
        wvt, wfc = sb("wvt", [P, NF, D]), sb("wfc", [P, NF, D])
        wvfc = sb("wvfc", [P, H0, D])
        headcol = sb("headcol", [P, NF, 32])
        headsel = sb("headsel", [P, NF, P], F32R)
        gamma_b, beta_b = sb("gamma_b", [P, D]), sb("beta_b", [P, D])
        minus_half = sb("minus_half", [P, NT])

        x = sb("x", [P, NT, D])
        xn = sb("xn", [P, NT, D + 1])
        xt_hi, xt_lo = sb("xt_hi", [P, N], F32R), sb("xt_lo", [P, N], F32R)
        kn = sb("kn", [P, 2, H0 * DK])
        kx = sb("kx", [P, NF, D + 1])
        ksum_col = sb("ksum_col", [P, NF, 32])
        kxt = sb("kxt", [P, NF, P])
        m = sb("m", [P, NF, D])
        q = sb("q", [P, NF, N])
        den = sb("den", [P, 256])
        rden = sb("rden", [P, 256])
        rden_hi, rden_lo = sb("rden_hi", [P, 4, 256], F32R), sb("rden_lo", [P, 4, 256], F32R)
        z = sb("z", [P, NT, D])
        norm = Norm(nc, sb, sem, "norm", 3)

        w_in = sem("w_in")
        w_ready = sem("w_ready")
        wvfc_mm = sem("wvfc_mm")
        x_loaded = sem("x_loaded")
        xn_ready = sem("xn_ready")
        xt_mm = sem("xt_mm")
        xt_hi_ready = sem("xt_hi_ready")
        xt_ready = sem("xt_ready")
        k_mm = sem("k_mm")
        k_ready = sem("k_ready")
        kx_mm = sem("kx_mm")
        kx_copied = sem("kx_copied")
        ksum_ready = sem("ksum_ready")
        kxt_mm = sem("kxt_mm")
        kxt_ready = sem("kxt_ready")
        m_mm = sem("m_mm")
        m_ready = sem("m_ready")
        q_mm = sem("q_mm")
        q_ready = sem("q_ready")
        den_mm = sem("den_mm")
        den_step = sem("den_step")
        rden_ready = sem("rden_ready")
        spread_mm = sem("spread_mm")
        qd_ready = sem("qd_ready")
        out_mm = sem("out_mm")
        z_ready = sem("z_ready")
        z_normed = sem("z_normed")
        affine = sem("affine")
        x_ready = sem("x_ready")
        stored = sem("stored")

        with nc.Block() as block:
            @block.sync
            def _(sp):
                sp.dma_start(q[:, 0, :], W_Q).then_inc(w_in, 16)
                sp.dma_start(q[:, 1, :], W_K).then_inc(w_in, 16)
                sp.dma_start(wvt[:, :, :], W_VT.rearrange("(f p) d -> p f d", p=P)).then_inc(w_in, 16)
                sp.dma_start(wfc[:, :, :], W_fc.rearrange("(f p) d -> p f d", p=P)).then_inc(w_in, 16)
                sp.dma_start(ident[:, :], c_ident).then_inc(w_in, 16)
                sp.dma_start(headcol[:, :, :], c_headcol.rearrange("p (f c) -> p f c", f=NF)).then_inc(w_in, 16)
                sp.dma_start(q[:, 2, :], c_headsel).then_inc(w_in, 16)
                sp.dma_start(gamma_b[:, :], gamma.rearrange("(a d) -> a d", a=1).broadcast_to([P, D])).then_inc(w_in, 16)
                sp.dma_start(beta_b[:, :], beta.rearrange("(a d) -> a d", a=1).broadcast_to([P, D])).then_inc(w_in, 16)

            @block.gpsimd
            def _(pool):
                nc.gpsimd.memset(minus_half[:, :], -0.5)
                nc.gpsimd.memset(xn[:, :, D:D + 1], 1.0)

            @block.vector
            def _(dve):
                nc.vector.memset(rden_hi[:, :, :].bitcast(F32), 0.0)
                nc.vector.memset(rden_lo[:, :, :].bitcast(F32), 0.0)
                dve.wait_ge(w_in, 9 * 16)
                split(nc, dve, wq_hi[:, :], wq_lo[:, :], q[:, 0, :], w_ready, 0)
                split(nc, dve, wk_hi[:, :], wk_lo[:, :], q[:, 1, :], w_ready, 2)
                nc.vector.tensor_copy(headsel[:, :, :].rearrange("p f c -> p (f c)"), q[:, 2, :])
                for n in range(H0 // 4):
                    dve.wait_ge(wvfc_mm, n + 1)
                    nc.vector.tensor_copy(wvfc[:, 4 * n:4 * n + 4, :].rearrange("p h d -> p (h d)"), ps[:, n, :])

            @block.tensor
            def _(pe):
                pe.wait_ge(w_in, 9 * 16)
                for n in range(H0):
                    s, f = n // NF, n % NF
                    mm = pe.matmul(ps[:, n // 4, (n % 4) * D:(n % 4 + 1) * D], wvt[64 * s:64 * s + 64, f, :],
                                   wfc[64 * s:64 * s + 64, f, :], start=True, stop=True)
                    if n % 4 == 3:
                        mm.then_inc(wvfc_mm, 1)
        clear(nc, sems)

        with nc.Fori(0, B) as b:
            with nc.Block() as block:
                @block.sync
                def _(sp):
                    sp.dma_start(x[:, :, :], x_in[b].rearrange("(t p) d -> p t d", p=P)).then_inc(x_loaded, 16)
                    sp.wait_ge(x_ready, 1)
                    sp.dma_start(x_out[b].rearrange("(t p) d -> p t d", p=P), x[:, :, :]).then_inc(stored, 16)
                    sp.wait_ge(stored, 16)

                @block.gpsimd
                def _(pool):
                    for k in range(3):
                        norm.root(pool, minus_half[:, :], k)

                @block.scalar
                def _(act):
                    for c in range(NC):
                        act.wait_ge(xt_mm, NT // NC * (c + 1))
                        nc.scalar.copy(xt_hi[:, c * CH:(c + 1) * CH], ps[:, c, :]).then_inc(xt_hi_ready, 1)
                    for t in range(NT):
                        for c in range(2):
                            n = 2 * t + c
                            act.wait_ge(k_mm, n + 1)
                            if t >= 2 and c == 0:
                                act.wait_ge(kx_mm, t - 1)
                            nc.scalar.activation(kn[:, t % 2, c * CH:(c + 1) * CH], ps[:, n % 4, :],
                                                 ACT.Sigmoid).then_inc(k_ready, 1)
                    for c in range(2):
                        act.wait_ge(kxt_mm, 4 * (c + 1))
                        nc.scalar.copy(kxt[:, 4 * c:4 * c + 4, :].rearrange("p f d -> p (f d)"),
                                       ps[:, c, :]).then_inc(kxt_ready, 1)
                    for c in range(2):
                        act.wait_ge(m_mm, 4 * (c + 1))
                        nc.scalar.copy(m[:, 4 * c:4 * c + 4, :].rearrange("p f d -> p (f d)"),
                                       ps[:, 2 + c, :]).then_inc(m_ready, 1)
                    for n in range(NF * NC):
                        f, c = n // NC, n % NC
                        act.wait_ge(q_mm, n + 1)
                        nc.scalar.activation(q[:, f, c * CH:(c + 1) * CH], ps[:, n % 4, :],
                                             ACT.Sigmoid).then_inc(q_ready, 1)

                @block.vector
                def _(dve):
                    dve.wait_ge(x_loaded, 16)
                    norm.moments(dve, lambda t: x[:, t, :], 0)
                    norm.apply(dve, lambda t: xn[:, t, 0:D], lambda t: x[:, t, :], 0, xn_ready)
                    for c in range(NC):
                        dve.wait_ge(xt_hi_ready, c + 1)
                        nc.vector.tensor_tensor(xt_lo[:, c * CH:(c + 1) * CH], ps[:, c, :],
                                                f32(xt_hi[:, c * CH:(c + 1) * CH]), ALU.subtract).then_inc(xt_ready, 1)
                    dve.wait_ge(kx_mm, NT)
                    for f in range(NF // 2):
                        nc.vector.tensor_copy(kx[:, 2 * f:2 * f + 2, :],
                                              ps[:, 4 + f, 0:2 * (D + 1)].rearrange("p (a d) -> p a d", a=2)
                                              ).then_inc(kx_copied, 1)
                    dve.wait_ge(kx_copied, NF // 2)
                    nc.vector.tensor_tensor(ksum_col[:, :, :], headcol[:, :, :],
                                            kx[:, :, D:D + 1].broadcast_to([P, NF, 32]), ALU.mult).then_inc(ksum_ready, 1)
                    dve.wait_ge(den_mm, 1)
                    nc.vector.tensor_scalar(den[:, :], ps[:, 4, 0:256], DEN_EPS, None, ALU.add).then_inc(den_step, 1)
                    dve.wait_ge(den_step, 1)
                    nc.vector.reciprocal(rden[:, :], den[:, :]).then_inc(den_step, 1)
                    dve.wait_ge(den_step, 2)
                    for g in range(4):
                        nc.vector.tensor_copy(rden_hi[32 * g:32 * g + 32, g, :],
                                              rden[32 * g:32 * g + 32, :]).then_inc(den_step, 1)
                    dve.wait_ge(den_step, 6)
                    for g in range(4):
                        nc.vector.tensor_tensor(rden_lo[32 * g:32 * g + 32, g, :], rden[32 * g:32 * g + 32, :],
                                                f32(rden_hi[32 * g:32 * g + 32, g, :]), ALU.subtract).then_inc(rden_ready, 1)
                    for n in range(NF * NC):
                        c, f = n // NF, n % NF
                        dve.wait_ge(spread_mm, n + 1)
                        cols = slice(c * CH, (c + 1) * CH)
                        nc.vector.tensor_tensor(q[:, f, cols], q[:, f, cols], ps[:, n % 4, :],
                                                ALU.mult).then_inc(qd_ready, 1)
                    for c in range(NC):
                        dve.wait_ge(out_mm, 4 * (c + 1))
                        nc.vector.tensor_tensor(z[:, 4 * c:4 * c + 4, :],
                                                ps[:, 6 + c, :].rearrange("p (t d) -> p t d", t=4),
                                                xn[:, 4 * c:4 * c + 4, 0:D], ALU.add).then_inc(z_ready, 1)
                    dve.wait_ge(z_ready, NC)
                    norm.moments(dve, lambda t: z[:, t, :], 1)
                    norm.apply(dve, lambda t: z[:, t, :], lambda t: z[:, t, :], 1, z_normed)
                    dve.wait_ge(z_normed, NT)
                    nc.vector.tensor_tensor(z[:, :, :], z[:, :, :],
                                            gamma_b[:, None, :].broadcast_to([P, NT, D]), ALU.mult).then_inc(affine, 1)
                    dve.wait_ge(affine, 1)
                    nc.vector.tensor_tensor(z[:, :, :], z[:, :, :],
                                            beta_b[:, None, :].broadcast_to([P, NT, D]), ALU.add).then_inc(affine, 1)
                    dve.wait_ge(affine, 2)
                    norm.moments(dve, lambda t: z[:, t, :], 2)
                    norm.apply(dve, lambda t: z[:, t, :], lambda t: z[:, t, :], 2, z_normed)
                    dve.wait_ge(z_normed, 2 * NT)
                    nc.vector.tensor_tensor(x[:, :, :], x[:, :, :], z[:, :, :], ALU.add).then_inc(x_ready, 1)

                @block.tensor
                def _(pe):
                    for t in range(NT):
                        pe.wait_ge(xn_ready, t + 1)
                        pe.transpose(ps[:, t // 4, (t % 4) * P:(t % 4 + 1) * P], xn[:, t, 0:D],
                                     ident[:, :]).then_inc(xt_mm, 1)

                    def three(out, lhs, rhs):
                        pe.matmul(out, lhs[0], rhs[0], start=True, stop=False)
                        pe.matmul(out, lhs[0], rhs[1], start=False, stop=False)
                        return pe.matmul(out, lhs[1], rhs[0], start=False, stop=True)

                    def k_times_x(t):
                        pe.wait_ge(k_ready, 2 * t + 2)
                        for f in range(NF):
                            mm = pe.matmul(ps[:, 4 + f // 2, (f % 2) * (D + 1):(f % 2 + 1) * (D + 1)],
                                           kn[:, t % 2, f * P:(f + 1) * P], xn[:, t, :],
                                           start=(t == 0 and f % 2 == 0), stop=(t == NT - 1), skip_group_check=True)
                        mm.then_inc(kx_mm, 1)

                    pe.wait_ge(xt_ready, NC)
                    for t in range(NT):
                        toks = slice(t * P, (t + 1) * P)
                        for c in range(2):
                            n = 2 * t + c
                            if n >= 4:
                                pe.wait_ge(k_ready, n - 3)
                            cols = slice(c * CH, (c + 1) * CH)
                            three(ps[:, n % 4, :], (xt_hi[:, toks], xt_lo[:, toks]),
                                  (wk_hi[:, cols], wk_lo[:, cols])).then_inc(k_mm, 1)
                        if t >= 1:
                            k_times_x(t - 1)
                    k_times_x(NT - 1)
                    pe.wait_ge(kx_copied, NF // 2)
                    for f in range(NF):
                        pe.transpose(ps[:, f // 4, (f % 4) * P:(f % 4 + 1) * P], kx[:, f, 0:D],
                                     ident[:, :]).then_inc(kxt_mm, 1)
                    for f in range(NF):
                        if f % 4 == 0:
                            pe.wait_ge(kxt_ready, f // 4 + 1)
                        for s in range(2):
                            mm = pe.matmul(ps[64 * s:64 * s + 64, 2 + f // 4, (f % 4) * P:(f % 4 + 1) * P],
                                           kxt[:, f, 64 * s:64 * s + 64], wvfc[:, NF * s + f, :], start=True, stop=True)
                        mm.then_inc(m_mm, 1)

                    def den_of(f):
                        pe.wait_ge(q_ready, 2 * f + 2)
                        for g in range(4):
                            mm = pe.matmul(ps[32 * g:32 * g + 32, 4, 0:256], ksum_col[:, f, :],
                                           q[:, f, 256 * g:256 * g + 256], start=(f == 0), stop=(f == NF - 1))
                        if f == NF - 1:
                            mm.then_inc(den_mm, 1)

                    pe.wait_ge(m_ready, 2)
                    pe.wait_ge(ksum_ready, 1)
                    for f in range(NF):
                        blk = slice(f * P, (f + 1) * P)
                        for c in range(NC):
                            n = NC * f + c
                            if n >= 4:
                                pe.wait_ge(q_ready, n - 3)
                            cols = slice(c * CH, (c + 1) * CH)
                            three(ps[:, n % 4, :], (wq_hi[:, blk], wq_lo[:, blk]),
                                  (xt_hi[:, cols], xt_lo[:, cols])).then_inc(q_mm, 1)
                        if f >= 1:
                            den_of(f - 1)
                    den_of(NF - 1)
                    pe.wait_ge(rden_ready, 4)

                    def out_of(c):
                        pe.wait_ge(qd_ready, NF * (c + 1))
                        for t in range(4 * c, 4 * c + 4):
                            for f in range(NF):
                                mm = pe.matmul(ps[:, 6 + c, (t % 4) * D:(t % 4 + 1) * D], q[:, f, t * P:(t + 1) * P],
                                               m[:, f, :], start=(f == 0), stop=(f == NF - 1))
                            mm.then_inc(out_mm, 1)

                    for n in range(NF * NC):
                        c, f = n // NF, n % NF
                        if n >= 4:
                            pe.wait_ge(qd_ready, n - 3)
                        pair = slice(2 * c, 2 * c + 2)
                        pe.matmul(ps[:, n % 4, :], headsel[:, f, :],
                                  rden_hi[:, pair, :].rearrange("p a n -> p (a n)"), start=True, stop=False)
                        pe.matmul(ps[:, n % 4, :], headsel[:, f, :],
                                  rden_lo[:, pair, :].rearrange("p a n -> p (a n)"),
                                  start=False, stop=True).then_inc(spread_mm, 1)
                        if n == NF + 3:
                            out_of(0)
                    out_of(1)
            clear(nc, sems)


def feed_forward(nc, tag, x_in, x_out, w1t, w1s, w2t, w2s, h1t, h1s, h2t, h2s, w3t, w3s, c_ident):
    with ExitStack() as ctx:
        def sb(name, shape, dt=F32):
            return ctx.enter_context(nc.sbuf_tensor(tag + name, shape, dt))

        sems = []

        def sem(name):
            s = ctx.enter_context(nc.semaphore(tag + name))
            sems.append(s)
            return s

        ps = ctx.enter_context(nc.psum_tensor(tag + "ps", [P, 8, CH], F32))

        ident = sb("ident", [P, P])
        w1, w2 = sb("w1", [P, HID], F32R), sb("w2", [P, HID], F32R)
        h1, h2 = sb("h1", [P, NB, HID], F32R), sb("h2", [P, NB, HID], F32R)
        w3 = sb("w3", [P, NB, D], F32R)
        raw = sb("raw", [P, 2 * HID + 2 * NB * HID + NB * D])
        s1, s2, s3, s4 = (sb(f"s{i}", [P, NB]) for i in range(4))
        s5 = sb("s5", [P, D])
        minus_half = sb("minus_half", [P, NT])

        x = sb("x", [P, NT, D])
        xn = sb("xn", [P, NT, D])
        xt_hi, xt_lo = sb("xt_hi", [P, N], F32R), sb("xt_lo", [P, N], F32R)
        hid_hi = [sb(f"hid_hi{i}", [P, NB, CH], F32R) for i in range(3)]
        hid_lo = [sb(f"hid_lo{i}", [P, NB, CH], F32R) for i in range(3)]
        gate = sb("gate", [P, 3, CH])
        full = sb("full", [P, 3, CH])
        z = sb("z", [P, NT, D])
        norm = Norm(nc, sb, sem, "norm", 2)

        w_in = sem("w_in")
        x_loaded = sem("x_loaded")
        xn_ready = sem("xn_ready")
        xt_mm = sem("xt_mm")
        xt_hi_ready = sem("xt_hi_ready")
        xt_ready = sem("xt_ready")
        up_mm = sem("up_mm")
        gate_ready = sem("gate_ready")
        full_ready = sem("full_ready")
        hi_ready = sem("hi_ready")
        lo_ready = sem("lo_ready")
        hid_mm = sem("hid_mm")
        gelu_full = sem("gelu_full")
        gelu_hi = sem("gelu_hi")
        gelu_lo = sem("gelu_lo")
        out_mm = sem("out_mm")
        z_ready = sem("z_ready")
        z_normed = sem("z_normed")
        x_ready = sem("x_ready")
        stored = sem("stored")

        o1, o2 = 2 * HID, 2 * HID + NB * HID
        o3 = o2 + NB * HID
        with nc.Block() as block:
            @block.sync
            def _(sp):
                sp.dma_start(raw[:, 0:HID], w1t).then_inc(w_in, 16)
                sp.dma_start(raw[:, HID:o1], w2t).then_inc(w_in, 16)
                sp.dma_start(raw[:, o1:o2].rearrange("p (k o) -> p k o", k=NB),
                             h1t.rearrange("(k p) o -> p k o", p=P)).then_inc(w_in, 16)
                sp.dma_start(raw[:, o2:o3].rearrange("p (k o) -> p k o", k=NB),
                             h2t.rearrange("(k p) o -> p k o", p=P)).then_inc(w_in, 16)
                sp.dma_start(raw[:, o3:].rearrange("p (k o) -> p k o", k=NB),
                             w3t.rearrange("(k p) o -> p k o", p=P)).then_inc(w_in, 16)
                for s, src in ((s1, w1s), (s2, w2s), (s3, h1s), (s4, h2s)):
                    sp.dma_start(s[:, :], src).then_inc(w_in, 16)
                sp.dma_start(s5[:, :], w3s.rearrange("(a d) -> a d", a=1).broadcast_to([P, D])).then_inc(w_in, 16)
                sp.dma_start(ident[:, :], c_ident).then_inc(w_in, 16)

            @block.gpsimd
            def _(pool):
                nc.gpsimd.memset(minus_half[:, :], -0.5)

            @block.vector
            def _(dve):
                dve.wait_ge(w_in, 11 * 16)
                nc.vector.tensor_copy(w1[:, :], raw[:, 0:HID])
                nc.vector.tensor_copy(w2[:, :], raw[:, HID:o1])
                nc.vector.tensor_copy(h1[:, :, :].rearrange("p k o -> p (k o)"), raw[:, o1:o2])
                nc.vector.tensor_copy(h2[:, :, :].rearrange("p k o -> p (k o)"), raw[:, o2:o3])
                nc.vector.tensor_copy(w3[:, :, :].rearrange("p k o -> p (k o)"), raw[:, o3:])
        clear(nc, sems)

        SRC = ((None, 0, 2), (None, 1, 0))
        DST = ((0, 2, 1), (1, 0, 2))

        with nc.Fori(0, B) as b:
            with nc.Block() as block:
                @block.sync
                def _(sp):
                    sp.dma_start(x[:, :, :], x_in[b].rearrange("(t p) d -> p t d", p=P)).then_inc(x_loaded, 16)
                    sp.wait_ge(x_ready, 1)
                    sp.dma_start(x_out[b].rearrange("(t p) d -> p t d", p=P), x[:, :, :]).then_inc(stored, 16)
                    sp.wait_ge(stored, 16)

                @block.gpsimd
                def _(pool):
                    norm.root(pool, minus_half[:, :], 0)
                    for n in range(NB * NC):
                        c, f = n // NB, n % NB
                        pool.wait_ge(full_ready, n + 1)
                        nc.gpsimd.tensor_copy(hid_hi[DST[c][0]][:, f, :], full[:, n % 3, :]).then_inc(hi_ready, 1)
                    norm.root(pool, minus_half[:, :], 1)

                @block.scalar
                def _(act):
                    for c in range(NC):
                        act.wait_ge(xt_mm, NT // NC * (c + 1))
                        nc.scalar.copy(xt_hi[:, c * CH:(c + 1) * CH], ps[:, 6 + c, :]).then_inc(xt_hi_ready, 1)
                    for n in range(NB * NC):
                        act.wait_ge(up_mm, n + 1)
                        if n >= 3:
                            act.wait_ge(full_ready, n - 2)
                        nc.scalar.activation(gate[:, n % 3, :], ps[:, n % 3, :], ACT.Silu,
                                             scale=s1[:, n % NB:n % NB + 1]).then_inc(gate_ready, 1)
                    act.wait_ge(lo_ready, NB * NC)
                    for n in range(2 * NB * NC):
                        stage, c, o = 1 + n // (NB * NC), n // NB % NC, n % NB
                        scale = (s3, s4)[stage - 1][:, o:o + 1]
                        act.wait_ge(hid_mm, n + 1)
                        nc.scalar.activation(hid_hi[DST[c][stage]][:, o, :], ps[:, n % 6, :], ACT.Gelu,
                                             scale=scale).then_inc(gelu_hi, 1)
                        if n >= 3:
                            act.wait_ge(gelu_lo, n - 2)
                        nc.scalar.activation(full[:, n % 3, :], ps[:, n % 6, :], ACT.Gelu,
                                             scale=scale).then_inc(gelu_full, 1)

                @block.vector
                def _(dve):
                    dve.wait_ge(x_loaded, 16)
                    norm.moments(dve, lambda t: x[:, t, :], 0)
                    norm.apply(dve, lambda t: xn[:, t, :], lambda t: x[:, t, :], 0, xn_ready)
                    for c in range(NC):
                        dve.wait_ge(xt_hi_ready, c + 1)
                        nc.vector.tensor_tensor(xt_lo[:, c * CH:(c + 1) * CH], ps[:, 6 + c, :],
                                                f32(xt_hi[:, c * CH:(c + 1) * CH]), ALU.subtract).then_inc(xt_ready, 1)

                    def lower(n):
                        dve.wait_ge(hi_ready, n + 1)
                        buf = DST[n // NB][0]
                        nc.vector.tensor_tensor(hid_lo[buf][:, n % NB, :], full[:, n % 3, :],
                                                f32(hid_hi[buf][:, n % NB, :]), ALU.subtract).then_inc(lo_ready, 1)

                    for n in range(NB * NC):
                        dve.wait_ge(gate_ready, n + 1)
                        if n >= 3:
                            dve.wait_ge(lo_ready, n - 2)
                        nc.vector.scalar_tensor_tensor(out=full[:, n % 3, :], in0=ps[:, 3 + n % 3, :],
                                                       scalar=s2[:, n % NB:n % NB + 1], in1=gate[:, n % 3, :],
                                                       op0=ALU.mult, op1=ALU.mult).then_inc(full_ready, 1)
                        if n >= 1:
                            lower(n - 1)
                    lower(NB * NC - 1)
                    for n in range(2 * NB * NC):
                        stage, c, o = 1 + n // (NB * NC), n // NB % NC, n % NB
                        buf = DST[c][stage]
                        dve.wait_ge(gelu_full, n + 1)
                        nc.vector.tensor_tensor(hid_lo[buf][:, o, :], full[:, n % 3, :], f32(hid_hi[buf][:, o, :]),
                                                ALU.subtract).then_inc(gelu_lo, 1)
                    for c in range(NC):
                        dve.wait_ge(out_mm, 4 * (c + 1))
                        nc.vector.tensor_tensor(z[:, 4 * c:4 * c + 4, :],
                                                ps[:, 6 + c, :].rearrange("p (t d) -> p t d", t=4),
                                                s5[:, None, :].broadcast_to([P, 4, D]), ALU.mult).then_inc(z_ready, 1)
                    dve.wait_ge(z_ready, NC)
                    norm.moments(dve, lambda t: z[:, t, :], 1)
                    norm.apply(dve, lambda t: z[:, t, :], lambda t: z[:, t, :], 1, z_normed)
                    dve.wait_ge(z_normed, NT)
                    nc.vector.tensor_tensor(x[:, :, :], x[:, :, :], z[:, :, :], ALU.add).then_inc(x_ready, 1)

                @block.tensor
                def _(pe):
                    for t in range(NT):
                        pe.wait_ge(xn_ready, t + 1)
                        pe.transpose(ps[:, 6 + t // 4, (t % 4) * P:(t % 4 + 1) * P], xn[:, t, :],
                                     ident[:, :]).then_inc(xt_mm, 1)
                    pe.wait_ge(xt_ready, NC)
                    for n in range(NB * NC):
                        c, f = n // NB, n % NB
                        cols, blk = slice(c * CH, (c + 1) * CH), slice(f * P, (f + 1) * P)
                        if n >= 3:
                            pe.wait_ge(full_ready, n - 2)
                        pe.matmul(ps[:, n % 3, :], w1[:, blk], xt_hi[:, cols], start=True, stop=False)
                        pe.matmul(ps[:, n % 3, :], w1[:, blk], xt_lo[:, cols], start=False, stop=True)
                        pe.matmul(ps[:, 3 + n % 3, :], w2[:, blk], xt_hi[:, cols], start=True, stop=False)
                        pe.matmul(ps[:, 3 + n % 3, :], w2[:, blk], xt_lo[:, cols], start=False,
                                  stop=True).then_inc(up_mm, 1)
                    for n in range(2 * NB * NC):
                        stage, c, o = 1 + n // (NB * NC), n // NB % NC, n % NB
                        w, src = (h1, h2)[stage - 1], SRC[c][stage]
                        if o == 0:
                            if stage == 1:
                                pe.wait_ge(lo_ready, NB * (c + 1))
                                pe.wait_ge(full_ready, NB * NC)
                            else:
                                pe.wait_ge(gelu_lo, NB * (c + 1))
                        if n >= 6:
                            pe.wait_ge(gelu_full, n - 5)
                        for k in range(NB):
                            pe.matmul(ps[:, n % 6, :], w[:, k, o * P:(o + 1) * P], hid_hi[src][:, k, :],
                                      start=(k == 0), stop=False)
                            mm = pe.matmul(ps[:, n % 6, :], w[:, k, o * P:(o + 1) * P], hid_lo[src][:, k, :],
                                           start=False, stop=(k == NB - 1))
                        mm.then_inc(hid_mm, 1)
                    for t in range(NT):
                        c = t // 4
                        src, toks = DST[c][2], slice(t % 4 * P, (t % 4 + 1) * P)
                        if t % 4 == 0:
                            pe.wait_ge(gelu_lo, NB * NC + NB * (c + 1))
                        for k in range(NB):
                            pe.matmul(ps[:, 6 + c, (t % 4) * D:(t % 4 + 1) * D], hid_hi[src][:, k, toks], w3[:, k, :],
                                      start=(k == 0), stop=False)
                            mm = pe.matmul(ps[:, 6 + c, (t % 4) * D:(t % 4 + 1) * D], hid_lo[src][:, k, toks],
                                           w3[:, k, :], start=False, stop=(k == NB - 1))
                        mm.then_inc(out_mm, 1)
            clear(nc, sems)


def window_attention(nc, x_in, x_out, WqkvT, bqkv, WgateT, bgate, WoutT, bout, pos_bias, offsets,
                     c_ident, c_dist, c_ones_rows, c_turned, table, parts):
    with ExitStack() as ctx:
        def sb(name, shape, dt=F32):
            return ctx.enter_context(nc.sbuf_tensor("wa_" + name, shape, dt))

        sems = []

        def sem(name):
            s = ctx.enter_context(nc.semaphore("wa_" + name))
            sems.append(s)
            return s

        ps = ctx.enter_context(nc.psum_tensor("wa_ps", [P, 8, CH], F32))

        ident = sb("ident", [P, P])
        raw = sb("raw", [P, 3 * D + D])
        wqk_hi, wqk_lo = sb("wqk_hi", [P, 2 * D], F32R), sb("wqk_lo", [P, 2 * D], F32R)
        wvg_hi, wvg_lo = sb("wvg_hi", [P, 2 * D], F32R), sb("wvg_lo", [P, 2 * D], F32R)
        wout = sb("wout", [P, D])
        bq, bk = sb("bq", [P, 1]), sb("bk", [P, 1])
        bvg_b, bout_b = sb("bvg_b", [P, 2 * D]), sb("bout_b", [P, D])
        minus_half = sb("minus_half", [P, NT])
        pos, off_i, off_f = sb("pos", [NOFF, H1]), sb("off_i", [NOFF, 1], I32), sb("off_f", [NOFF, 1])
        ones = sb("ones", [NOFF, H1])
        dist = sb("dist", [NOFF, 2 * TAB])
        hit = sb("hit", [NOFF, 2 * TAB])
        missing = sb("missing", [H1, 2, TAB])
        bias_row = sb("bias_row", [H1, 2, TAB])
        bias_qk, bias_kq = sb("bias_qk", [P, H1, WIN]), sb("bias_kq", [P, H1, WIN])
        ones_rows = sb("ones_rows", [P, GH])
        turned = sb("turned", [P, P])

        x = sb("x", [P, NT, D])
        xn = sb("xn", [P, NT, D])
        xt_hi, xt_lo = sb("xt_hi", [P, N], F32R), sb("xt_lo", [P, N], F32R)
        qk = sb("qk", [P, 2, N])
        qk_hi, qk_lo = sb("qk_hi", [P, 2, N], F32R), sb("qk_lo", [P, 2, N], F32R)
        vp = sb("vp", [P, NT, H1, 32])
        gate = sb("gate", [P, NT, D])
        qcat = sb("qcat", [P, NG, N], F32R)
        kz = sb("kz", [P, 2, GH, N], F32R)
        junk = sb("junk", [P, 4, WIN])
        top = sb("top", [P, NT, GH])
        negtop = sb("negtop", [P, NT, P])
        biased = sb("biased", [P, 2, GH, WIN])
        prob = sb("prob", [P, 2, GH, WIN])
        ot = sb("ot", [P, N])
        rden = sb("rden", [P, 4, GH, 1])
        flat = qk[:, 1, :].rearrange("p (t d) -> p t d", t=NT)
        flat_t = qk[:, 0, :]
        z = xn
        norm = Norm(nc, sb, sem, "norm", 2)

        w_in = sem("w_in")
        w_ready = sem("w_ready")
        hit_ready = sem("hit_ready")
        table_mm = sem("table_mm")
        table_step = sem("table_step")
        table_out = sem("table_out")
        table_in = sem("table_in")
        flip_mm = sem("flip_mm")
        flip_copied = sem("flip_copied")
        x_loaded = sem("x_loaded")
        xn_ready = sem("xn_ready")
        xt_mm = sem("xt_mm")
        xt_hi_ready = sem("xt_hi_ready")
        xt_ready = sem("xt_ready")
        qk_mm = sem("qk_mm")
        qk_biased = sem("qk_biased")
        qk_ready = sem("qk_ready")
        parts_out = sem("parts_out")
        q_in = sem("q_in")
        k_in = [sem(f"k_in{i}") for i in range(2)]
        rows_zero = sem("rows_zero")
        vg_mm = sem("vg_mm")
        v_ready = sem("v_ready")
        gate_ready = sem("gate_ready")
        s_mm = sem("s_mm")
        s_used = sem("s_used")
        top_step = sem("top_step")
        top_mm = sem("top_mm")
        top_ready = sem("top_ready")
        biased_ready = sem("biased_ready")
        prob_ready = sem("prob_ready")
        pv_mm = sem("pv_mm")
        ot_copied = sem("ot_copied")
        back_mm = sem("back_mm")
        rden_ready = sem("rden_ready")
        flat_ready = sem("flat_ready")
        gated = sem("gated")
        flat_t_mm = sem("flat_t_mm")
        flat_t_ready = sem("flat_t_ready")
        out_mm = sem("out_mm")
        z_ready = sem("z_ready")
        z_normed = sem("z_normed")
        x_ready = sem("x_ready")
        stored = sem("stored")

        FLIPS = H1 * WIN // CH
        with nc.Block() as block:
            @block.sync
            def _(sp):
                sp.dma_start(raw[:, 0:3 * D], WqkvT).then_inc(w_in, 16)
                sp.dma_start(raw[:, 3 * D:], WgateT).then_inc(w_in, 16)
                sp.dma_start(wout[:, :], WoutT).then_inc(w_in, 16)
                sp.dma_start(bq[:, :], bqkv[0:D].rearrange("(p a) -> p a", a=1)).then_inc(w_in, 16)
                sp.dma_start(bk[:, :], bqkv[D:2 * D].rearrange("(p a) -> p a", a=1)).then_inc(w_in, 16)
                sp.dma_start(bvg_b[:, 0:D], bqkv[2 * D:].rearrange("(a d) -> a d", a=1).broadcast_to([P, D])).then_inc(w_in, 16)
                sp.dma_start(bvg_b[:, D:], bgate.rearrange("(a d) -> a d", a=1).broadcast_to([P, D])).then_inc(w_in, 16)
                sp.dma_start(bout_b[:, :], bout.rearrange("(a d) -> a d", a=1).broadcast_to([P, D])).then_inc(w_in, 16)
                sp.dma_start(pos[:, :], pos_bias).then_inc(w_in, 16)
                sp.dma_start(off_i[:, :], offsets.rearrange("(p a) -> p a", a=1)).then_inc(w_in, 16)
                sp.dma_start(dist[:, :], c_dist).then_inc(w_in, 16)
                sp.dma_start(ident[:, :], c_ident).then_inc(w_in, 16)
                sp.dma_start(ones_rows[:, :], c_ones_rows).then_inc(w_in, 16)
                sp.dma_start(turned[:, :], c_turned).then_inc(w_in, 16)
                sp.wait_ge(table_step, 4)
                sp.dma_start(table, bias_row[:, :, :]).then_inc(table_out, 16)
                sp.wait_ge(table_out, 16)
                half = H1 // 2
                upside_down = (bias_qk[:, :, :], biased[:, :, :, :].rearrange("p a h n -> p (a h) n"),
                               prob[:, :, :, :].rearrange("p a h n -> p (a h) n"))
                for dst, n, h, nh in zip(upside_down, (0, 1, 1), (0, 0, half), (H1, half, half)):
                    src = bass.AP(table.tensor, (2 * h + n) * TAB + 1, [[1, P], [2 * TAB, nh], [1, WIN]])
                    sp.dma_start(dst, src).then_inc(table_in, 16)

            @block.gpsimd
            def _(pool):
                nc.gpsimd.memset(minus_half[:, :], -0.5)
                nc.gpsimd.memset(ones[:, :], 1.0).then_inc(w_ready, 1)
                nc.gpsimd.memset(vp[:, :, :, :], 0.0).then_inc(w_ready, 1)
                pool.wait_ge(w_ready, 2)
                nc.gpsimd.memset(vp[:, :, :, HD:HD + 1], 1.0)
                nc.gpsimd.memset(negtop[:, :, :], 0.0)

            @block.vector
            def _(dve):
                nc.vector.memset(kz[:, :, :, :].bitcast(F32), 0.0).then_inc(hit_ready, 1)
                dve.wait_ge(w_in, 14 * 16)
                nc.vector.tensor_copy(off_f[:, :], off_i[:, :]).then_inc(hit_ready, 1)
                dve.wait_ge(hit_ready, 2)
                nc.vector.tensor_scalar(hit[:, :], dist[:, :], off_f[:, 0:1], None, ALU.is_equal).then_inc(hit_ready, 1)
                for i in range(GH):
                    nc.vector.tensor_scalar(kz[:, :, i, :], f32(kz[:, :, i, :]), ones_rows[:, i:i + 1], None, ALU.add)
                split(nc, dve, wqk_hi[:, :], wqk_lo[:, :], raw[:, 0:2 * D], hit_ready, 3)
                split(nc, dve, wvg_hi[:, :], wvg_lo[:, :], raw[:, 2 * D:], hit_ready, 5)
                nc.vector.tensor_scalar(bq[:, :], bq[:, :], float(HD) ** -0.5, None, ALU.mult)
                for n in range(2):
                    dve.wait_ge(table_mm, n + 1)
                    nc.vector.tensor_scalar(missing[:, n, :], ps[0:H1, 2 + n, 0:TAB], -1.0, FAR, ALU.add,
                                            ALU.mult).then_inc(table_step, 1)
                    dve.wait_ge(table_step, 2 * n + 1)
                    nc.vector.tensor_tensor(bias_row[:, n, :], ps[0:H1, n, 0:TAB], missing[:, n, :],
                                            ALU.add).then_inc(table_step, 1)
                flipped = [t[:, :, :].rearrange("p h n -> p (h n)") for t in (bias_kq, bias_qk)]
                for n in range(2 * FLIPS):
                    dve.wait_ge(flip_mm, n + 1)
                    cols = slice(n % FLIPS * CH, (n % FLIPS + 1) * CH)
                    nc.vector.tensor_copy(flipped[n // FLIPS][:, cols], ps[:, 4 + n % 4, :]).then_inc(flip_copied, 1)

            @block.tensor
            def _(pe):
                pe.wait_ge(w_ready, 1)
                pe.wait_ge(hit_ready, 3)
                for n in range(2):
                    cols = slice(n * TAB, (n + 1) * TAB)
                    pe.matmul(ps[0:H1, n, 0:TAB], pos[:, :], hit[:, cols], start=True, stop=True)
                    pe.matmul(ps[0:H1, 2 + n, 0:TAB], ones[:, :], hit[:, cols], start=True, stop=True).then_inc(table_mm, 1)
                pe.wait_ge(table_in, 3 * 16)
                raw_rows = [bias_qk[:, :, :].rearrange("p h n -> p (h n)"),
                            biased[:, :, :, :].rearrange("p a h n -> p (a h n)"),
                            prob[:, :, :, :].rearrange("p a h n -> p (a h n)")]
                for n in range(2 * FLIPS):
                    m = n % FLIPS if n < FLIPS else (n - FLIPS) % (FLIPS // 2)
                    src = raw_rows[0 if n < FLIPS else 1 + (n - FLIPS) // (FLIPS // 2)]
                    if n >= 4:
                        pe.wait_ge(flip_copied, n - 3)
                    pe.matmul(ps[:, 4 + n % 4, :], turned[:, :], src[:, m * CH:(m + 1) * CH], start=True,
                              stop=True).then_inc(flip_mm, 1)
        clear(nc, sems)

        QP = (0, 0, 1)
        KP = (0, 1, 0)
        PER_G = 2 * NT * GH

        def keys_of(t):
            lo = max(0, P * t - REACH)
            return lo, lo - (P * t - REACH)

        with nc.Fori(0, B) as b:
            with nc.Block() as block:
                @block.sync
                def _(sp):
                    sp.dma_start(x[:, :, :], x_in[b].rearrange("(t p) d -> p t d", p=P)).then_inc(x_loaded, 16)
                    sp.wait_ge(qk_ready, 8)
                    sp.dma_start(parts[0].rearrange("a p n -> p a n"), f32(qk_hi[:, :, :])).then_inc(parts_out, 16)
                    sp.dma_start(parts[1].rearrange("a p n -> p a n"), f32(qk_lo[:, :, :])).then_inc(parts_out, 16)
                    sp.wait_ge(parts_out, 32)
                    for r in range(3):
                        sp.dma_start(f32(qcat[32 * r:32 * r + 32, :, :]),
                                     parts[QP[r], 0].rearrange("(g r) n -> r g n", g=NG)).then_inc(q_in, 16)
                    for g in range(NG):
                        if g >= 2:
                            sp.wait_ge(pv_mm, NT * (g - 1))
                        for r in range(3):
                            for i in range(GH):
                                row = 32 * g + HD * i
                                sp.dma_start(f32(kz[32 * r + HD * i:32 * r + HD * (i + 1), g % 2, i, :]),
                                             parts[KP[r], 1, row:row + HD, :]).then_inc(k_in[g % 2], 16)
                    sp.wait_ge(x_ready, 1)
                    sp.dma_start(x_out[b].rearrange("(t p) d -> p t d", p=P), x[:, :, :]).then_inc(stored, 16)
                    sp.wait_ge(stored, 16)

                @block.gpsimd
                def _(pool):
                    nc.gpsimd.memset(f32(qcat[96:128, :, :]), 0.0).then_inc(rows_zero, 1)
                    pool.wait_ge(rows_zero, 1)
                    norm.root(pool, minus_half[:, :], 0)
                    norm.root(pool, minus_half[:, :], 1)

                @block.scalar
                def _(act):
                    for c in range(NC):
                        act.wait_ge(xt_mm, NT // NC * (c + 1))
                        nc.scalar.copy(xt_hi[:, c * CH:(c + 1) * CH], ps[:, c, :]).then_inc(xt_hi_ready, 1)
                    for a, (scale, bias) in enumerate(((float(HD) ** -0.5, bq), (1.0, bk))):
                        for c in range(NC):
                            act.wait_ge(qk_mm, 2 * a + c + 1)
                            nc.scalar.activation(qk[:, a, c * CH:(c + 1) * CH], ps[:, 2 + 2 * a + c, :], ACT.Identity,
                                                 bias=bias[:, 0:1], scale=scale).then_inc(qk_biased, 1)
                    act.wait_ge(v_ready, 2 * NT)
                    nc.scalar.activation(gate[:, :, :], gate[:, :, :], ACT.Sigmoid).then_inc(gate_ready, 1)
                    for g in range(NG):
                        for j in range(NT):
                            n = g * NT + j
                            cols = min(WIN, N - P * j)
                            act.wait_ge(biased_ready, GH * (n + 1))
                            if n >= 2:
                                act.wait_ge(pv_mm, n - 1)
                            nc.scalar.activation(prob[:, n % 2, :, 0:cols], biased[:, n % 2, :, 0:cols],
                                                 ACT.Exp).then_inc(prob_ready, 1)
                        for c in range(NC):
                            act.wait_ge(pv_mm, NT * (g + 1))
                            if g >= 1 and c == 0:
                                act.wait_ge(back_mm, NT * g)
                            nc.scalar.copy(ot[:, c * CH:(c + 1) * CH], ps[:, 4 + c, :]).then_inc(ot_copied, 1)
                    for c in range(NC):
                        act.wait_ge(flat_t_mm, 4 * (c + 1))
                        nc.scalar.copy(flat_t[:, c * CH:(c + 1) * CH], ps[:, c, :]).then_inc(flat_t_ready, 1)

                @block.vector
                def _(dve):
                    dve.wait_ge(x_loaded, 16)
                    norm.moments(dve, lambda t: x[:, t, :], 0)
                    norm.apply(dve, lambda t: xn[:, t, :], lambda t: x[:, t, :], 0, xn_ready)
                    for c in range(NC):
                        dve.wait_ge(xt_hi_ready, c + 1)
                        nc.vector.tensor_tensor(xt_lo[:, c * CH:(c + 1) * CH], ps[:, c, :],
                                                f32(xt_hi[:, c * CH:(c + 1) * CH]), ALU.subtract).then_inc(xt_ready, 1)
                    for n in range(2 * NC):
                        a, cols = n // NC, slice((n % NC) * CH, (n % NC + 1) * CH)
                        dve.wait_ge(qk_biased, n + 1)
                        split(nc, dve, qk_hi[:, a, cols], qk_lo[:, a, cols], qk[:, a, cols], qk_ready, 2 * n)
                    for t in range(NT):
                        dve.wait_ge(vg_mm, t + 1)
                        bank = ps[:, 6 + t % 2, :]
                        nc.vector.tensor_tensor(vp[:, t, :, 0:HD], bank[:, 0:D].rearrange("p (h d) -> p h d", h=H1),
                                                bvg_b[:, 0:D].rearrange("p (h d) -> p h d", h=H1),
                                                ALU.add).then_inc(v_ready, 1)
                        nc.vector.tensor_tensor(gate[:, t, :], bank[:, D:2 * D], bvg_b[:, D:], ALU.add).then_inc(v_ready, 1)
                    steps = 0
                    for g in range(NG):
                        base = g * PER_G
                        for t in range(NT):
                            lo, skip = keys_of(t)
                            cols = P * (t + 1) - lo
                            for i in range(GH):
                                n = base + GH * t + i
                                dve.wait_ge(s_mm, n + 1)
                                used = NT * GH * g + GH * t + i
                                if used >= 4:
                                    dve.wait_ge(s_used, used - 3)
                                nc.vector.tensor_tensor_reduce(
                                    out=junk[:, used % 4, 0:cols], in0=ps[:, n % 4, 0:cols], in1=bias_qk[:, GH * g + i, skip:WIN],
                                    scale=1.0, scalar=-FAR, op0=ALU.add, op1=ALU.max,
                                    accum_out=top[:, t, i:i + 1]).then_inc(s_used, 1)
                        pair = negtop[:, :, 96:96 + 2 * GH].rearrange("p t (i a) -> p t i a", a=2)
                        dve.wait_ge(s_used, NT * GH * (g + 1))
                        if g >= 1:
                            dve.wait_ge(top_mm, NT * g)
                        nc.vector.tensor_scalar(pair[:, :, :, 0].bitcast(F32R), top[:, :, :], -1.0, None,
                                                ALU.mult).then_inc(top_step, 1)
                        dve.wait_ge(top_step, 2 * g + 1)
                        nc.vector.scalar_tensor_tensor(out=pair[:, :, :, 1].bitcast(F32R), in0=top[:, :, :], scalar=-1.0,
                                                       in1=pair[:, :, :, 0], op0=ALU.mult,
                                                       op1=ALU.subtract).then_inc(top_step, 1)
                        for c in range(NC):
                            dve.wait_ge(top_mm, NT * g + 4 * (c + 1))
                            nc.vector.tensor_copy(qcat[96:128, g, c * CH:(c + 1) * CH],
                                                  ps[96:128, 6 + c, :]).then_inc(top_ready, 1)
                        for j in range(NT):
                            cols = min(WIN, N - P * j)
                            if g * NT + j >= 2:
                                dve.wait_ge(prob_ready, g * NT + j - 1)
                            for i in range(GH):
                                n = base + NT * GH + GH * j + i
                                dve.wait_ge(s_mm, n + 1)
                                nc.vector.tensor_tensor(biased[:, j % 2, i, 0:cols], ps[:, n % 4, 0:cols],
                                                        bias_kq[:, GH * g + i, 0:cols], ALU.add).then_inc(biased_ready, 1)
                        for c in range(NC):
                            dve.wait_ge(back_mm, NT * g + 4 * (c + 1))
                            if g + c >= 1:
                                dve.wait_ge(flat_ready, NC * g + c)
                            bank = ps[:, 6 + c, :].rearrange("p (t i e) -> p t i e", t=4, i=GH)
                            nc.vector.reciprocal(rden[:, :, :, :], bank[:, :, :, HD:HD + 1]).then_inc(rden_ready, 1)
                            dve.wait_ge(rden_ready, NC * g + c + 1)
                            nc.vector.tensor_tensor(
                                flat[:, 4 * c:4 * c + 4, 32 * g:32 * g + 32].rearrange("p t (i e) -> p t i e", i=GH),
                                bank[:, :, :, 0:HD], rden[:, :, :, :].broadcast_to([P, 4, GH, HD]),
                                ALU.mult).then_inc(flat_ready, 1)
                    dve.wait_ge(flat_ready, NC * NG)
                    dve.wait_ge(gate_ready, 1)
                    nc.vector.tensor_tensor(flat[:, :, :], flat[:, :, :], gate[:, :, :], ALU.mult).then_inc(gated, 1)
                    for c in range(NC):
                        dve.wait_ge(out_mm, 4 * (c + 1))
                        nc.vector.tensor_tensor(z[:, 4 * c:4 * c + 4, :],
                                                ps[:, 2 + c, :].rearrange("p (t d) -> p t d", t=4),
                                                bout_b[:, None, :].broadcast_to([P, 4, D]), ALU.add).then_inc(z_ready, 1)
                    dve.wait_ge(z_ready, NC)
                    norm.moments(dve, lambda t: z[:, t, :], 1)
                    norm.apply(dve, lambda t: z[:, t, :], lambda t: z[:, t, :], 1, z_normed)
                    dve.wait_ge(z_normed, NT)
                    nc.vector.tensor_tensor(x[:, :, :], x[:, :, :], z[:, :, :], ALU.add).then_inc(x_ready, 1)

                @block.tensor
                def _(pe):
                    for t in range(NT):
                        pe.wait_ge(xn_ready, t + 1)
                        pe.transpose(ps[:, t // 4, (t % 4) * P:(t % 4 + 1) * P], xn[:, t, :],
                                     ident[:, :]).then_inc(xt_mm, 1)

                    def three(out, lhs, rhs):
                        pe.matmul(out, lhs[0], rhs[0], start=True, stop=False)
                        pe.matmul(out, lhs[0], rhs[1], start=False, stop=False)
                        return pe.matmul(out, lhs[1], rhs[0], start=False, stop=True)

                    pe.wait_ge(xt_ready, NC)
                    for a in range(2):
                        for c in range(NC):
                            cols = slice(c * CH, (c + 1) * CH)
                            three(ps[:, 2 + 2 * a + c, :], (wqk_hi[:, a * D:(a + 1) * D], wqk_lo[:, a * D:(a + 1) * D]),
                                  (xt_hi[:, cols], xt_lo[:, cols])).then_inc(qk_mm, 1)
                    for t in range(NT):
                        toks = slice(t * P, (t + 1) * P)
                        if t >= 2:
                            pe.wait_ge(v_ready, 2 * (t - 1))
                        three(ps[:, 6 + t % 2, 0:2 * D], (xt_hi[:, toks], xt_lo[:, toks]),
                              (wvg_hi[:, :], wvg_lo[:, :])).then_inc(vg_mm, 1)
                    pe.wait_ge(qk_biased, 2 * NC)
                    pe.wait_ge(v_ready, 2 * NT)
                    pe.wait_ge(q_in, 3 * 16)
                    pe.wait_ge(rows_zero, 1)

                    def scores(n, out, lhs, rhs):
                        g, r = n // PER_G, n % PER_G
                        half = NT * GH
                        if 4 <= r < half + 4:
                            pe.wait_ge(s_used, half * g + r - 3)
                        elif n >= 4:
                            before = half * g + r - 3 if r < 4 else half * g + r - half - 3
                            pe.wait_ge(biased_ready, before)
                        pe.matmul(out, lhs, rhs, start=True, stop=True).then_inc(s_mm, 1)

                    def weighted(g, j):
                        n = g * NT + j
                        pe.wait_ge(prob_ready, n + 1)
                        if g >= 1 and j == 0:
                            pe.wait_ge(ot_copied, NC * g)
                        first, last = P * j, min(N, P * j + WIN)
                        for c in range(NC):
                            a, z_ = max(first, c * CH), min(last, (c + 1) * CH)
                            if a >= z_:
                                continue
                            opens = j == (0 if c == 0 else (CH - WIN) // P + 1)
                            for i in range(GH):
                                mm = pe.matmul(ps[32 * i:32 * i + 32, 4 + c, a - c * CH:z_ - c * CH],
                                               vp[:, j, GH * g + i, :], prob[:, n % 2, i, a - first:z_ - first],
                                               start=opens, stop=(j == NT - 1), skip_group_check=True)
                        mm.then_inc(pv_mm, 1)

                    for g in range(NG):
                        base = g * PER_G
                        pe.wait_ge(k_in[g % 2], 12 * 16 * (g // 2 + 1))
                        for t in range(NT):
                            lo, _ = keys_of(t)
                            for i in range(GH):
                                n = base + GH * t + i
                                scores(n, ps[:, n % 4, 0:P * (t + 1) - lo], qcat[:, g, t * P:(t + 1) * P],
                                       kz[:, g % 2, i, lo:P * (t + 1)])
                        pe.wait_ge(top_step, 2 * (g + 1))
                        if g >= 1:
                            pe.wait_ge(flat_ready, NC * g)
                        for t in range(NT):
                            pe.transpose(ps[:, 6 + t // 4, (t % 4) * P:(t % 4 + 1) * P], negtop[:, t, :],
                                         ident[:, :]).then_inc(top_mm, 1)
                        pe.wait_ge(top_ready, NC * (g + 1))
                        for j in range(NT):
                            cols = min(WIN, N - P * j)
                            for i in range(GH):
                                n = base + NT * GH + GH * j + i
                                scores(n, ps[:, n % 4, 0:cols], kz[:, g % 2, i, j * P:(j + 1) * P],
                                       qcat[:, g, j * P:j * P + cols])
                            if j >= 1:
                                weighted(g, j - 1)
                        weighted(g, NT - 1)
                        pe.wait_ge(ot_copied, NC * (g + 1))
                        for t in range(NT):
                            pe.transpose(ps[:, 6 + t // 4, (t % 4) * P:(t % 4 + 1) * P], ot[:, t * P:(t + 1) * P],
                                         ident[:, :]).then_inc(back_mm, 1)
                    pe.wait_ge(gated, 1)
                    for t in range(NT):
                        pe.transpose(ps[:, t // 4, (t % 4) * P:(t % 4 + 1) * P], flat[:, t, :],
                                     ident[:, :]).then_inc(flat_t_mm, 1)
                    for t in range(NT):
                        if t % 4 == 0:
                            pe.wait_ge(flat_t_ready, t // 4 + 1)
                        pe.matmul(ps[:, 2 + t // 4, (t % 4) * D:(t % 4 + 1) * D], flat_t[:, t * P:(t + 1) * P],
                                  wout[:, :], start=True, stop=True).then_inc(out_mm, 1)
            clear(nc, sems)


def build(nc, a, out):
    mid = [nc.dram_tensor(f"x_after_{i}", (B, N, D), F32).ap() for i in range(3)]
    table = nc.dram_tensor("bias_by_distance", (H1, 2, TAB), F32).ap()
    parts = nc.dram_tensor("q_k_parts", (2, 2, P, N), F32).ap()
    linear_attention(nc, a["x"], mid[0], a["L0_WQ"], a["L0_WK"], a["L0_WVT"], a["L0_Wfc"], a["gamma"], a["beta"],
                     a["ident"], a["headcol"], a["headsel"])
    for layer, x_in, x_out in ((0, mid[0], mid[1]), (1, mid[2], out)):
        if layer == 1:
            window_attention(nc, mid[1], mid[2], a["WqkvT"], a["bqkv"], a["WgateT"], a["bgate"], a["WoutT"], a["bout"],
                             a["pos_bias"], a["offsets"], a["ident"], a["dist"], a["ones_rows"], a["turned"], table, parts)
        w = {k: a[f"L{layer}_{k}"] for k in ("w1t", "w1s", "w2t", "w2s", "h1t", "h1s", "h2t", "h2s", "w3t", "w3s")}
        feed_forward(nc, f"ff{layer}_", x_in, x_out, c_ident=a["ident"], **w)


def constants():
    part, col = np.arange(P)[:, None], np.arange(P)[None, :]
    headcol = np.zeros((P, NF, 32), np.float32)
    headsel = np.zeros((P, NF, P), np.float32)
    for f in range(NF):
        headcol[:, f, :] = np.arange(32)[None, :] == 2 * f + part // DK
        headsel[:, f, :] = part % 32 == 2 * f + col // DK
    e = np.arange(TAB, dtype=np.float32) - P
    dist = np.concatenate([e, REACH - e])[None, :].repeat(NOFF, 0)
    ones_rows = (part // 2 == 48 + np.arange(GH)[None, :]).astype(np.float32)
    return {"ident": np.eye(P, dtype=np.float32), "turned": np.eye(P, dtype=np.float32)[::-1].copy(),
            "headcol": headcol.reshape(P, -1), "headsel": headsel.reshape(P, -1),
            "dist": np.ascontiguousarray(dist), "ones_rows": ones_rows}


def kernel(**inputs):
    import concourse.bacc as bacc
    from concourse.bass_utils import run_bass_kernel_spmd as run

    def take(name):
        return np.ascontiguousarray(inputs[name])

    def flip(name):
        return np.ascontiguousarray(np.asarray(inputs[name]).T)

    arrays = {"x": take("L0_attn_inputs"), "L0_WQ": take("L0_attn_W_Q"), "L0_WK": take("L0_attn_W_K"),
              "L0_WVT": flip("L0_attn_W_V"), "L0_Wfc": take("L0_attn_W_fc"), "gamma": take("L0_attn_gamma"),
              "beta": take("L0_attn_beta"), "WqkvT": flip("L1_attn_Wqkv"), "bqkv": take("L1_attn_bqkv"),
              "WgateT": flip("L1_attn_Wgate"), "bgate": take("L1_attn_bgate"), "WoutT": flip("L1_attn_Wout"),
              "bout": take("L1_attn_bout"), "pos_bias": take("L1_attn_pos_bias"), "offsets": take("L1_attn_offsets")}
    for layer in (0, 1):
        for w in ("w1", "w2", "h1", "h2", "w3"):
            arrays[f"L{layer}_{w}t"] = flip(f"L{layer}_ffn_{w}_w")
            scale = take(f"L{layer}_ffn_{w}_s")
            arrays[f"L{layer}_{w}s"] = scale if w == "w3" else np.ascontiguousarray(scale.reshape(NB, P).T)
    arrays.update(constants())

    nc = bacc.Bacc("TRN2", target_bir_lowering=False, num_devices=1)
    aps = {k: nc.dram_tensor(f"in_{k}", v.shape, mybir.dt.from_np(v.dtype), kind="ExternalInput").ap()
           for k, v in arrays.items()}
    out = nc.dram_tensor("out_x", (B, N, D), F32, kind="ExternalOutput").ap()
    build(nc, aps, out)
    r = run(nc, [{f"in_{k}": v for k, v in arrays.items()}], core_ids=[0])
    return r.results[0]["out_x"]
```

```python
import numpy as np
from contextlib import ExitStack

import concourse.bass as bass
from concourse import mybir

F32 = mybir.dt.float32
F32R = mybir.dt.float32r
I32 = mybir.dt.int32
ALU = mybir.AluOpType
ACT = mybir.ActivationFunctionType
AX = mybir.AxisListType

P = 128
B, N, D = 8, 1024, 128
NT = N // P
CH = 512
NC = N // CH
H0, DK = 16, 64
NF = H0 * DK // P
HID = 512
NB = HID // P
H1, HD = 16, 8
NG, GH = 4, 4
NOFF = 68
REACH = 192
WIN = P + REACH
TAB = P + WIN
EPS = 1e-5
DEN_EPS = 1e-8
FAR = 1e30


def f32(ap):
    return ap.bitcast(F32)


class Norm:

    def __init__(self, nc, sb, sem, tag):
        self.nc = nc
        self.stats = sb(f"{tag}_stats", [P, NT, 6])
        self.mean_var = sb(f"{tag}_mean_var", [P, NT, 2])
        self.var_eps = sb(f"{tag}_var_eps", [P, NT])
        self.rstd = sb(f"{tag}_rstd", [P, NT])
        self.stats_done = sem(f"{tag}_stats_done")
        self.moments_done = sem(f"{tag}_moments_done")
        self.eps_added = sem(f"{tag}_eps_added")
        self.rstd_ready = sem(f"{tag}_rstd_ready")

    def statistics(self, src, tiles=range(NT)):
        for t in tiles:
            self.nc.vector.bn_stats(self.stats[:, t, :], src[:, t, 0:D]).then_inc(self.stats_done, 1)

    def moments(self, dve):
        dve.wait_ge(self.stats_done, NT)
        for t in range(NT):
            self.nc.vector.bn_aggr(self.mean_var[:, t, :], self.stats[:, t, :]).then_inc(self.moments_done, 1)

    def root(self, pool, minus_half):
        pool.wait_ge(self.moments_done, NT)
        self.nc.gpsimd.tensor_scalar(self.var_eps[:, :], self.mean_var[:, :, 1], EPS, None,
                                     ALU.add).then_inc(self.eps_added, 1)
        pool.wait_ge(self.eps_added, 1)
        self.nc.gpsimd.tensor_tensor(self.rstd[:, :], self.var_eps[:, :], minus_half,
                                     ALU.pow).then_inc(self.rstd_ready, 1)

    def apply(self, dve, out, src, done, tiles=range(NT)):
        dve.wait_ge(self.moments_done, NT)
        dve.wait_ge(self.rstd_ready, 1)
        for t in tiles:
            self.nc.vector.tensor_scalar(out[:, t, 0:D], src[:, t, 0:D], self.mean_var[:, t, 0:1],
                                         self.rstd[:, t:t + 1], ALU.subtract, ALU.mult).then_inc(done, 1)


def turns(nc, sems, turn, head, tail):
    head()
    clear(nc, sems)
    turn(0, 0, has_tail=False)
    clear(nc, sems)
    with nc.Fori(0, B // 2 - 1) as i:
        for s in (1, 0):
            turn(i * 2 + (2 - s), s)
            clear(nc, sems)
    turn(B - 1, 1, has_head=False)
    clear(nc, sems)
    tail()
    clear(nc, sems)


def rows(ap, k):
    return ap[k].rearrange("(t p) d -> p t d", p=P)


def split(nc, eng, hi, lo, x, done, base):
    nc.vector.tensor_copy(hi, x).then_inc(done, 1)
    eng.wait_ge(done, base + 1)
    nc.vector.tensor_tensor(lo, x, f32(hi), ALU.subtract).then_inc(done, 1)


def clear(nc, sems):
    with nc.Block() as block:
        @block.sync
        def _(sp):
            for s in sems:
                sp.sem_clear(s)


def linear_attention(nc, x_in, x_out, W_Q, W_K, W_VT, W_fc, gamma, beta, c_ident, c_headcol, c_headsel):
    with ExitStack() as ctx:
        def sb(name, shape, dt=F32):
            return ctx.enter_context(nc.sbuf_tensor("la_" + name, shape, dt))

        sems = []

        def sem(name):
            s = ctx.enter_context(nc.semaphore("la_" + name))
            sems.append(s)
            return s

        ps = ctx.enter_context(nc.psum_tensor("la_ps", [P, 8, CH], F32))

        ident = sb("ident", [P, P])
        wq_hi, wq_lo = sb("wq_hi", [P, H0 * DK], F32R), sb("wq_lo", [P, H0 * DK], F32R)
        wk_hi, wk_lo = sb("wk_hi", [P, H0 * DK], F32R), sb("wk_lo", [P, H0 * DK], F32R)
        wvt, wfc = sb("wvt", [P, NF, D]), sb("wfc", [P, NF, D])
        wvfc = sb("wvfc", [P, H0, D])
        headcol = sb("headcol", [P, NF, 32])
        headsel = sb("headsel", [P, NF, P], F32R)
        gamma_b, beta_b = sb("gamma_b", [P, D]), sb("beta_b", [P, D])
        minus_half = sb("minus_half", [P, NT])

        x = [sb(f"x{i}", [P, NT, D]) for i in range(2)]
        fresh = sb("fresh", [P, NT, D])
        xn = [sb(f"xn{i}", [P, NT, D + 1]) for i in range(2)]
        xt_hi = [sb(f"xt_hi{i}", [P, N], F32R) for i in range(2)]
        xt_lo = [sb(f"xt_lo{i}", [P, N], F32R) for i in range(2)]
        z = [sb(f"z{i}", [P, NT, D]) for i in range(2)]
        kn = sb("kn", [P, 2, H0 * DK])
        kx = sb("kx", [P, NF, D + 1])
        ksum_col = sb("ksum_col", [P, NF, 32])
        kxt = sb("kxt", [P, NF, P])
        m = sb("m", [P, NF, D])
        q = sb("q", [P, NF, N])
        den = [sb(f"den{c}", [P, P]) for c in range(NC)]
        rden = [sb(f"rden{c}", [P, P]) for c in range(NC)]
        rden_hi, rden_lo = sb("rden_hi", [P, NC, 4, P], F32R), sb("rden_lo", [P, NC, 4, P], F32R)
        norm_in = Norm(nc, sb, sem, "norm_in")
        norm_sum = Norm(nc, sb, sem, "norm_sum")
        norm_out = Norm(nc, sb, sem, "norm_out")

        w_in = sem("w_in")
        w_ready = sem("w_ready")
        wvfc_mm = sem("wvfc_mm")
        x_loaded = sem("x_loaded")
        xn_ready = sem("xn_ready")
        xt_mm = sem("xt_mm")
        xt_hi_ready = sem("xt_hi_ready")
        xt_ready = sem("xt_ready")
        k_mm = sem("k_mm")
        k_ready = sem("k_ready")
        kx_mm = sem("kx_mm")
        kx_copied = sem("kx_copied")
        ksum_ready = sem("ksum_ready")
        kxt_mm = sem("kxt_mm")
        kxt_ready = sem("kxt_ready")
        m_mm = sem("m_mm")
        m_ready = sem("m_ready")
        q_mm = sem("q_mm")
        q_ready = sem("q_ready")
        den_mm = sem("den_mm")
        den_step = sem("den_step")
        rden_ready = sem("rden_ready")
        spread_mm = sem("spread_mm")
        qd_ready = sem("qd_ready")
        out_mm = sem("out_mm")
        z_normed = sem("z_normed")
        affine = sem("affine")
        y_ready = sem("y_ready")
        stored = sem("stored")

        with nc.Block() as block:
            @block.sync
            def _(sp):
                sp.dma_start(q[:, 0, :], W_Q).then_inc(w_in, 16)
                sp.dma_start(q[:, 1, :], W_K).then_inc(w_in, 16)
                sp.dma_start(wvt[:, :, :], W_VT.rearrange("(f p) d -> p f d", p=P)).then_inc(w_in, 16)
                sp.dma_start(wfc[:, :, :], W_fc.rearrange("(f p) d -> p f d", p=P)).then_inc(w_in, 16)
                sp.dma_start(ident[:, :], c_ident).then_inc(w_in, 16)
                sp.dma_start(headcol[:, :, :], c_headcol.rearrange("p (f c) -> p f c", f=NF)).then_inc(w_in, 16)
                sp.dma_start(q[:, 2, :], c_headsel).then_inc(w_in, 16)
                sp.dma_start(gamma_b[:, :], gamma.rearrange("(a d) -> a d", a=1).broadcast_to([P, D])).then_inc(w_in, 16)
                sp.dma_start(beta_b[:, :], beta.rearrange("(a d) -> a d", a=1).broadcast_to([P, D])).then_inc(w_in, 16)

            @block.gpsimd
            def _(pool):
                nc.gpsimd.memset(minus_half[:, :], -0.5)
                for i in range(2):
                    nc.gpsimd.memset(xn[i][:, :, D:D + 1], 1.0)

            @block.vector
            def _(dve):
                nc.vector.memset(rden_hi[:, :, :, :].bitcast(F32), 0.0)
                nc.vector.memset(rden_lo[:, :, :, :].bitcast(F32), 0.0)
                dve.wait_ge(w_in, 9 * 16)
                split(nc, dve, wq_hi[:, :], wq_lo[:, :], q[:, 0, :], w_ready, 0)
                split(nc, dve, wk_hi[:, :], wk_lo[:, :], q[:, 1, :], w_ready, 2)
                nc.vector.tensor_copy(headsel[:, :, :].rearrange("p f c -> p (f c)"), q[:, 2, :])
                for n in range(H0 // 4):
                    dve.wait_ge(wvfc_mm, n + 1)
                    nc.vector.tensor_copy(wvfc[:, 4 * n:4 * n + 4, :].rearrange("p h d -> p (h d)"), ps[:, n, :])

            @block.tensor
            def _(pe):
                pe.wait_ge(w_in, 9 * 16)
                for n in range(H0):
                    s, f = n // NF, n % NF
                    mm = pe.matmul(ps[:, n // 4, (n % 4) * D:(n % 4 + 1) * D], wvt[64 * s:64 * s + 64, f, :],
                                   wfc[64 * s:64 * s + 64, f, :], start=True, stop=True)
                    if n % 4 == 3:
                        mm.then_inc(wvfc_mm, 1)
        clear(nc, sems)

        def head_dve(dve, s):
            dve.wait_ge(x_loaded, 16)
            norm_in.statistics(fresh)
            norm_in.moments(dve)
            norm_in.apply(dve, xn[s], fresh, xn_ready)

        def head_pe(pe, s, bank):
            for t in range(NT):
                pe.wait_ge(xn_ready, t + 1)
                pe.transpose(ps[:, bank + t // 4, (t % 4) * P:(t % 4 + 1) * P], xn[s][:, t, 0:D],
                             ident[:, :]).then_inc(xt_mm, 1)

        def head_act(act, s, bank):
            for c in range(NC):
                act.wait_ge(xt_mm, 4 * (c + 1))
                nc.scalar.copy(xt_hi[s][:, c * CH:(c + 1) * CH], ps[:, bank + c, :]).then_inc(xt_hi_ready, 1)

        def head_lower(dve, s, bank):
            for c in range(NC):
                dve.wait_ge(xt_hi_ready, c + 1)
                nc.vector.tensor_tensor(xt_lo[s][:, c * CH:(c + 1) * CH], ps[:, bank + c, :],
                                        f32(xt_hi[s][:, c * CH:(c + 1) * CH]), ALU.subtract).then_inc(xt_ready, 1)

        def tail_dve(dve, s):
            norm_sum.statistics(z[s])
            norm_sum.moments(dve)
            norm_sum.apply(dve, z[s], z[s], z_normed)
            dve.wait_ge(z_normed, NT)
            nc.vector.tensor_tensor(z[s][:, :, :], z[s][:, :, :],
                                    gamma_b[:, None, :].broadcast_to([P, NT, D]), ALU.mult).then_inc(affine, 1)
            dve.wait_ge(affine, 1)
            nc.vector.tensor_tensor(z[s][:, :, :], z[s][:, :, :],
                                    beta_b[:, None, :].broadcast_to([P, NT, D]), ALU.add).then_inc(affine, 1)
            dve.wait_ge(affine, 2)
            norm_out.statistics(z[s])
            norm_out.moments(dve)
            norm_out.apply(dve, z[s], z[s], z_normed)
            dve.wait_ge(z_normed, 2 * NT)
            nc.vector.tensor_tensor(z[s][:, :, :], x[s][:, :, :], z[s][:, :, :], ALU.add).then_inc(y_ready, 1)

        def tail_pool(pool):
            norm_sum.root(pool, minus_half[:, :])
            norm_out.root(pool, minus_half[:, :])

        def tail_store(sp, k, s):
            sp.wait_ge(y_ready, 1)
            sp.dma_start(rows(x_out, k), z[s][:, :, :]).then_inc(stored, 16)

        def head():
            with nc.Block() as block:
                @block.sync
                def _(sp):
                    sp.dma_start(fresh[:, :, :], rows(x_in, 0)).then_inc(x_loaded, 16)

                @block.gpsimd
                def _(pool):
                    norm_in.root(pool, minus_half[:, :])
                    pool.wait_ge(x_loaded, 16)
                    nc.gpsimd.tensor_copy(x[0][:, :, :], fresh[:, :, :])

                @block.scalar
                def _(act):
                    head_act(act, 0, 6)

                @block.vector
                def _(dve):
                    head_dve(dve, 0)
                    head_lower(dve, 0, 6)

                @block.tensor
                def _(pe):
                    head_pe(pe, 0, 6)

        def tail():
            with nc.Block() as block:
                @block.sync
                def _(sp):
                    tail_store(sp, B - 1, 1)
                    sp.wait_ge(stored, 16)

                @block.gpsimd
                def _(pool):
                    tail_pool(pool)

                @block.vector
                def _(dve):
                    tail_dve(dve, 1)

        def turn(k, s, has_head=True, has_tail=True):
            with nc.Block() as block:
                @block.sync
                def _(sp):
                    if has_head:
                        sp.dma_start(fresh[:, :, :], rows(x_in, k + 1)).then_inc(x_loaded, 16)
                    if has_tail:
                        tail_store(sp, k - 1, 1 - s)
                        sp.wait_ge(stored, 16)

                @block.gpsimd
                def _(pool):
                    if has_tail:
                        tail_pool(pool)
                    if has_head:
                        norm_in.root(pool, minus_half[:, :])
                        if has_tail:
                            pool.wait_ge(y_ready, 1)
                        pool.wait_ge(x_loaded, 16)
                        nc.gpsimd.tensor_copy(x[1 - s][:, :, :], fresh[:, :, :])

                @block.scalar
                def _(act):
                    for t in range(NT):
                        for c in range(2):
                            n = 2 * t + c
                            act.wait_ge(k_mm, n + 1)
                            if t >= 2 and c == 0:
                                act.wait_ge(kx_mm, t - 1)
                            nc.scalar.activation(kn[:, t % 2, c * CH:(c + 1) * CH], ps[:, n % 4, :],
                                                 ACT.Sigmoid).then_inc(k_ready, 1)
                    for n in range(NF * NC):
                        c, f = n // NF, n % NF
                        act.wait_ge(q_mm, n + 1)
                        nc.scalar.activation(q[:, f, c * CH:(c + 1) * CH], ps[:, n % 4, :],
                                             ACT.Sigmoid).then_inc(q_ready, 1)
                        if n == 5:
                            for i in range(2):
                                act.wait_ge(kxt_mm, 4 * (i + 1))
                                nc.scalar.copy(kxt[:, 4 * i:4 * i + 4, :].rearrange("p f d -> p (f d)"),
                                               ps[:, 6 + i, :]).then_inc(kxt_ready, 1)
                        if n == 9:
                            for i in range(2):
                                act.wait_ge(m_mm, 4 * (i + 1))
                                nc.scalar.copy(m[:, 4 * i:4 * i + 4, :].rearrange("p f d -> p (f d)"),
                                               ps[:, 6 + i, :]).then_inc(m_ready, 1)
                    if has_head:
                        head_act(act, 1 - s, 6)

                @block.vector
                def _(dve):
                    if has_tail:
                        tail_dve(dve, 1 - s)
                    if has_head:
                        head_dve(dve, 1 - s)
                    dve.wait_ge(kx_mm, NT)
                    for f in range(NF // 2):
                        nc.vector.tensor_copy(kx[:, 2 * f:2 * f + 2, :],
                                              ps[:, 4 + f, 0:2 * (D + 1)].rearrange("p (a d) -> p a d", a=2)
                                              ).then_inc(kx_copied, 1)
                    dve.wait_ge(kx_copied, NF // 2)
                    nc.vector.tensor_tensor(ksum_col[:, :, :], headcol[:, :, :],
                                            kx[:, :, D:D + 1].broadcast_to([P, NF, 32]), ALU.mult).then_inc(ksum_ready, 1)

                    def invert(c):
                        dve.wait_ge(den_mm, c + 1)
                        nc.vector.tensor_scalar(den[c][:, :], ps[:, 4 + c, 0:P], DEN_EPS, None,
                                                ALU.add).then_inc(den_step, 1)
                        dve.wait_ge(den_step, 6 * c + 1)
                        nc.vector.reciprocal(rden[c][:, :], den[c][:, :]).then_inc(den_step, 1)
                        dve.wait_ge(den_step, 6 * c + 2)
                        for g in range(4):
                            nc.vector.tensor_copy(rden_hi[32 * g:32 * g + 32, c, g, :],
                                                  rden[c][32 * g:32 * g + 32, :]).then_inc(den_step, 1)
                        dve.wait_ge(den_step, 6 * c + 6)
                        for g in range(4):
                            nc.vector.tensor_tensor(rden_lo[32 * g:32 * g + 32, c, g, :], rden[c][32 * g:32 * g + 32, :],
                                                    f32(rden_hi[32 * g:32 * g + 32, c, g, :]),
                                                    ALU.subtract).then_inc(rden_ready, 1)

                    invert(0)
                    for n in range(NF * NC):
                        c, f = n // NF, n % NF
                        dve.wait_ge(spread_mm, n + 1)
                        cols = slice(c * CH, (c + 1) * CH)
                        nc.vector.tensor_tensor(q[:, f, cols], q[:, f, cols], ps[:, n % 4, :],
                                                ALU.mult).then_inc(qd_ready, 1)
                        if n == 3:
                            invert(1)
                        if n == NF - 1 and has_head:
                            head_lower(dve, 1 - s, 6)
                    for c in range(NC):
                        dve.wait_ge(out_mm, 4 * (c + 1))
                        nc.vector.tensor_tensor(z[s][:, 4 * c:4 * c + 4, :],
                                                ps[:, 6 + c, :].rearrange("p (t d) -> p t d", t=4),
                                                xn[s][:, 4 * c:4 * c + 4, 0:D], ALU.add)

                @block.tensor
                def _(pe):
                    def three(out, lhs, rhs):
                        pe.matmul(out, lhs[0], rhs[0], start=True, stop=False)
                        pe.matmul(out, lhs[0], rhs[1], start=False, stop=False)
                        return pe.matmul(out, lhs[1], rhs[0], start=False, stop=True)

                    def k_times_x(t):
                        pe.wait_ge(k_ready, 2 * t + 2)
                        for f in range(NF):
                            mm = pe.matmul(ps[:, 4 + f // 2, (f % 2) * (D + 1):(f % 2 + 1) * (D + 1)],
                                           kn[:, t % 2, f * P:(f + 1) * P], xn[s][:, t, :],
                                           start=(t == 0 and f % 2 == 0), stop=(t == NT - 1), skip_group_check=True)
                        mm.then_inc(kx_mm, 1)

                    for t in range(NT):
                        toks = slice(t * P, (t + 1) * P)
                        for c in range(2):
                            n = 2 * t + c
                            if n >= 4:
                                pe.wait_ge(k_ready, n - 3)
                            cols = slice(c * CH, (c + 1) * CH)
                            three(ps[:, n % 4, :], (xt_hi[s][:, toks], xt_lo[s][:, toks]),
                                  (wk_hi[:, cols], wk_lo[:, cols])).then_inc(k_mm, 1)
                        if t >= 1:
                            k_times_x(t - 1)
                    k_times_x(NT - 1)

                    def transpose_sums():
                        pe.wait_ge(kx_copied, NF // 2)
                        for f in range(NF):
                            pe.transpose(ps[:, 6 + f // 4, (f % 4) * P:(f % 4 + 1) * P], kx[:, f, 0:D],
                                         ident[:, :]).then_inc(kxt_mm, 1)

                    def times_wvfc():
                        pe.wait_ge(kxt_ready, 2)
                        for f in range(NF):
                            for h in range(2):
                                mm = pe.matmul(ps[64 * h:64 * h + 64, 6 + f // 4, (f % 4) * P:(f % 4 + 1) * P],
                                               kxt[:, f, 64 * h:64 * h + 64], wvfc[:, NF * h + f, :],
                                               start=True, stop=True)
                            mm.then_inc(m_mm, 1)

                    def den_of(n):
                        c, f = n // NF, n % NF
                        pe.wait_ge(q_ready, n + 1)
                        pe.wait_ge(ksum_ready, 1)
                        for g in range(4):
                            mm = pe.matmul(ps[32 * g:32 * g + 32, 4 + c, 0:P], ksum_col[:, f, :],
                                           q[:, f, c * CH + P * g:c * CH + P * (g + 1)],
                                           start=(f == 0), stop=(f == NF - 1))
                        if f == NF - 1:
                            mm.then_inc(den_mm, 1)

                    LAG = 4
                    for n in range(NF * NC):
                        c, f = n // NF, n % NF
                        blk, cols = slice(f * P, (f + 1) * P), slice(c * CH, (c + 1) * CH)
                        if n >= 4:
                            pe.wait_ge(q_ready, n - 3)
                        else:
                            pe.wait_ge(k_ready, 2 * NT - 3 + n)
                        three(ps[:, n % 4, :], (wq_hi[:, blk], wq_lo[:, blk]),
                              (xt_hi[s][:, cols], xt_lo[s][:, cols])).then_inc(q_mm, 1)
                        if n == 3:
                            transpose_sums()
                        if n == 7:
                            times_wvfc()
                        if n >= LAG:
                            den_of(n - LAG)
                    for n in range(NF * NC - LAG, NF * NC):
                        den_of(n)

                    def spread(n):
                        c, f = n // NF, n % NF
                        if n >= 4:
                            pe.wait_ge(qd_ready, n - 3)
                        else:
                            pe.wait_ge(q_ready, NF * NC - 3 + n)
                        pe.wait_ge(rden_ready, 4 * (c + 1))
                        pe.matmul(ps[:, n % 4, :], headsel[:, f, :],
                                  rden_hi[:, c, :, :].rearrange("p a n -> p (a n)"), start=True, stop=False)
                        pe.matmul(ps[:, n % 4, :], headsel[:, f, :],
                                  rden_lo[:, c, :, :].rearrange("p a n -> p (a n)"),
                                  start=False, stop=True).then_inc(spread_mm, 1)

                    def out_of(t):
                        c = t // 4
                        pe.wait_ge(qd_ready, NF * (c + 1))
                        if has_head:
                            pe.wait_ge(xt_ready, c + 1)
                        for f in range(NF):
                            mm = pe.matmul(ps[:, 6 + c, (t % 4) * D:(t % 4 + 1) * D], q[:, f, t * P:(t + 1) * P],
                                           m[:, f, :], start=(f == 0), stop=(f == NF - 1))
                        mm.then_inc(out_mm, 1)

                    for n in range(4):
                        spread(n)
                    pe.wait_ge(m_ready, 2)
                    if has_head:
                        head_pe(pe, 1 - s, 6)
                    for n in range(4, NF + 4):
                        spread(n)
                    for t in range(4):
                        out_of(t)
                        spread(NF + 4 + t)
                    for t in range(4, NT):
                        out_of(t)

        turns(nc, sems, turn, head, tail)


def feed_forward(nc, tag, x_in, x_out, w1t, w1s, w2t, w2s, h1t, h1s, h2t, h2s, w3t, w3s, c_ident):
    with ExitStack() as ctx:
        def sb(name, shape, dt=F32):
            return ctx.enter_context(nc.sbuf_tensor(tag + name, shape, dt))

        sems = []

        def sem(name):
            s = ctx.enter_context(nc.semaphore(tag + name))
            sems.append(s)
            return s

        ps = ctx.enter_context(nc.psum_tensor(tag + "ps", [P, 8, CH], F32))

        ident = sb("ident", [P, P])
        w1, w2 = sb("w1", [P, HID], F32R), sb("w2", [P, HID], F32R)
        h1, h2 = sb("h1", [P, NB, HID], F32R), sb("h2", [P, NB, HID], F32R)
        w3 = sb("w3", [P, NB, D], F32R)
        raw = sb("raw", [P, 2 * HID + 2 * NB * HID + NB * D])
        s1, s2, s3, s4 = (sb(f"s{i}", [P, NB]) for i in range(4))
        s5 = sb("s5", [P, D])
        minus_half = sb("minus_half", [P, NT])

        x = [sb(f"x{i}", [P, NT, D]) for i in range(2)]
        fresh = sb("fresh", [P, NT, D])
        xn = sb("xn", [P, NT, D])
        xt_hi = [sb(f"xt_hi{i}", [P, N], F32R) for i in range(2)]
        xt_lo = [sb(f"xt_lo{i}", [P, N], F32R) for i in range(2)]
        z = [sb(f"z{i}", [P, NT, D]) for i in range(2)]
        hid_hi = [sb(f"hid_hi{i}", [P, NB, CH], F32R) for i in range(3)]
        hid_lo = [sb(f"hid_lo{i}", [P, NB, CH], F32R) for i in range(3)]
        gate = sb("gate", [P, 3, CH])
        full = sb("full", [P, 3, CH])
        norm_in = Norm(nc, sb, sem, "norm_in")
        norm_out = Norm(nc, sb, sem, "norm_out")

        w_in = sem("w_in")
        x_loaded = sem("x_loaded")
        xn_ready = sem("xn_ready")
        xt_mm = sem("xt_mm")
        xt_hi_ready = sem("xt_hi_ready")
        xt_ready = sem("xt_ready")
        up_mm = sem("up_mm")
        gate_ready = sem("gate_ready")
        full_ready = sem("full_ready")
        hi_ready = sem("hi_ready")
        lo_ready = sem("lo_ready")
        hid_mm = sem("hid_mm")
        gelu_full = sem("gelu_full")
        gelu_hi = sem("gelu_hi")
        gelu_lo = sem("gelu_lo")
        out_mm = sem("out_mm")
        late_out_mm = sem("late_out_mm")
        late_z_ready = sem("late_z_ready")
        z_normed = sem("z_normed")
        y_ready = sem("y_ready")
        stored = sem("stored")

        o1, o2 = 2 * HID, 2 * HID + NB * HID
        o3 = o2 + NB * HID
        with nc.Block() as block:
            @block.sync
            def _(sp):
                sp.dma_start(raw[:, 0:HID], w1t).then_inc(w_in, 16)
                sp.dma_start(raw[:, HID:o1], w2t).then_inc(w_in, 16)
                sp.dma_start(raw[:, o1:o2].rearrange("p (k o) -> p k o", k=NB),
                             h1t.rearrange("(k p) o -> p k o", p=P)).then_inc(w_in, 16)
                sp.dma_start(raw[:, o2:o3].rearrange("p (k o) -> p k o", k=NB),
                             h2t.rearrange("(k p) o -> p k o", p=P)).then_inc(w_in, 16)
                sp.dma_start(raw[:, o3:].rearrange("p (k o) -> p k o", k=NB),
                             w3t.rearrange("(k p) o -> p k o", p=P)).then_inc(w_in, 16)
                for s, src in ((s1, w1s), (s2, w2s), (s3, h1s), (s4, h2s)):
                    sp.dma_start(s[:, :], src).then_inc(w_in, 16)
                sp.dma_start(s5[:, :], w3s.rearrange("(a d) -> a d", a=1).broadcast_to([P, D])).then_inc(w_in, 16)
                sp.dma_start(ident[:, :], c_ident).then_inc(w_in, 16)

            @block.gpsimd
            def _(pool):
                nc.gpsimd.memset(minus_half[:, :], -0.5)

            @block.vector
            def _(dve):
                dve.wait_ge(w_in, 11 * 16)
                nc.vector.tensor_copy(w1[:, :], raw[:, 0:HID])
                nc.vector.tensor_copy(w2[:, :], raw[:, HID:o1])
                nc.vector.tensor_copy(h1[:, :, :].rearrange("p k o -> p (k o)"), raw[:, o1:o2])
                nc.vector.tensor_copy(h2[:, :, :].rearrange("p k o -> p (k o)"), raw[:, o2:o3])
                nc.vector.tensor_copy(w3[:, :, :].rearrange("p k o -> p (k o)"), raw[:, o3:])
        clear(nc, sems)

        SRC = ((None, 0, 2), (None, 1, 0))
        DST = ((0, 2, 1), (1, 0, 2))

        TR = 6

        def bank_of(n):
            return 6 + n if n < 2 else (n - 2) % 6

        LAST_UP = (6, 7, 5)

        def head_pe(pe, s):
            for t in range(NT):
                pe.wait_ge(xn_ready, t + 1)
                pe.transpose(ps[:, TR + t // 4, (t % 4) * P:(t % 4 + 1) * P], xn[:, t, :],
                             ident[:, :]).then_inc(xt_mm, 1)

        def head_act(act, s, c):
            act.wait_ge(xt_mm, 4 * (c + 1))
            nc.scalar.copy(xt_hi[s][:, c * CH:(c + 1) * CH], ps[:, TR + c, :]).then_inc(xt_hi_ready, 1)

        def head_lower(dve, s, c):
            dve.wait_ge(xt_hi_ready, c + 1)
            nc.vector.tensor_tensor(xt_lo[s][:, c * CH:(c + 1) * CH], ps[:, TR + c, :],
                                    f32(xt_hi[s][:, c * CH:(c + 1) * CH]), ALU.subtract).then_inc(xt_ready, 1)

        first, second = range(NT // 2), range(NT // 2, NT)

        def tail_step(dve, s, i):
            if i == 0:
                norm_out.statistics(z[s], first)
            elif i == 1:
                norm_out.statistics(z[s], second)
            elif i == 2:
                norm_out.moments(dve)
            elif i == 3:
                norm_out.apply(dve, z[s], z[s], z_normed, first)
            elif i == 4:
                norm_out.apply(dve, z[s], z[s], z_normed, second)
            elif i == 5:
                dve.wait_ge(z_normed, NT)
                nc.vector.tensor_tensor(z[s][:, :, :], x[s][:, :, :], z[s][:, :, :], ALU.add).then_inc(y_ready, 1)

        def head_step(dve, s, i):
            if i == 0:
                dve.wait_ge(x_loaded, 16)
                norm_in.statistics(fresh, first)
            elif i == 1:
                norm_in.statistics(fresh, second)
            elif i == 2:
                norm_in.moments(dve)
            elif i == 3:
                norm_in.apply(dve, xn, fresh, xn_ready, first)
            elif i == 4:
                norm_in.apply(dve, xn, fresh, xn_ready, second)

        def out_of(pe, c, t, done):
            src, toks = DST[c][2], slice(t * P, (t + 1) * P)
            for k_ in range(NB):
                pe.matmul(ps[:, TR + c, t * D:(t + 1) * D], hid_hi[src][:, k_, toks],
                          w3[:, k_, :], start=(k_ == 0), stop=False)
                mm = pe.matmul(ps[:, TR + c, t * D:(t + 1) * D], hid_lo[src][:, k_, toks],
                               w3[:, k_, :], start=False, stop=(k_ == NB - 1))
            mm.then_inc(done, 1)

        def z_of(dve, s, c, done):
            dve.wait_ge(done, 4)
            return nc.vector.tensor_tensor(z[s][:, 4 * c:4 * c + 4, :],
                                           ps[:, TR + c, :].rearrange("p (t d) -> p t d", t=4),
                                           s5[:, None, :].broadcast_to([P, 4, D]), ALU.mult)

        def late_z(dve, s):
            z_of(dve, s, 1, late_out_mm).then_inc(late_z_ready, 1)

        def tail_store(sp, k, s):
            sp.wait_ge(y_ready, 1)
            sp.dma_start(rows(x_out, k), z[s][:, :, :]).then_inc(stored, 16)

        def head():
            with nc.Block() as block:
                @block.sync
                def _(sp):
                    sp.dma_start(fresh[:, :, :], rows(x_in, 0)).then_inc(x_loaded, 16)

                @block.gpsimd
                def _(pool):
                    norm_in.root(pool, minus_half[:, :])
                    pool.wait_ge(x_loaded, 16)
                    nc.gpsimd.tensor_copy(x[0][:, :, :], fresh[:, :, :])

                @block.scalar
                def _(act):
                    for c in range(NC):
                        head_act(act, 0, c)

                @block.vector
                def _(dve):
                    for i in range(5):
                        head_step(dve, 0, i)
                    for c in range(NC):
                        head_lower(dve, 0, c)

                @block.tensor
                def _(pe):
                    head_pe(pe, 0)

        def tail():
            with nc.Block() as block:
                @block.sync
                def _(sp):
                    tail_store(sp, B - 1, 1)
                    sp.wait_ge(stored, 16)

                @block.gpsimd
                def _(pool):
                    norm_out.root(pool, minus_half[:, :])

                @block.vector
                def _(dve):
                    late_z(dve, 1)
                    dve.wait_ge(late_z_ready, 1)
                    for i in range(6):
                        tail_step(dve, 1, i)

                @block.tensor
                def _(pe):
                    for t in range(4):
                        out_of(pe, 1, t, late_out_mm)

        def turn(k, s, has_head=True, has_tail=True):
            with nc.Block() as block:
                @block.sync
                def _(sp):
                    if has_head:
                        sp.dma_start(fresh[:, :, :], rows(x_in, k + 1)).then_inc(x_loaded, 16)
                    if has_tail:
                        tail_store(sp, k - 1, 1 - s)
                        sp.wait_ge(stored, 16)

                @block.gpsimd
                def _(pool):
                    if has_head:
                        norm_in.root(pool, minus_half[:, :])
                    if has_tail:
                        norm_out.root(pool, minus_half[:, :])
                        pool.wait_ge(y_ready, 1)
                    if has_head:
                        pool.wait_ge(x_loaded, 16)
                        nc.gpsimd.tensor_copy(x[1 - s][:, :, :], fresh[:, :, :])

                @block.scalar
                def _(act):
                    def upper(n):
                        act.wait_ge(full_ready, n + 1)
                        nc.scalar.copy(hid_hi[DST[n // NB][0]][:, n % NB, :], full[:, n % 3, :]).then_inc(hi_ready, 1)

                    for n in range(NB * NC):
                        act.wait_ge(up_mm, n + 1)
                        if n >= 3:
                            act.wait_ge(full_ready, n - 2)
                        nc.scalar.activation(gate[:, n % 3, :], ps[:, n % 3, :], ACT.Silu,
                                             scale=s1[:, n % NB:n % NB + 1]).then_inc(gate_ready, 1)
                        if n >= 1:
                            upper(n - 1)
                    upper(NB * NC - 1)
                    for n in range(2 * NB * NC):
                        stage, c, o = 1 + n // (NB * NC), n // NB % NC, n % NB
                        scale = (s3, s4)[stage - 1][:, o:o + 1]
                        act.wait_ge(hid_mm, n + 1)
                        nc.scalar.activation(hid_hi[DST[c][stage]][:, o, :], ps[:, bank_of(n), :], ACT.Gelu,
                                             scale=scale).then_inc(gelu_hi, 1)
                        if n >= 3:
                            act.wait_ge(gelu_lo, n - 2)
                        else:
                            act.wait_ge(lo_ready, NB * NC)
                        nc.scalar.activation(full[:, n % 3, :], ps[:, bank_of(n), :], ACT.Gelu,
                                             scale=scale).then_inc(gelu_full, 1)
                        if has_head and n in (5, 6):
                            head_act(act, 1 - s, n - 5)

                @block.vector
                def _(dve):
                    def lower(n):
                        dve.wait_ge(hi_ready, n + 1)
                        buf = DST[n // NB][0]
                        nc.vector.tensor_tensor(hid_lo[buf][:, n % NB, :], full[:, n % 3, :],
                                                f32(hid_hi[buf][:, n % NB, :]), ALU.subtract).then_inc(lo_ready, 1)

                    for n in range(NB * NC):
                        dve.wait_ge(gate_ready, n + 1)
                        if n >= 3:
                            dve.wait_ge(lo_ready, n - 2)
                        nc.vector.scalar_tensor_tensor(out=full[:, n % 3, :], in0=ps[:, 3 + n % 3, :],
                                                       scalar=s2[:, n % NB:n % NB + 1], in1=gate[:, n % 3, :],
                                                       op0=ALU.mult, op1=ALU.mult).then_inc(full_ready, 1)
                        if n >= 1:
                            lower(n - 1)
                    lower(NB * NC - 1)
                    if has_tail:
                        late_z(dve, 1 - s)
                    for n in range(2 * NB * NC):
                        stage, c, o = 1 + n // (NB * NC), n // NB % NC, n % NB
                        buf = DST[c][stage]
                        dve.wait_ge(gelu_full, n + 1)
                        nc.vector.tensor_tensor(hid_lo[buf][:, o, :], full[:, n % 3, :], f32(hid_hi[buf][:, o, :]),
                                                ALU.subtract).then_inc(gelu_lo, 1)
                        if has_tail:
                            if n == 4:
                                dve.wait_ge(late_z_ready, 1)
                            for i in {4: (0,), 5: (1, 2), 7: (3,), 8: (4,), 9: (5,)}.get(n, ()):
                                tail_step(dve, 1 - s, i)
                        if has_head:
                            for i in {0: (0,), 1: (1, 2), 3: (3,), 4: (4,)}.get(n, ()):
                                head_step(dve, 1 - s, i)
                            if n in (6, 7):
                                head_lower(dve, 1 - s, n - 6)
                    z_of(dve, s, 0, out_mm)

                @block.tensor
                def _(pe):
                    for n in range(NB * NC):
                        c, f = n // NB, n % NB
                        cols, blk = slice(c * CH, (c + 1) * CH), slice(f * P, (f + 1) * P)
                        if n >= 3:
                            pe.wait_ge(full_ready, n - 2)
                        pe.matmul(ps[:, n % 3, :], w1[:, blk], xt_hi[s][:, cols], start=True, stop=False)
                        pe.matmul(ps[:, n % 3, :], w1[:, blk], xt_lo[s][:, cols], start=False, stop=True)
                        pe.matmul(ps[:, 3 + n % 3, :], w2[:, blk], xt_hi[s][:, cols], start=True, stop=False)
                        pe.matmul(ps[:, 3 + n % 3, :], w2[:, blk], xt_lo[s][:, cols], start=False,
                                  stop=True).then_inc(up_mm, 1)
                        if n >= 4 and has_tail:
                            out_of(pe, 1, n - 4, late_out_mm)
                    for n in range(2 * NB * NC):
                        stage, c, o = 1 + n // (NB * NC), n // NB % NC, n % NB
                        w, src = (h1, h2)[stage - 1], SRC[c][stage]
                        if o == 0:
                            if stage == 1:
                                pe.wait_ge(lo_ready, NB * (c + 1))
                            else:
                                pe.wait_ge(gelu_lo, NB * (c + 1))
                        if n < 2:
                            if n == 1 and has_tail:
                                pe.wait_ge(late_z_ready, 1)
                        elif n < 8:
                            pe.wait_ge(full_ready, LAST_UP[(n - 2) % 3] + 1)
                        else:
                            pe.wait_ge(gelu_full, n - 5)
                        for k_ in range(NB):
                            pe.matmul(ps[:, bank_of(n), :], w[:, k_, o * P:(o + 1) * P], hid_hi[src][:, k_, :],
                                      start=(k_ == 0), stop=False)
                            mm = pe.matmul(ps[:, bank_of(n), :], w[:, k_, o * P:(o + 1) * P], hid_lo[src][:, k_, :],
                                           start=False, stop=(k_ == NB - 1))
                        mm.then_inc(hid_mm, 1)
                        if has_head and n == 5:
                            head_pe(pe, 1 - s)
                    pe.wait_ge(gelu_lo, NB * NC + NB)
                    if has_head:
                        pe.wait_ge(xt_ready, 1)
                    for t in range(4):
                        out_of(pe, 0, t, out_mm)

        turns(nc, sems, turn, head, tail)


def window_attention(nc, x_in, x_out, WqkvT, bqkv, WgateT, bgate, WoutT, bout, pos_bias, offsets,
                     c_ident, c_dist, c_ones_rows, c_turned, table, parts):
    with ExitStack() as ctx:
        def sb(name, shape, dt=F32):
            return ctx.enter_context(nc.sbuf_tensor("wa_" + name, shape, dt))

        sems = []

        def sem(name):
            s = ctx.enter_context(nc.semaphore("wa_" + name))
            sems.append(s)
            return s

        ps = ctx.enter_context(nc.psum_tensor("wa_ps", [P, 8, CH], F32))

        BY_VECTOR = (2, 2, 2, 4)
        vector_heads = [GH * g + i for g in range(NG) for i in range(BY_VECTOR[g])]
        tensor_heads = [h for h in range(H1) if h not in vector_heads]

        ident, ident_r = sb("ident", [P, P]), sb("ident_r", [P, P], F32R)
        wqk_hi, wqk_lo = sb("wqk_hi", [P, 2 * D], F32R), sb("wqk_lo", [P, 2 * D], F32R)
        wvg_hi, wvg_lo = sb("wvg_hi", [P, 2 * D], F32R), sb("wvg_lo", [P, 2 * D], F32R)
        wout = sb("wout", [P, D])
        bq, bk = sb("bq", [P, 1]), sb("bk", [P, 1])
        bvg_b, bout_b = sb("bvg_b", [P, 2 * D]), sb("bout_b", [P, D])
        minus_half = sb("minus_half", [P, NT])
        pos, off_i, off_f = sb("pos", [NOFF, H1]), sb("off_i", [NOFF, 1], I32), sb("off_f", [NOFF, 1])
        ones = sb("ones", [NOFF, H1])
        ones_rows = sb("ones_rows", [P, GH])
        bias_qk = sb("bias_qk", [P, H1, WIN])
        bias_kq = sb("bias_kq", [P, len(vector_heads), WIN])
        bias_kq_hi = sb("bias_kq_hi", [P, len(tensor_heads), WIN], F32R)
        bias_kq_lo = sb("bias_kq_lo", [P, len(tensor_heads), WIN], F32R)

        x = [sb(f"x{i}", [P, NT, D]) for i in range(2)]
        gate = [sb(f"gate{i}", [P, NT, D]) for i in range(2)]
        xn = sb("xn", [P, NT, D])
        z = xn
        xt_hi, xt_lo = sb("xt_hi", [P, N], F32R), sb("xt_lo", [P, N], F32R)
        qk_hi, qk_lo = sb("qk_hi", [P, 2, N], F32R), sb("qk_lo", [P, 2, N], F32R)
        vp = sb("vp", [P, NT, H1, 32])
        qcat = sb("qcat", [P, NG, N], F32R)
        kz = sb("kz", [P, 3, GH, N], F32R)
        top = sb("top", [P, 2, NT, GH])
        negtop = sb("negtop", [P, NT, P])
        prob = sb("prob", [P, 3 * GH * WIN])
        prob_of = prob[:, :].rearrange("p (a i n) -> p a i n", a=3, i=GH)
        qk = prob[:, 0:2 * N].rearrange("p (a n) -> p a n", a=2)
        flat_t = prob[:, 2 * N:3 * N]
        junk = f32(qk_lo[:, :, :]).rearrange("p a n -> p (a n)")[:, 0:4 * WIN].rearrange("p (a n) -> p a n", a=4)
        ot = sb("ot", [P, N])
        rden = sb("rden", [P, 4, GH, 1])
        flat = sb("flat", [P, NT, D])
        raw = x[0][:, :, :].rearrange("p t d -> p (t d)")[:, 0:4 * D]
        dist = xn[:, :, :].rearrange("p t d -> p (t d)")[0:NOFF, 0:2 * TAB]
        hit = ot[0:NOFF, 0:2 * TAB]
        missing = x[1][:, :, :].rearrange("p t d -> p (t d)")[0:H1, 0:2 * TAB].rearrange("p (a n) -> p a n", a=2)
        bias_row = gate[0][:, :, :].rearrange("p t d -> p (t d)")[0:H1, 0:2 * TAB].rearrange("p (a n) -> p a n", a=2)
        turned = gate[1][:, 0, :]
        norm_in = Norm(nc, sb, sem, "norm_in")
        norm_out = Norm(nc, sb, sem, "norm_out")

        w_in = sem("w_in")
        w_ready = sem("w_ready")
        hit_ready = sem("hit_ready")
        table_mm = sem("table_mm")
        table_step = sem("table_step")
        table_out = sem("table_out")
        table_in = sem("table_in")
        flip_mm = sem("flip_mm")
        flip_copied = sem("flip_copied")
        x_loaded = sem("x_loaded")
        xn_ready = sem("xn_ready")
        xt_mm = sem("xt_mm")
        xt_hi_ready = sem("xt_hi_ready")
        xt_ready = sem("xt_ready")
        qk_mm = sem("qk_mm")
        qk_biased = sem("qk_biased")
        qk_ready = sem("qk_ready")
        parts_out = sem("parts_out")
        q_in = sem("q_in")
        k_in = [sem(f"k_in{i}") for i in range(3)]
        rows_zero = sem("rows_zero")
        vg_mm = sem("vg_mm")
        v_ready = sem("v_ready")
        gate_ready = sem("gate_ready")
        s_mm = sem("s_mm")
        top_taken = sem("top_taken")
        bias_added = sem("bias_added")
        top_step = sem("top_step")
        top_mm = sem("top_mm")
        top_ready = sem("top_ready")
        prob_ready = sem("prob_ready")
        pv_mm = sem("pv_mm")
        ot_copied = sem("ot_copied")
        back_mm = sem("back_mm")
        rden_ready = sem("rden_ready")
        flat_ready = sem("flat_ready")
        last_back_mm = sem("last_back_mm")
        last_rden_ready = sem("last_rden_ready")
        last_flat_ready = sem("last_flat_ready")
        gated = sem("gated")
        flat_t_mm = sem("flat_t_mm")
        flat_t_ready = sem("flat_t_ready")
        out_mm = sem("out_mm")
        z_ready = sem("z_ready")
        z_normed = sem("z_normed")
        y_ready = sem("y_ready")
        stored = sem("stored")

        with nc.Block() as block:
            @block.sync
            def _(sp):
                sp.dma_start(raw[:, 0:3 * D], WqkvT).then_inc(w_in, 16)
                sp.dma_start(raw[:, 3 * D:], WgateT).then_inc(w_in, 16)
                sp.dma_start(wout[:, :], WoutT).then_inc(w_in, 16)
                sp.dma_start(bq[:, :], bqkv[0:D].rearrange("(p a) -> p a", a=1)).then_inc(w_in, 16)
                sp.dma_start(bk[:, :], bqkv[D:2 * D].rearrange("(p a) -> p a", a=1)).then_inc(w_in, 16)
                sp.dma_start(bvg_b[:, 0:D], bqkv[2 * D:].rearrange("(a d) -> a d", a=1).broadcast_to([P, D])).then_inc(w_in, 16)
                sp.dma_start(bvg_b[:, D:], bgate.rearrange("(a d) -> a d", a=1).broadcast_to([P, D])).then_inc(w_in, 16)
                sp.dma_start(bout_b[:, :], bout.rearrange("(a d) -> a d", a=1).broadcast_to([P, D])).then_inc(w_in, 16)
                sp.dma_start(pos[:, :], pos_bias).then_inc(w_in, 16)
                sp.dma_start(off_i[:, :], offsets.rearrange("(p a) -> p a", a=1)).then_inc(w_in, 16)
                sp.dma_start(dist, c_dist).then_inc(w_in, 16)
                sp.dma_start(ident[:, :], c_ident).then_inc(w_in, 16)
                sp.dma_start(ones_rows[:, :], c_ones_rows).then_inc(w_in, 16)
                sp.dma_start(turned, c_turned).then_inc(w_in, 16)
                sp.wait_ge(table_step, 4)
                sp.dma_start(table, bias_row).then_inc(table_out, 16)
                sp.wait_ge(table_out, 16)
                heads = 3 * GH
                for dst, n, h, nh in ((bias_qk[:, :, :], 0, 0, H1),
                                      (prob[:, :].rearrange("p (h n) -> p h n", h=heads), 1, 0, heads),
                                      (junk, 1, heads, H1 - heads)):
                    src = bass.AP(table.tensor, (2 * h + n) * TAB + 1, [[1, P], [2 * TAB, nh], [1, WIN]])
                    sp.dma_start(dst, src).then_inc(table_in, 16)

            @block.gpsimd
            def _(pool):
                nc.gpsimd.memset(minus_half[:, :], -0.5)
                nc.gpsimd.memset(ones[:, :], 1.0).then_inc(w_ready, 1)
                nc.gpsimd.memset(vp[:, :, :, :], 0.0).then_inc(w_ready, 1)
                pool.wait_ge(w_ready, 2)
                nc.gpsimd.memset(vp[:, :, :, HD:HD + 1], 1.0)
                nc.gpsimd.memset(negtop[:, :, :], 0.0)

            @block.vector
            def _(dve):
                nc.vector.memset(kz[:, :, :, :].bitcast(F32), 0.0).then_inc(hit_ready, 1)
                dve.wait_ge(w_in, 14 * 16)
                nc.vector.tensor_copy(off_f[:, :], off_i[:, :]).then_inc(hit_ready, 1)
                dve.wait_ge(hit_ready, 2)
                nc.vector.tensor_scalar(hit, dist, off_f[:, 0:1], None, ALU.is_equal).then_inc(hit_ready, 1)
                for i in range(GH):
                    nc.vector.tensor_scalar(kz[:, :, i, :], f32(kz[:, :, i, :]), ones_rows[:, i:i + 1], None, ALU.add)
                split(nc, dve, wqk_hi[:, :], wqk_lo[:, :], raw[:, 0:2 * D], hit_ready, 3)
                split(nc, dve, wvg_hi[:, :], wvg_lo[:, :], raw[:, 2 * D:], hit_ready, 5)
                nc.vector.tensor_scalar(bq[:, :], bq[:, :], float(HD) ** -0.5, None, ALU.mult)
                nc.vector.tensor_copy(ident_r[:, :], ident[:, :])
                for n in range(2):
                    dve.wait_ge(table_mm, n + 1)
                    nc.vector.tensor_scalar(missing[:, n, :], ps[0:H1, 2 + n, 0:TAB], -1.0, FAR, ALU.add,
                                            ALU.mult).then_inc(table_step, 1)
                    dve.wait_ge(table_step, 2 * n + 1)
                    nc.vector.tensor_tensor(bias_row[:, n, :], ps[0:H1, n, 0:TAB], missing[:, n, :],
                                            ALU.add).then_inc(table_step, 1)
                for n in range(2 * H1):
                    dve.wait_ge(flip_mm, n + 1)
                    h, rows_ = n % H1, ps[:, 4 + n % 4, 0:WIN]
                    if n >= H1:
                        nc.vector.tensor_copy(bias_qk[:, h, :], rows_).then_inc(flip_copied, 2)
                    elif h in vector_heads:
                        nc.vector.tensor_copy(bias_kq[:, vector_heads.index(h), :], rows_).then_inc(flip_copied, 2)
                    else:
                        m = tensor_heads.index(h)
                        split(nc, dve, bias_kq_hi[:, m, :], bias_kq_lo[:, m, :], rows_, flip_copied, 2 * n)

            @block.tensor
            def _(pe):
                pe.wait_ge(w_ready, 1)
                pe.wait_ge(hit_ready, 3)
                for n in range(2):
                    cols = slice(n * TAB, (n + 1) * TAB)
                    pe.matmul(ps[0:H1, n, 0:TAB], pos[:, :], hit[:, cols], start=True, stop=True)
                    pe.matmul(ps[0:H1, 2 + n, 0:TAB], ones[:, :], hit[:, cols], start=True, stop=True).then_inc(table_mm, 1)
                pe.wait_ge(table_in, 3 * 16)
                for n in range(2 * H1):
                    h = n % H1
                    if n < H1:
                        src = bias_qk[:, h, :]
                    elif h < 3 * GH:
                        src = prob[:, h * WIN:(h + 1) * WIN]
                    else:
                        src = junk[:, h - 3 * GH, :]
                    if n >= 4:
                        pe.wait_ge(flip_copied, 2 * (n - 3))
                    pe.matmul(ps[:, 4 + n % 4, 0:WIN], turned, src, start=True, stop=True).then_inc(flip_mm, 1)
        clear(nc, sems)

        QP = (0, 0, 1)
        KP = (0, 1, 0)

        TOPS, PROBS = 0, 1
        steps = []
        for r in range(NG + 1):
            for u in range(NT + 1):
                if r < NG and u < NT:
                    steps.append((TOPS, r, u))
                if r >= 1 and u >= 1:
                    steps.append((PROBS, r - 1, u - 1))
        place = {step: m for m, step in enumerate(steps)}

        def scores_done(kind, g, t, i):
            return GH * place[kind, g, t] + i + 1

        def added_before(g, t):
            return NT * sum(BY_VECTOR[:g]) + BY_VECTOR[g] * t

        def keys_of(t):
            lo = max(0, P * t - REACH)
            return lo, lo - (P * t - REACH)

        def queries_of(j):
            return min(WIN, N - P * j)

        TR = 6

        def head_norm(dve, s, stored_before):
            dve.wait_ge(x_loaded, 16)
            norm_in.statistics(x[s])
            norm_in.moments(dve)
            if stored_before:
                dve.wait_ge(stored, 16)
            norm_in.apply(dve, xn, x[s], xn_ready)

        def head_pe(pe):
            for t in range(NT):
                pe.wait_ge(xn_ready, t + 1)
                pe.transpose(ps[:, TR + t // 4, (t % 4) * P:(t % 4 + 1) * P], xn[:, t, :],
                             ident[:, :]).then_inc(xt_mm, 1)

        def head_act(act):
            for c in range(NC):
                act.wait_ge(xt_mm, 4 * (c + 1))
                nc.scalar.copy(xt_hi[:, c * CH:(c + 1) * CH], ps[:, TR + c, :]).then_inc(xt_hi_ready, 1)

        def head_lower(dve):
            for c in range(NC):
                dve.wait_ge(xt_hi_ready, c + 1)
                nc.vector.tensor_tensor(xt_lo[:, c * CH:(c + 1) * CH], ps[:, TR + c, :],
                                        f32(xt_hi[:, c * CH:(c + 1) * CH]), ALU.subtract).then_inc(xt_ready, 1)

        def back(pe, done):
            for t in range(NT):
                pe.transpose(ps[:, TR + t // 4, (t % 4) * P:(t % 4 + 1) * P], ot[:, t * P:(t + 1) * P],
                             ident[:, :]).then_inc(done, 1)

        def divide(dve, g, before, turned_back, inverse, divided):
            for c in range(NC):
                dve.wait_ge(turned_back, NT * before + 4 * (c + 1))
                if before + c >= 1:
                    dve.wait_ge(divided, NC * before + c)
                bank = ps[:, TR + c, :].rearrange("p (t i e) -> p t i e", t=4, i=GH)
                nc.vector.reciprocal(rden[:, :, :, :], bank[:, :, :, HD:HD + 1]).then_inc(inverse, 1)
                dve.wait_ge(inverse, NC * before + c + 1)
                nc.vector.tensor_tensor(
                    flat[:, 4 * c:4 * c + 4, 32 * g:32 * g + 32].rearrange("p t (i e) -> p t i e", i=GH),
                    bank[:, :, :, 0:HD], rden[:, :, :, :].broadcast_to([P, 4, GH, HD]),
                    ALU.mult).then_inc(divided, 1)

        def tail_gate(dve, s):
            divide(dve, NG - 1, 0, last_back_mm, last_rden_ready, last_flat_ready)
            dve.wait_ge(last_flat_ready, NC)
            nc.vector.tensor_tensor(flat[:, :, :], flat[:, :, :], gate[s][:, :, :], ALU.mult).then_inc(gated, 1)

        def tail_flat_t(pe):
            pe.wait_ge(gated, 1)
            for t in range(NT):
                pe.transpose(ps[:, TR + t // 4, (t % 4) * P:(t % 4 + 1) * P], flat[:, t, :],
                             ident[:, :]).then_inc(flat_t_mm, 1)

        def tail_act(act):
            for c in range(NC):
                act.wait_ge(flat_t_mm, 4 * (c + 1))
                nc.scalar.copy(flat_t[:, c * CH:(c + 1) * CH], ps[:, TR + c, :]).then_inc(flat_t_ready, 1)

        def tail_out(pe):
            for t in range(NT):
                if t % 4 == 0:
                    pe.wait_ge(flat_t_ready, t // 4 + 1)
                pe.matmul(ps[:, TR + t // 4, (t % 4) * D:(t % 4 + 1) * D], flat_t[:, t * P:(t + 1) * P],
                          wout[:, :], start=True, stop=True).then_inc(out_mm, 1)

        def tail_z(dve):
            for c in range(NC):
                dve.wait_ge(out_mm, 4 * (c + 1))
                nc.vector.tensor_tensor(z[:, 4 * c:4 * c + 4, :],
                                        ps[:, TR + c, :].rearrange("p (t d) -> p t d", t=4),
                                        bout_b[:, None, :].broadcast_to([P, 4, D]), ALU.add).then_inc(z_ready, 1)

        def tail_norm(dve, s):
            dve.wait_ge(z_ready, NC)
            norm_out.statistics(z)
            norm_out.moments(dve)

        def tail_residual(dve, s):
            norm_out.apply(dve, z, z, z_normed)
            dve.wait_ge(z_normed, NT)
            nc.vector.tensor_tensor(z[:, :, :], x[s][:, :, :], z[:, :, :], ALU.add).then_inc(y_ready, 1)

        def tail_store(sp, k):
            sp.wait_ge(y_ready, 1)
            sp.dma_start(rows(x_out, k), z[:, :, :]).then_inc(stored, 16)

        def head():
            with nc.Block() as block:
                @block.sync
                def _(sp):
                    sp.dma_start(x[0][:, :, :], rows(x_in, 0)).then_inc(x_loaded, 16)

                @block.gpsimd
                def _(pool):
                    norm_in.root(pool, minus_half[:, :])

                @block.scalar
                def _(act):
                    head_act(act)

                @block.vector
                def _(dve):
                    head_norm(dve, 0, False)
                    head_lower(dve)

                @block.tensor
                def _(pe):
                    head_pe(pe)

        def tail():
            with nc.Block() as block:
                @block.sync
                def _(sp):
                    tail_store(sp, B - 1)
                    sp.wait_ge(stored, 16)

                @block.gpsimd
                def _(pool):
                    norm_out.root(pool, minus_half[:, :])

                @block.scalar
                def _(act):
                    tail_act(act)

                @block.vector
                def _(dve):
                    tail_gate(dve, 1)
                    tail_z(dve)
                    tail_norm(dve, 1)
                    tail_residual(dve, 1)

                @block.tensor
                def _(pe):
                    back(pe, last_back_mm)
                    tail_flat_t(pe)
                    tail_out(pe)

        def turn(k, s, has_head=True, has_tail=True):
            with nc.Block() as block:
                @block.sync
                def _(sp):
                    sp.wait_ge(qk_ready, 8)
                    sp.dma_start(parts[0].rearrange("a p n -> p a n"), f32(qk_hi[:, :, :])).then_inc(parts_out, 16)
                    sp.dma_start(parts[1].rearrange("a p n -> p a n"), f32(qk_lo[:, :, :])).then_inc(parts_out, 16)
                    sp.wait_ge(parts_out, 32)
                    for r in range(3):
                        sp.dma_start(f32(qcat[32 * r:32 * r + 32, :, :]),
                                     parts[QP[r], 0].rearrange("(g r) n -> r g n", g=NG)).then_inc(q_in, 16)
                    for g in range(NG):
                        if g == 3:
                            sp.wait_ge(s_mm, scores_done(PROBS, 0, NT - 1, GH - 1))
                        for r in range(3):
                            for i in range(GH):
                                row = 32 * g + HD * i
                                sp.dma_start(f32(kz[32 * r + HD * i:32 * r + HD * (i + 1), g % 3, i, :]),
                                             parts[KP[r], 1, row:row + HD, :]).then_inc(k_in[g % 3], 16)
                    if has_tail:
                        tail_store(sp, k - 1)
                    if has_head:
                        sp.dma_start(x[1 - s][:, :, :], rows(x_in, k + 1)).then_inc(x_loaded, 16)
                    if has_tail:
                        sp.wait_ge(stored, 16)

                @block.gpsimd
                def _(pool):
                    nc.gpsimd.memset(f32(qcat[96:128, :, :]), 0.0).then_inc(rows_zero, 1)
                    pool.wait_ge(rows_zero, 1)
                    if has_tail:
                        norm_out.root(pool, minus_half[:, :])
                    if has_head:
                        norm_in.root(pool, minus_half[:, :])

                @block.scalar
                def _(act):
                    for a, (scale, bias) in enumerate(((float(HD) ** -0.5, bq), (1.0, bk))):
                        for c in range(NC):
                            act.wait_ge(qk_mm, 2 * a + c + 1)
                            nc.scalar.activation(qk[:, a, c * CH:(c + 1) * CH], ps[:, 2 * a + c, :], ACT.Identity,
                                                 bias=bias[:, 0:1], scale=scale).then_inc(qk_biased, 1)
                    if has_tail:
                        tail_act(act)
                    act.wait_ge(v_ready, 2 * NT)
                    nc.scalar.activation(gate[s][:, :, :], gate[s][:, :, :], ACT.Sigmoid).then_inc(gate_ready, 1)
                    for g in range(NG):
                        for j in range(NT):
                            n = g * NT + j
                            cols = queries_of(j)
                            if n >= 3:
                                act.wait_ge(pv_mm, n - 2)
                            for i in range(GH):
                                if i < BY_VECTOR[g]:
                                    act.wait_ge(bias_added, added_before(g, j) + i + 1)
                                    src = prob_of[:, n % 3, i, 0:cols]
                                else:
                                    act.wait_ge(s_mm, scores_done(PROBS, g, j, i))
                                    src = ps[:, i, 0:cols]
                                nc.scalar.activation(prob_of[:, n % 3, i, 0:cols], src, ACT.Exp).then_inc(prob_ready, 1)
                            if g == NG - 1 and j == NT - 2 and has_head:
                                head_act(act)
                        for c in range(NC):
                            act.wait_ge(pv_mm, NT * (g + 1))
                            if g >= 1 and c == 0:
                                act.wait_ge(back_mm, NT * g)
                            nc.scalar.copy(ot[:, c * CH:(c + 1) * CH], ps[:, 4 + c, :]).then_inc(ot_copied, 1)

                @block.vector
                def _(dve):
                    for n in range(2 * NC):
                        a, cols = n // NC, slice((n % NC) * CH, (n % NC + 1) * CH)
                        dve.wait_ge(qk_biased, n + 1)
                        split(nc, dve, qk_hi[:, a, cols], qk_lo[:, a, cols], qk[:, a, cols], qk_ready, 2 * n)
                    if has_tail:
                        tail_gate(dve, 1 - s)
                    for t in range(NT):
                        dve.wait_ge(vg_mm, t + 1)
                        bank = ps[:, 4 + t % 2, :]
                        nc.vector.tensor_tensor(vp[:, t, :, 0:HD], bank[:, 0:D].rearrange("p (h d) -> p h d", h=H1),
                                                bvg_b[:, 0:D].rearrange("p (h d) -> p h d", h=H1),
                                                ALU.add).then_inc(v_ready, 1)
                        nc.vector.tensor_tensor(gate[s][:, t, :], bank[:, D:2 * D], bvg_b[:, D:], ALU.add).then_inc(v_ready, 1)
                    if has_tail:
                        tail_z(dve)

                    def tops(g, t):
                        lo, skip = keys_of(t)
                        cols = P * (t + 1) - lo
                        for i in range(GH):
                            used = GH * (NT * g + t) + i
                            dve.wait_ge(s_mm, scores_done(TOPS, g, t, i))
                            if used >= 4:
                                dve.wait_ge(top_taken, used - 3)
                            nc.vector.tensor_tensor_reduce(
                                out=junk[:, i, 0:cols], in0=ps[:, i, 0:cols], in1=bias_qk[:, GH * g + i, skip:WIN],
                                scale=1.0, scalar=-FAR, op0=ALU.add, op1=ALU.max,
                                accum_out=top[:, g % 2, t, i:i + 1]).then_inc(top_taken, 1)

                    def minus_tops(g):
                        pair = negtop[:, :, 96:96 + 2 * GH].rearrange("p t (i a) -> p t i a", a=2)
                        dve.wait_ge(top_taken, NT * GH * (g + 1))
                        if g >= 1:
                            dve.wait_ge(top_mm, NT * g)
                        nc.vector.tensor_scalar(pair[:, :, :, 0].bitcast(F32R), top[:, g % 2, :, :], -1.0, None,
                                                ALU.mult).then_inc(top_step, 1)
                        dve.wait_ge(top_step, 2 * g + 1)
                        nc.vector.scalar_tensor_tensor(out=pair[:, :, :, 1].bitcast(F32R), in0=top[:, g % 2, :, :],
                                                       scalar=-1.0, in1=pair[:, :, :, 0], op0=ALU.mult,
                                                       op1=ALU.subtract).then_inc(top_step, 1)

                    def place_tops(g):
                        for c in range(NC):
                            dve.wait_ge(top_mm, NT * g + 4 * (c + 1))
                            nc.vector.tensor_copy(qcat[96:128, g, c * CH:(c + 1) * CH],
                                                  ps[96:128, TR + c, :]).then_inc(top_ready, 1)

                    def biases(g, j):
                        n, cols = g * NT + j, queries_of(j)
                        if n >= 3:
                            dve.wait_ge(pv_mm, n - 2)
                        for i in range(BY_VECTOR[g]):
                            dve.wait_ge(s_mm, scores_done(PROBS, g, j, i))
                            nc.vector.tensor_tensor(prob_of[:, n % 3, i, 0:cols], ps[:, i, 0:cols],
                                                    bias_kq[:, vector_heads.index(GH * g + i), 0:cols],
                                                    ALU.add).then_inc(bias_added, 1)

                    for r in range(NG + 1):
                        for u in range(NT + 1):
                            if r >= 1 and u == 0:
                                minus_tops(r - 1)
                            if r < NG and u < NT:
                                tops(r, u)
                            if r >= 1 and u == 0:
                                place_tops(r - 1)
                            if r >= 1 and u >= 1:
                                biases(r - 1, u - 1)
                            if r >= 2 and u == 4:
                                divide(dve, r - 2, r - 2, back_mm, rden_ready, flat_ready)
                            if has_tail:
                                if (r, u) == (3, 1):
                                    tail_norm(dve, 1 - s)
                                if (r, u) == (3, 6):
                                    tail_residual(dve, 1 - s)
                            if has_head:
                                if (r, u) == (4, 3):
                                    head_norm(dve, 1 - s, has_tail)
                                if (r, u) == (4, 8):
                                    head_lower(dve)

                @block.tensor
                def _(pe):
                    def three(out, lhs, rhs):
                        pe.matmul(out, lhs[0], rhs[0], start=True, stop=False)
                        pe.matmul(out, lhs[0], rhs[1], start=False, stop=False)
                        return pe.matmul(out, lhs[1], rhs[0], start=False, stop=True)

                    for a in range(2):
                        for c in range(NC):
                            cols = slice(c * CH, (c + 1) * CH)
                            three(ps[:, 2 * a + c, :], (wqk_hi[:, a * D:(a + 1) * D], wqk_lo[:, a * D:(a + 1) * D]),
                                  (xt_hi[:, cols], xt_lo[:, cols])).then_inc(qk_mm, 1)
                    if has_tail:
                        back(pe, last_back_mm)
                    for t in range(NT):
                        toks = slice(t * P, (t + 1) * P)
                        if t >= 2:
                            pe.wait_ge(v_ready, 2 * (t - 1))
                        three(ps[:, 4 + t % 2, 0:2 * D], (xt_hi[:, toks], xt_lo[:, toks]),
                              (wvg_hi[:, :], wvg_lo[:, :])).then_inc(vg_mm, 1)
                        if t == 3 and has_tail:
                            tail_flat_t(pe)
                    if has_tail:
                        tail_out(pe)
                    pe.wait_ge(qk_biased, 2 * NC)
                    pe.wait_ge(v_ready, 2 * NT)
                    pe.wait_ge(q_in, 3 * 16)
                    pe.wait_ge(rows_zero, 1)

                    def bank_free(m, i):
                        kind, g, t = steps[m - 1]
                        if kind == TOPS:
                            pe.wait_ge(top_taken, GH * (NT * g + t) + i + 1)
                        elif i < BY_VECTOR[g]:
                            pe.wait_ge(bias_added, added_before(g, t) + i + 1)
                        else:
                            pe.wait_ge(prob_ready, GH * (NT * g + t) + i + 1)

                    def scores_for_tops(g, t):
                        lo, _ = keys_of(t)
                        for i in range(GH):
                            if place[TOPS, g, t] >= 1:
                                bank_free(place[TOPS, g, t], i)
                            pe.matmul(ps[:, i, 0:P * (t + 1) - lo], qcat[:, g, t * P:(t + 1) * P],
                                      kz[:, g % 3, i, lo:P * (t + 1)], start=True, stop=True).then_inc(s_mm, 1)

                    def scores_for_probs(g, j):
                        cols = queries_of(j)
                        for i in range(GH):
                            bank_free(place[PROBS, g, j], i)
                            out = ps[:, i, 0:cols]
                            by_vector = i < BY_VECTOR[g]
                            mm = pe.matmul(out, kz[:, g % 3, i, j * P:(j + 1) * P], qcat[:, g, j * P:j * P + cols],
                                           start=True, stop=by_vector)
                            if not by_vector:
                                m = tensor_heads.index(GH * g + i)
                                pe.matmul(out, ident_r[:, :], bias_kq_hi[:, m, 0:cols], start=False, stop=False)
                                mm = pe.matmul(out, ident_r[:, :], bias_kq_lo[:, m, 0:cols], start=False, stop=True)
                            mm.then_inc(s_mm, 1)

                    def weighted(g, j):
                        n = g * NT + j
                        pe.wait_ge(prob_ready, GH * (n + 1))
                        if g >= 1 and j == 0:
                            pe.wait_ge(ot_copied, NC * g)
                        first, last = P * j, min(N, P * j + WIN)
                        for c in range(NC):
                            a, z_ = max(first, c * CH), min(last, (c + 1) * CH)
                            if a >= z_:
                                continue
                            opens = j == (0 if c == 0 else (CH - WIN) // P + 1)
                            for i in range(GH):
                                mm = pe.matmul(ps[32 * i:32 * i + 32, 4 + c, a - c * CH:z_ - c * CH],
                                               vp[:, j, GH * g + i, :], prob_of[:, n % 3, i, a - first:z_ - first],
                                               start=opens, stop=(j == NT - 1), skip_group_check=True)
                        mm.then_inc(pv_mm, 1)

                    for r in range(NG + 1):
                        if r < NG:
                            pe.wait_ge(k_in[r % 3], 12 * 16 * (r // 3 + 1))
                        for u in range(NT + 1):
                            if r < NG and u < NT:
                                scores_for_tops(r, u)
                            if r >= 2 and u == 0:
                                weighted(r - 2, NT - 1)
                            if r >= 1 and u == 0:
                                pe.wait_ge(top_step, 2 * r)
                                if r >= 3:
                                    pe.wait_ge(flat_ready, NC * (r - 2))
                                elif r == 1 and has_tail:
                                    pe.wait_ge(z_ready, NC)
                                for t in range(NT):
                                    pe.transpose(ps[:, TR + t // 4, (t % 4) * P:(t % 4 + 1) * P], negtop[:, t, :],
                                                 ident[:, :]).then_inc(top_mm, 1)
                            if r >= 1 and u == 1:
                                pe.wait_ge(top_ready, NC * r)
                            if r >= 1 and u >= 1:
                                scores_for_probs(r - 1, u - 1)
                            if r >= 1 and u >= 2:
                                weighted(r - 1, u - 2)
                            if r >= 2 and u == 3:
                                pe.wait_ge(ot_copied, NC * (r - 1))
                                back(pe, back_mm)
                            if r == NG and u == 7 and has_head:
                                pe.wait_ge(flat_ready, NC * (NG - 1))
                                head_pe(pe)
                    weighted(NG - 1, NT - 1)

        turns(nc, sems, turn, head, tail)


def build(nc, a, out):
    mid = [nc.dram_tensor(f"x_after_{i}", (B, N, D), F32).ap() for i in range(3)]
    table = nc.dram_tensor("bias_by_distance", (H1, 2, TAB), F32).ap()
    parts = nc.dram_tensor("q_k_parts", (2, 2, P, N), F32).ap()
    linear_attention(nc, a["x"], mid[0], a["L0_WQ"], a["L0_WK"], a["L0_WVT"], a["L0_Wfc"], a["gamma"], a["beta"],
                     a["ident"], a["headcol"], a["headsel"])
    for layer, x_in, x_out in ((0, mid[0], mid[1]), (1, mid[2], out)):
        if layer == 1:
            window_attention(nc, mid[1], mid[2], a["WqkvT"], a["bqkv"], a["WgateT"], a["bgate"], a["WoutT"], a["bout"],
                             a["pos_bias"], a["offsets"], a["ident"], a["dist"], a["ones_rows"], a["turned"], table, parts)
        w = {k: a[f"L{layer}_{k}"] for k in ("w1t", "w1s", "w2t", "w2s", "h1t", "h1s", "h2t", "h2s", "w3t", "w3s")}
        feed_forward(nc, f"ff{layer}_", x_in, x_out, c_ident=a["ident"], **w)


def constants():
    part, col = np.arange(P)[:, None], np.arange(P)[None, :]
    headcol = np.zeros((P, NF, 32), np.float32)
    headsel = np.zeros((P, NF, P), np.float32)
    for f in range(NF):
        headcol[:, f, :] = np.arange(32)[None, :] == 2 * f + part // DK
        headsel[:, f, :] = part % 32 == 2 * f + col // DK
    e = np.arange(TAB, dtype=np.float32) - P
    dist = np.concatenate([e, REACH - e])[None, :].repeat(NOFF, 0)
    ones_rows = (part // 2 == 48 + np.arange(GH)[None, :]).astype(np.float32)
    return {"ident": np.eye(P, dtype=np.float32), "turned": np.eye(P, dtype=np.float32)[::-1].copy(),
            "headcol": headcol.reshape(P, -1), "headsel": headsel.reshape(P, -1),
            "dist": np.ascontiguousarray(dist), "ones_rows": ones_rows}


def kernel(**inputs):
    import concourse.bacc as bacc
    from concourse.bass_utils import run_bass_kernel_spmd as run

    def take(name):
        return np.ascontiguousarray(inputs[name])

    def flip(name):
        return np.ascontiguousarray(np.asarray(inputs[name]).T)

    arrays = {"x": take("L0_attn_inputs"), "L0_WQ": take("L0_attn_W_Q"), "L0_WK": take("L0_attn_W_K"),
              "L0_WVT": flip("L0_attn_W_V"), "L0_Wfc": take("L0_attn_W_fc"), "gamma": take("L0_attn_gamma"),
              "beta": take("L0_attn_beta"), "WqkvT": flip("L1_attn_Wqkv"), "bqkv": take("L1_attn_bqkv"),
              "WgateT": flip("L1_attn_Wgate"), "bgate": take("L1_attn_bgate"), "WoutT": flip("L1_attn_Wout"),
              "bout": take("L1_attn_bout"), "pos_bias": take("L1_attn_pos_bias"), "offsets": take("L1_attn_offsets")}
    for layer in (0, 1):
        for w in ("w1", "w2", "h1", "h2", "w3"):
            arrays[f"L{layer}_{w}t"] = flip(f"L{layer}_ffn_{w}_w")
            scale = take(f"L{layer}_ffn_{w}_s")
            arrays[f"L{layer}_{w}s"] = scale if w == "w3" else np.ascontiguousarray(scale.reshape(NB, P).T)
    arrays.update(constants())

    nc = bacc.Bacc("TRN2", target_bir_lowering=False, num_devices=1)
    aps = {k: nc.dram_tensor(f"in_{k}", v.shape, mybir.dt.from_np(v.dtype), kind="ExternalInput").ap()
           for k, v in arrays.items()}
    out = nc.dram_tensor("out_x", (B, N, D), F32, kind="ExternalOutput").ap()
    build(nc, aps, out)
    r = run(nc, [{f"in_{k}": v for k, v in arrays.items()}], core_ids=[0])
    return r.results[0]["out_x"]
```

```python
import numpy as np
from contextlib import ExitStack

import concourse.bass as bass
from concourse import mybir

F32 = mybir.dt.float32
F32R = mybir.dt.float32r
I32 = mybir.dt.int32
ALU = mybir.AluOpType
ACT = mybir.ActivationFunctionType
AX = mybir.AxisListType

P = 128
B, N, D = 8, 1024, 128
NT = N // P
CH = 512
NC = N // CH
H0, DK = 16, 64
NF = H0 * DK // P
HID = 512
NB = HID // P
H1, HD = 16, 8
NG, GH = 4, 4
NOFF = 68
REACH = 192
WIN = P + REACH
TAB = P + WIN
EPS = 1e-5
DEN_EPS = 1e-8
FAR = 1e30


def f32(ap):
    return ap.bitcast(F32)


class Norm:

    def __init__(self, nc, buffers, sem, tag):
        self.nc = nc
        self.stats, self.mean_var, self.var_eps, self.rstd = buffers
        self.stats_done = sem(f"{tag}_stats_done")
        self.moments_done = sem(f"{tag}_moments_done")
        self.eps_added = sem(f"{tag}_eps_added")
        self.rstd_ready = sem(f"{tag}_rstd_ready")

    def statistics(self, src, tiles=range(NT)):
        for t in tiles:
            self.nc.vector.bn_stats(self.stats[:, t, :], src[:, t, 0:D]).then_inc(self.stats_done, 1)

    def moments(self, dve):
        dve.wait_ge(self.stats_done, NT)
        for t in range(NT):
            self.nc.vector.bn_aggr(self.mean_var[:, t, :], self.stats[:, t, :]).then_inc(self.moments_done, 1)

    def root(self, pool, minus_half):
        pool.wait_ge(self.moments_done, NT)
        self.nc.gpsimd.tensor_scalar(self.var_eps[:, :], self.mean_var[:, :, 1], EPS, None,
                                     ALU.add).then_inc(self.eps_added, 1)
        pool.wait_ge(self.eps_added, 1)
        self.nc.gpsimd.tensor_tensor(self.rstd[:, :], self.var_eps[:, :], minus_half,
                                     ALU.pow).then_inc(self.rstd_ready, 1)

    def apply(self, dve, out, src, done, tiles=range(NT)):
        dve.wait_ge(self.moments_done, NT)
        dve.wait_ge(self.rstd_ready, 1)
        for t in tiles:
            self.nc.vector.tensor_scalar(out[:, t, 0:D], src[:, t, 0:D], self.mean_var[:, t, 0:1],
                                         self.rstd[:, t:t + 1], ALU.subtract, ALU.mult).then_inc(done, 1)


def norm_buffers(sb, tag):
    return (sb(f"{tag}_stats", [P, NT, 6]), sb(f"{tag}_mean_var", [P, NT, 2]), sb(f"{tag}_var_eps", [P, NT]),
            sb(f"{tag}_rstd", [P, NT]))


def clear(sp, semaphores):
    for s in semaphores:
        sp.sem_clear(s)


def turns(nc, ctx, tag, program):
    used = ([], [])

    def taker(n):
        def sem(name):
            s = ctx.enter_context(nc.semaphore(f"{tag}{name}_{n}"))
            used[n].append(s)
            return s
        return sem

    set_up, turn_0, _ = program(taker(0), used[1])
    _, turn_1, tail = program(taker(1), used[0])
    set_up()
    turn_1(0, 0, has_tail=False)
    with nc.Fori(0, B // 2 - 1) as i:
        turn_0(i * 2 + 1, 1)
        turn_1(i * 2 + 2, 0)
    turn_0(B - 1, 1, has_head=False)
    tail()
    with nc.Block() as block:
        @block.sync
        def _(sp):
            clear(sp, used[0] + used[1])


def rows(ap, k):
    return ap[k].rearrange("(t p) d -> p t d", p=P)


def split(nc, eng, hi, lo, x, done, base):
    nc.vector.tensor_copy(hi, x).then_inc(done, 1)
    eng.wait_ge(done, base + 1)
    nc.vector.tensor_tensor(lo, x, f32(hi), ALU.subtract).then_inc(done, 1)


def linear_attention(nc, x_in, x_out, W_Q, W_K, W_VT, W_fc, gamma, beta, c_ident, c_headcol, c_headsel):
    with ExitStack() as ctx:
        def sb(name, shape, dt=F32):
            return ctx.enter_context(nc.sbuf_tensor("la_" + name, shape, dt))

        ps = ctx.enter_context(nc.psum_tensor("la_ps", [P, 8, CH], F32))

        ident = sb("ident", [P, P])
        wq_hi, wq_lo = sb("wq_hi", [P, H0 * DK], F32R), sb("wq_lo", [P, H0 * DK], F32R)
        wk_hi, wk_lo = sb("wk_hi", [P, H0 * DK], F32R), sb("wk_lo", [P, H0 * DK], F32R)
        wvt, wfc = sb("wvt", [P, NF, D]), sb("wfc", [P, NF, D])
        wvfc = sb("wvfc", [P, H0, D])
        headcol = sb("headcol", [P, NF, 32])
        headsel = sb("headsel", [P, NF, P], F32R)
        gamma_b, beta_b = sb("gamma_b", [P, D]), sb("beta_b", [P, D])
        minus_half = sb("minus_half", [P, NT])

        x = [sb(f"x{i}", [P, NT, D]) for i in range(2)]
        fresh = sb("fresh", [P, NT, D])
        xn = [sb(f"xn{i}", [P, NT, D + 1]) for i in range(2)]
        xt_hi = [sb(f"xt_hi{i}", [P, N], F32R) for i in range(2)]
        xt_lo = [sb(f"xt_lo{i}", [P, N], F32R) for i in range(2)]
        z = [sb(f"z{i}", [P, NT, D]) for i in range(2)]
        kn = sb("kn", [P, 2, H0 * DK])
        kx = sb("kx", [P, NF, D + 1])
        ksum_col = sb("ksum_col", [P, NF, 32])
        kxt = sb("kxt", [P, NF, P])
        m = sb("m", [P, NF, D])
        q = sb("q", [P, NF, N])
        den = [sb(f"den{c}", [P, P]) for c in range(NC)]
        rden = [sb(f"rden{c}", [P, P]) for c in range(NC)]
        rden_hi, rden_lo = sb("rden_hi", [P, NC, 4, P], F32R), sb("rden_lo", [P, NC, 4, P], F32R)
        norm_in_bufs = norm_buffers(sb, "norm_in")
        norm_sum_bufs = norm_buffers(sb, "norm_sum")
        norm_out_bufs = norm_buffers(sb, "norm_out")

        def program(sem, others):
            norm_in = Norm(nc, norm_in_bufs, sem, "norm_in")
            norm_sum = Norm(nc, norm_sum_bufs, sem, "norm_sum")
            norm_out = Norm(nc, norm_out_bufs, sem, "norm_out")

            w_in = sem("w_in")
            w_ready = sem("w_ready")
            wvfc_mm = sem("wvfc_mm")
            x_loaded = sem("x_loaded")
            constants_ready = sem("constants_ready")
            xn_ready = sem("xn_ready")
            xt_mm = sem("xt_mm")
            xt_hi_ready = sem("xt_hi_ready")
            xt_ready = sem("xt_ready")
            k_mm = sem("k_mm")
            k_ready = sem("k_ready")
            kx_mm = sem("kx_mm")
            kx_copied = sem("kx_copied")
            ksum_ready = sem("ksum_ready")
            kxt_mm = sem("kxt_mm")
            kxt_ready = sem("kxt_ready")
            m_mm = sem("m_mm")
            m_ready = sem("m_ready")
            q_mm = sem("q_mm")
            q_ready = sem("q_ready")
            den_mm = sem("den_mm")
            den_step = sem("den_step")
            rden_ready = sem("rden_ready")
            spread_mm = sem("spread_mm")
            qd_ready = sem("qd_ready")
            out_mm = sem("out_mm")
            z_normed = sem("z_normed")
            affine = sem("affine")
            y_ready = sem("y_ready")
            stored = sem("stored")


            def head_dve(dve, s):
                dve.wait_ge(x_loaded, 16)
                norm_in.statistics(fresh)
                norm_in.moments(dve)
                norm_in.apply(dve, xn[s], fresh, xn_ready)

            def head_pe(pe, s, bank):
                for t in range(NT):
                    pe.wait_ge(xn_ready, t + 1)
                    pe.transpose(ps[:, bank + t // 4, (t % 4) * P:(t % 4 + 1) * P], xn[s][:, t, 0:D],
                                 ident[:, :]).then_inc(xt_mm, 1)

            def head_act(act, s, bank):
                for c in range(NC):
                    act.wait_ge(xt_mm, 4 * (c + 1))
                    nc.scalar.copy(xt_hi[s][:, c * CH:(c + 1) * CH], ps[:, bank + c, :]).then_inc(xt_hi_ready, 1)

            def head_lower(dve, s, bank):
                for c in range(NC):
                    dve.wait_ge(xt_hi_ready, c + 1)
                    nc.vector.tensor_tensor(xt_lo[s][:, c * CH:(c + 1) * CH], ps[:, bank + c, :],
                                            f32(xt_hi[s][:, c * CH:(c + 1) * CH]), ALU.subtract).then_inc(xt_ready, 1)

            def tail_dve(dve, s):
                norm_sum.statistics(z[s])
                norm_sum.moments(dve)
                norm_sum.apply(dve, z[s], z[s], z_normed)
                dve.wait_ge(z_normed, NT)
                nc.vector.tensor_tensor(z[s][:, :, :], z[s][:, :, :],
                                        gamma_b[:, None, :].broadcast_to([P, NT, D]), ALU.mult).then_inc(affine, 1)
                dve.wait_ge(affine, 1)
                nc.vector.tensor_tensor(z[s][:, :, :], z[s][:, :, :],
                                        beta_b[:, None, :].broadcast_to([P, NT, D]), ALU.add).then_inc(affine, 1)
                dve.wait_ge(affine, 2)
                norm_out.statistics(z[s])
                norm_out.moments(dve)
                norm_out.apply(dve, z[s], z[s], z_normed)
                dve.wait_ge(z_normed, 2 * NT)
                nc.vector.tensor_tensor(z[s][:, :, :], x[s][:, :, :], z[s][:, :, :], ALU.add).then_inc(y_ready, 1)

            def tail_pool(pool):
                norm_sum.root(pool, minus_half[:, :])
                norm_out.root(pool, minus_half[:, :])

            def tail_store(sp, k, s):
                sp.wait_ge(y_ready, 1)
                sp.dma_start(rows(x_out, k), z[s][:, :, :]).then_inc(stored, 16)

            def set_up():
                with nc.Block() as block:
                    @block.sync
                    def _(sp):
                        sp.dma_start(fresh[:, :, :], rows(x_in, 0)).then_inc(x_loaded, 16)
                        sp.dma_start(q[:, 0, :], W_Q).then_inc(w_in, 16)
                        sp.dma_start(q[:, 1, :], W_K).then_inc(w_in, 16)
                        sp.dma_start(wvt[:, :, :], W_VT.rearrange("(f p) d -> p f d", p=P)).then_inc(w_in, 16)
                        sp.dma_start(wfc[:, :, :], W_fc.rearrange("(f p) d -> p f d", p=P)).then_inc(w_in, 16)
                        sp.dma_start(ident[:, :], c_ident).then_inc(w_in, 16)
                        sp.dma_start(headcol[:, :, :], c_headcol.rearrange("p (f c) -> p f c", f=NF)).then_inc(w_in, 16)
                        sp.dma_start(q[:, 2, :], c_headsel).then_inc(w_in, 16)
                        sp.dma_start(gamma_b[:, :], gamma.rearrange("(a d) -> a d", a=1).broadcast_to([P, D])).then_inc(w_in, 16)
                        sp.dma_start(beta_b[:, :], beta.rearrange("(a d) -> a d", a=1).broadcast_to([P, D])).then_inc(w_in, 16)

                    @block.gpsimd
                    def _(pool):
                        nc.gpsimd.memset(minus_half[:, :], -0.5).then_inc(constants_ready, 1)
                        for i in range(2):
                            nc.gpsimd.memset(xn[i][:, :, D:D + 1], 1.0).then_inc(constants_ready, 1)
                        pool.wait_ge(constants_ready, 3)
                        norm_in.root(pool, minus_half[:, :])
                        pool.wait_ge(x_loaded, 16)
                        nc.gpsimd.tensor_copy(x[0][:, :, :], fresh[:, :, :])

                    @block.scalar
                    def _(act):
                        head_act(act, 0, 6)

                    @block.vector
                    def _(dve):
                        nc.vector.memset(rden_hi[:, :, :, :].bitcast(F32), 0.0)
                        nc.vector.memset(rden_lo[:, :, :, :].bitcast(F32), 0.0)
                        head_dve(dve, 0)
                        dve.wait_ge(w_in, 9 * 16)
                        split(nc, dve, wq_hi[:, :], wq_lo[:, :], q[:, 0, :], w_ready, 0)
                        split(nc, dve, wk_hi[:, :], wk_lo[:, :], q[:, 1, :], w_ready, 2)
                        nc.vector.tensor_copy(headsel[:, :, :].rearrange("p f c -> p (f c)"), q[:, 2, :])
                        head_lower(dve, 0, 6)
                        for n in range(H0 // 4):
                            dve.wait_ge(wvfc_mm, n + 1)
                            nc.vector.tensor_copy(wvfc[:, 4 * n:4 * n + 4, :].rearrange("p h d -> p (h d)"), ps[:, n, :])

                    @block.tensor
                    def _(pe):
                        pe.wait_ge(w_in, 9 * 16)
                        for n in range(H0):
                            s, f = n // NF, n % NF
                            mm = pe.matmul(ps[:, n // 4, (n % 4) * D:(n % 4 + 1) * D], wvt[64 * s:64 * s + 64, f, :],
                                           wfc[64 * s:64 * s + 64, f, :], start=True, stop=True)
                            if n % 4 == 3:
                                mm.then_inc(wvfc_mm, 1)
                        head_pe(pe, 0, 6)

            def tail():
                with nc.Block() as block:
                    @block.sync
                    def _(sp):
                        tail_store(sp, B - 1, 1)
                        sp.wait_ge(stored, 16)

                    @block.gpsimd
                    def _(pool):
                        tail_pool(pool)

                    @block.vector
                    def _(dve):
                        tail_dve(dve, 1)

            def turn(k, s, has_head=True, has_tail=True):
                with nc.Block() as block:
                    @block.sync
                    def _(sp):
                        if has_head:
                            sp.dma_start(fresh[:, :, :], rows(x_in, k + 1)).then_inc(x_loaded, 16)
                        clear(sp, others)
                        if has_tail:
                            tail_store(sp, k - 1, 1 - s)
                            sp.wait_ge(stored, 16)

                    @block.gpsimd
                    def _(pool):
                        if has_tail:
                            tail_pool(pool)
                        if has_head:
                            norm_in.root(pool, minus_half[:, :])
                            if has_tail:
                                pool.wait_ge(y_ready, 1)
                            pool.wait_ge(x_loaded, 16)
                            nc.gpsimd.tensor_copy(x[1 - s][:, :, :], fresh[:, :, :])

                    @block.scalar
                    def _(act):
                        for t in range(NT):
                            for c in range(2):
                                n = 2 * t + c
                                act.wait_ge(k_mm, n + 1)
                                if t >= 2 and c == 0:
                                    act.wait_ge(kx_mm, t - 1)
                                nc.scalar.activation(kn[:, t % 2, c * CH:(c + 1) * CH], ps[:, n % 4, :],
                                                     ACT.Sigmoid).then_inc(k_ready, 1)
                        for n in range(NF * NC):
                            c, f = n // NF, n % NF
                            act.wait_ge(q_mm, n + 1)
                            nc.scalar.activation(q[:, f, c * CH:(c + 1) * CH], ps[:, n % 4, :],
                                                 ACT.Sigmoid).then_inc(q_ready, 1)
                            if n == 5:
                                for i in range(2):
                                    act.wait_ge(kxt_mm, 4 * (i + 1))
                                    nc.scalar.copy(kxt[:, 4 * i:4 * i + 4, :].rearrange("p f d -> p (f d)"),
                                                   ps[:, 6 + i, :]).then_inc(kxt_ready, 1)
                            if n == 9:
                                for i in range(2):
                                    act.wait_ge(m_mm, 4 * (i + 1))
                                    nc.scalar.copy(m[:, 4 * i:4 * i + 4, :].rearrange("p f d -> p (f d)"),
                                                   ps[:, 6 + i, :]).then_inc(m_ready, 1)
                        if has_head:
                            head_act(act, 1 - s, 6)

                    @block.vector
                    def _(dve):
                        if has_tail:
                            tail_dve(dve, 1 - s)
                        if has_head:
                            head_dve(dve, 1 - s)
                        dve.wait_ge(kx_mm, NT)
                        for f in range(NF // 2):
                            nc.vector.tensor_copy(kx[:, 2 * f:2 * f + 2, :],
                                                  ps[:, 4 + f, 0:2 * (D + 1)].rearrange("p (a d) -> p a d", a=2)
                                                  ).then_inc(kx_copied, 1)
                        dve.wait_ge(kx_copied, NF // 2)
                        nc.vector.tensor_tensor(ksum_col[:, :, :], headcol[:, :, :],
                                                kx[:, :, D:D + 1].broadcast_to([P, NF, 32]), ALU.mult).then_inc(ksum_ready, 1)

                        def invert(c):
                            dve.wait_ge(den_mm, c + 1)
                            nc.vector.tensor_scalar(den[c][:, :], ps[:, 4 + c, 0:P], DEN_EPS, None,
                                                    ALU.add).then_inc(den_step, 1)
                            dve.wait_ge(den_step, 6 * c + 1)
                            nc.vector.reciprocal(rden[c][:, :], den[c][:, :]).then_inc(den_step, 1)
                            dve.wait_ge(den_step, 6 * c + 2)
                            for g in range(4):
                                nc.vector.tensor_copy(rden_hi[32 * g:32 * g + 32, c, g, :],
                                                      rden[c][32 * g:32 * g + 32, :]).then_inc(den_step, 1)
                            dve.wait_ge(den_step, 6 * c + 6)
                            for g in range(4):
                                nc.vector.tensor_tensor(rden_lo[32 * g:32 * g + 32, c, g, :], rden[c][32 * g:32 * g + 32, :],
                                                        f32(rden_hi[32 * g:32 * g + 32, c, g, :]),
                                                        ALU.subtract).then_inc(rden_ready, 1)

                        invert(0)
                        for n in range(NF * NC):
                            c, f = n // NF, n % NF
                            dve.wait_ge(spread_mm, n + 1)
                            cols = slice(c * CH, (c + 1) * CH)
                            nc.vector.tensor_tensor(q[:, f, cols], q[:, f, cols], ps[:, n % 4, :],
                                                    ALU.mult).then_inc(qd_ready, 1)
                            if n == 3:
                                invert(1)
                            if n == NF - 1 and has_head:
                                head_lower(dve, 1 - s, 6)
                        for c in range(NC):
                            dve.wait_ge(out_mm, 4 * (c + 1))
                            nc.vector.tensor_tensor(z[s][:, 4 * c:4 * c + 4, :],
                                                    ps[:, 6 + c, :].rearrange("p (t d) -> p t d", t=4),
                                                    xn[s][:, 4 * c:4 * c + 4, 0:D], ALU.add)

                    @block.tensor
                    def _(pe):
                        def three(out, lhs, rhs):
                            pe.matmul(out, lhs[0], rhs[0], start=True, stop=False)
                            pe.matmul(out, lhs[0], rhs[1], start=False, stop=False)
                            return pe.matmul(out, lhs[1], rhs[0], start=False, stop=True)

                        def k_times_x(t):
                            pe.wait_ge(k_ready, 2 * t + 2)
                            for f in range(NF):
                                mm = pe.matmul(ps[:, 4 + f // 2, (f % 2) * (D + 1):(f % 2 + 1) * (D + 1)],
                                               kn[:, t % 2, f * P:(f + 1) * P], xn[s][:, t, :],
                                               start=(t == 0 and f % 2 == 0), stop=(t == NT - 1), skip_group_check=True)
                            mm.then_inc(kx_mm, 1)

                        for t in range(NT):
                            toks = slice(t * P, (t + 1) * P)
                            for c in range(2):
                                n = 2 * t + c
                                if n >= 4:
                                    pe.wait_ge(k_ready, n - 3)
                                cols = slice(c * CH, (c + 1) * CH)
                                three(ps[:, n % 4, :], (xt_hi[s][:, toks], xt_lo[s][:, toks]),
                                      (wk_hi[:, cols], wk_lo[:, cols])).then_inc(k_mm, 1)
                            if t >= 1:
                                k_times_x(t - 1)
                        k_times_x(NT - 1)

                        def transpose_sums():
                            pe.wait_ge(kx_copied, NF // 2)
                            for f in range(NF):
                                pe.transpose(ps[:, 6 + f // 4, (f % 4) * P:(f % 4 + 1) * P], kx[:, f, 0:D],
                                             ident[:, :]).then_inc(kxt_mm, 1)

                        def times_wvfc():
                            pe.wait_ge(kxt_ready, 2)
                            for f in range(NF):
                                for h in range(2):
                                    mm = pe.matmul(ps[64 * h:64 * h + 64, 6 + f // 4, (f % 4) * P:(f % 4 + 1) * P],
                                                   kxt[:, f, 64 * h:64 * h + 64], wvfc[:, NF * h + f, :],
                                                   start=True, stop=True)
                                mm.then_inc(m_mm, 1)

                        def den_of(n):
                            c, f = n // NF, n % NF
                            pe.wait_ge(q_ready, n + 1)
                            pe.wait_ge(ksum_ready, 1)
                            for g in range(4):
                                mm = pe.matmul(ps[32 * g:32 * g + 32, 4 + c, 0:P], ksum_col[:, f, :],
                                               q[:, f, c * CH + P * g:c * CH + P * (g + 1)],
                                               start=(f == 0), stop=(f == NF - 1))
                            if f == NF - 1:
                                mm.then_inc(den_mm, 1)

                        LAG = 4
                        for n in range(NF * NC):
                            c, f = n // NF, n % NF
                            blk, cols = slice(f * P, (f + 1) * P), slice(c * CH, (c + 1) * CH)
                            if n >= 4:
                                pe.wait_ge(q_ready, n - 3)
                            else:
                                pe.wait_ge(k_ready, 2 * NT - 3 + n)
                            three(ps[:, n % 4, :], (wq_hi[:, blk], wq_lo[:, blk]),
                                  (xt_hi[s][:, cols], xt_lo[s][:, cols])).then_inc(q_mm, 1)
                            if n == 3:
                                transpose_sums()
                            if n == 7:
                                times_wvfc()
                            if n >= LAG:
                                den_of(n - LAG)
                        for n in range(NF * NC - LAG, NF * NC):
                            den_of(n)

                        def spread(n):
                            c, f = n // NF, n % NF
                            if n >= 4:
                                pe.wait_ge(qd_ready, n - 3)
                            else:
                                pe.wait_ge(q_ready, NF * NC - 3 + n)
                            pe.wait_ge(rden_ready, 4 * (c + 1))
                            pe.matmul(ps[:, n % 4, :], headsel[:, f, :],
                                      rden_hi[:, c, :, :].rearrange("p a n -> p (a n)"), start=True, stop=False)
                            pe.matmul(ps[:, n % 4, :], headsel[:, f, :],
                                      rden_lo[:, c, :, :].rearrange("p a n -> p (a n)"),
                                      start=False, stop=True).then_inc(spread_mm, 1)

                        def out_of(t):
                            c = t // 4
                            pe.wait_ge(qd_ready, NF * (c + 1))
                            if has_head:
                                pe.wait_ge(xt_ready, c + 1)
                            for f in range(NF):
                                mm = pe.matmul(ps[:, 6 + c, (t % 4) * D:(t % 4 + 1) * D], q[:, f, t * P:(t + 1) * P],
                                               m[:, f, :], start=(f == 0), stop=(f == NF - 1))
                            mm.then_inc(out_mm, 1)

                        for n in range(4):
                            spread(n)
                        pe.wait_ge(m_ready, 2)
                        if has_head:
                            head_pe(pe, 1 - s, 6)
                        for n in range(4, NF + 4):
                            spread(n)
                        for t in range(4):
                            out_of(t)
                            spread(NF + 4 + t)
                        for t in range(4, NT):
                            out_of(t)
            return set_up, turn, tail

        turns(nc, ctx, "la_", program)


def feed_forward(nc, tag, x_in, x_out, w1t, w1s, w2t, w2s, h1t, h1s, h2t, h2s, w3t, w3s, c_ident):
    with ExitStack() as ctx:
        def sb(name, shape, dt=F32):
            return ctx.enter_context(nc.sbuf_tensor(tag + name, shape, dt))

        ps = ctx.enter_context(nc.psum_tensor(tag + "ps", [P, 8, CH], F32))

        ident = sb("ident", [P, P])
        w1, w2 = sb("w1", [P, HID], F32R), sb("w2", [P, HID], F32R)
        h1, h2 = sb("h1", [P, NB, HID], F32R), sb("h2", [P, NB, HID], F32R)
        w3 = sb("w3", [P, NB, D], F32R)
        raw = sb("raw", [P, 2 * HID + 2 * NB * HID + NB * D])
        s1, s2, s3, s4 = (sb(f"s{i}", [P, NB]) for i in range(4))
        s5 = sb("s5", [P, D])
        minus_half = sb("minus_half", [P, NT])

        x = [sb(f"x{i}", [P, NT, D]) for i in range(2)]
        fresh = sb("fresh", [P, NT, D])
        xn = sb("xn", [P, NT, D])
        xt_hi = [sb(f"xt_hi{i}", [P, N], F32R) for i in range(2)]
        xt_lo = [sb(f"xt_lo{i}", [P, N], F32R) for i in range(2)]
        z = [sb(f"z{i}", [P, NT, D]) for i in range(2)]
        hid_hi = [sb(f"hid_hi{i}", [P, NB, CH], F32R) for i in range(3)]
        hid_lo = [sb(f"hid_lo{i}", [P, NB, CH], F32R) for i in range(3)]
        gate = sb("gate", [P, 3, CH])
        full = sb("full", [P, 3, CH])
        norm_in_bufs = norm_buffers(sb, "norm_in")
        norm_out_bufs = norm_buffers(sb, "norm_out")

        def program(sem, others):
            norm_in = Norm(nc, norm_in_bufs, sem, "norm_in")
            norm_out = Norm(nc, norm_out_bufs, sem, "norm_out")

            w_in = sem("w_in")
            x_loaded = sem("x_loaded")
            constants_ready = sem("constants_ready")
            xn_ready = sem("xn_ready")
            xt_mm = sem("xt_mm")
            xt_hi_ready = sem("xt_hi_ready")
            xt_ready = sem("xt_ready")
            up_mm = sem("up_mm")
            gate_ready = sem("gate_ready")
            full_ready = sem("full_ready")
            hi_ready = sem("hi_ready")
            lo_ready = sem("lo_ready")
            hid_mm = sem("hid_mm")
            gelu_full = sem("gelu_full")
            gelu_hi = sem("gelu_hi")
            gelu_lo = sem("gelu_lo")
            out_mm = sem("out_mm")
            late_out_mm = sem("late_out_mm")
            late_z_ready = sem("late_z_ready")
            z_normed = sem("z_normed")
            y_ready = sem("y_ready")
            stored = sem("stored")

            o1, o2 = 2 * HID, 2 * HID + NB * HID
            o3 = o2 + NB * HID

            SRC = ((None, 0, 2), (None, 1, 0))
            DST = ((0, 2, 1), (1, 0, 2))

            TR = 6

            def bank_of(n):
                return 6 + n if n < 2 else (n - 2) % 6

            LAST_UP = (6, 7, 5)

            def head_pe(pe, s):
                for t in range(NT):
                    pe.wait_ge(xn_ready, t + 1)
                    pe.transpose(ps[:, TR + t // 4, (t % 4) * P:(t % 4 + 1) * P], xn[:, t, :],
                                 ident[:, :]).then_inc(xt_mm, 1)

            def head_act(act, s, c):
                act.wait_ge(xt_mm, 4 * (c + 1))
                nc.scalar.copy(xt_hi[s][:, c * CH:(c + 1) * CH], ps[:, TR + c, :]).then_inc(xt_hi_ready, 1)

            def head_lower(dve, s, c):
                dve.wait_ge(xt_hi_ready, c + 1)
                nc.vector.tensor_tensor(xt_lo[s][:, c * CH:(c + 1) * CH], ps[:, TR + c, :],
                                        f32(xt_hi[s][:, c * CH:(c + 1) * CH]), ALU.subtract).then_inc(xt_ready, 1)

            first, second = range(NT // 2), range(NT // 2, NT)

            def tail_step(dve, s, i):
                if i == 0:
                    norm_out.statistics(z[s], first)
                elif i == 1:
                    norm_out.statistics(z[s], second)
                elif i == 2:
                    norm_out.moments(dve)
                elif i == 3:
                    norm_out.apply(dve, z[s], z[s], z_normed, first)
                elif i == 4:
                    norm_out.apply(dve, z[s], z[s], z_normed, second)
                elif i == 5:
                    dve.wait_ge(z_normed, NT)
                    nc.vector.tensor_tensor(z[s][:, :, :], x[s][:, :, :], z[s][:, :, :], ALU.add).then_inc(y_ready, 1)

            def head_step(dve, s, i):
                if i == 0:
                    dve.wait_ge(x_loaded, 16)
                    norm_in.statistics(fresh, first)
                elif i == 1:
                    norm_in.statistics(fresh, second)
                elif i == 2:
                    norm_in.moments(dve)
                elif i == 3:
                    norm_in.apply(dve, xn, fresh, xn_ready, first)
                elif i == 4:
                    norm_in.apply(dve, xn, fresh, xn_ready, second)

            def out_of(pe, c, t, done):
                src, toks = DST[c][2], slice(t * P, (t + 1) * P)
                for k_ in range(NB):
                    pe.matmul(ps[:, TR + c, t * D:(t + 1) * D], hid_hi[src][:, k_, toks],
                              w3[:, k_, :], start=(k_ == 0), stop=False)
                    mm = pe.matmul(ps[:, TR + c, t * D:(t + 1) * D], hid_lo[src][:, k_, toks],
                                   w3[:, k_, :], start=False, stop=(k_ == NB - 1))
                mm.then_inc(done, 1)

            def z_of(dve, s, c, done):
                dve.wait_ge(done, 4)
                return nc.vector.tensor_tensor(z[s][:, 4 * c:4 * c + 4, :],
                                               ps[:, TR + c, :].rearrange("p (t d) -> p t d", t=4),
                                               s5[:, None, :].broadcast_to([P, 4, D]), ALU.mult)

            def late_z(dve, s):
                z_of(dve, s, 1, late_out_mm).then_inc(late_z_ready, 1)

            def tail_store(sp, k, s):
                sp.wait_ge(y_ready, 1)
                sp.dma_start(rows(x_out, k), z[s][:, :, :]).then_inc(stored, 16)

            def set_up():
                with nc.Block() as block:
                    @block.sync
                    def _(sp):
                        sp.dma_start(fresh[:, :, :], rows(x_in, 0)).then_inc(x_loaded, 16)
                        sp.dma_start(ident[:, :], c_ident).then_inc(w_in, 16)
                        sp.dma_start(raw[:, 0:HID], w1t).then_inc(w_in, 16)
                        sp.dma_start(raw[:, HID:o1], w2t).then_inc(w_in, 16)
                        sp.dma_start(raw[:, o1:o2].rearrange("p (k o) -> p k o", k=NB),
                                     h1t.rearrange("(k p) o -> p k o", p=P)).then_inc(w_in, 16)
                        sp.dma_start(raw[:, o2:o3].rearrange("p (k o) -> p k o", k=NB),
                                     h2t.rearrange("(k p) o -> p k o", p=P)).then_inc(w_in, 16)
                        sp.dma_start(raw[:, o3:].rearrange("p (k o) -> p k o", k=NB),
                                     w3t.rearrange("(k p) o -> p k o", p=P)).then_inc(w_in, 16)
                        for s, src in ((s1, w1s), (s2, w2s), (s3, h1s), (s4, h2s)):
                            sp.dma_start(s[:, :], src).then_inc(w_in, 16)
                        sp.dma_start(s5[:, :], w3s.rearrange("(a d) -> a d", a=1).broadcast_to([P, D])).then_inc(w_in, 16)

                    @block.gpsimd
                    def _(pool):
                        nc.gpsimd.memset(minus_half[:, :], -0.5).then_inc(constants_ready, 1)
                        pool.wait_ge(constants_ready, 1)
                        norm_in.root(pool, minus_half[:, :])
                        pool.wait_ge(x_loaded, 16)
                        nc.gpsimd.tensor_copy(x[0][:, :, :], fresh[:, :, :])

                    @block.scalar
                    def _(act):
                        for c in range(NC):
                            head_act(act, 0, c)

                    @block.vector
                    def _(dve):
                        for i in range(5):
                            head_step(dve, 0, i)
                        dve.wait_ge(w_in, 11 * 16)
                        nc.vector.tensor_copy(w1[:, :], raw[:, 0:HID])
                        nc.vector.tensor_copy(w2[:, :], raw[:, HID:o1])
                        nc.vector.tensor_copy(h1[:, :, :].rearrange("p k o -> p (k o)"), raw[:, o1:o2])
                        nc.vector.tensor_copy(h2[:, :, :].rearrange("p k o -> p (k o)"), raw[:, o2:o3])
                        nc.vector.tensor_copy(w3[:, :, :].rearrange("p k o -> p (k o)"), raw[:, o3:])
                        for c in range(NC):
                            head_lower(dve, 0, c)

                    @block.tensor
                    def _(pe):
                        pe.wait_ge(w_in, 11 * 16)
                        head_pe(pe, 0)

            def tail():
                with nc.Block() as block:
                    @block.sync
                    def _(sp):
                        tail_store(sp, B - 1, 1)
                        sp.wait_ge(stored, 16)

                    @block.gpsimd
                    def _(pool):
                        norm_out.root(pool, minus_half[:, :])

                    @block.vector
                    def _(dve):
                        late_z(dve, 1)
                        dve.wait_ge(late_z_ready, 1)
                        for i in range(6):
                            tail_step(dve, 1, i)

                    @block.tensor
                    def _(pe):
                        for t in range(4):
                            out_of(pe, 1, t, late_out_mm)

            def turn(k, s, has_head=True, has_tail=True):
                with nc.Block() as block:
                    @block.sync
                    def _(sp):
                        if has_head:
                            sp.dma_start(fresh[:, :, :], rows(x_in, k + 1)).then_inc(x_loaded, 16)
                        clear(sp, others)
                        if has_tail:
                            tail_store(sp, k - 1, 1 - s)
                            sp.wait_ge(stored, 16)

                    @block.gpsimd
                    def _(pool):
                        if has_head:
                            norm_in.root(pool, minus_half[:, :])
                        if has_tail:
                            norm_out.root(pool, minus_half[:, :])
                            pool.wait_ge(y_ready, 1)
                        if has_head:
                            pool.wait_ge(x_loaded, 16)
                            nc.gpsimd.tensor_copy(x[1 - s][:, :, :], fresh[:, :, :])

                    @block.scalar
                    def _(act):
                        def upper(n):
                            act.wait_ge(full_ready, n + 1)
                            nc.scalar.copy(hid_hi[DST[n // NB][0]][:, n % NB, :], full[:, n % 3, :]).then_inc(hi_ready, 1)

                        for n in range(NB * NC):
                            act.wait_ge(up_mm, n + 1)
                            if n >= 3:
                                act.wait_ge(full_ready, n - 2)
                            nc.scalar.activation(gate[:, n % 3, :], ps[:, n % 3, :], ACT.Silu,
                                                 scale=s1[:, n % NB:n % NB + 1]).then_inc(gate_ready, 1)
                            if n >= 1:
                                upper(n - 1)
                        upper(NB * NC - 1)
                        for n in range(2 * NB * NC):
                            stage, c, o = 1 + n // (NB * NC), n // NB % NC, n % NB
                            scale = (s3, s4)[stage - 1][:, o:o + 1]
                            act.wait_ge(hid_mm, n + 1)
                            nc.scalar.activation(hid_hi[DST[c][stage]][:, o, :], ps[:, bank_of(n), :], ACT.Gelu,
                                                 scale=scale).then_inc(gelu_hi, 1)
                            if n >= 3:
                                act.wait_ge(gelu_lo, n - 2)
                            else:
                                act.wait_ge(lo_ready, NB * NC)
                            nc.scalar.activation(full[:, n % 3, :], ps[:, bank_of(n), :], ACT.Gelu,
                                                 scale=scale).then_inc(gelu_full, 1)
                            if has_head and n in (5, 6):
                                head_act(act, 1 - s, n - 5)

                    @block.vector
                    def _(dve):
                        def lower(n):
                            dve.wait_ge(hi_ready, n + 1)
                            buf = DST[n // NB][0]
                            nc.vector.tensor_tensor(hid_lo[buf][:, n % NB, :], full[:, n % 3, :],
                                                    f32(hid_hi[buf][:, n % NB, :]), ALU.subtract).then_inc(lo_ready, 1)

                        for n in range(NB * NC):
                            dve.wait_ge(gate_ready, n + 1)
                            if n >= 3:
                                dve.wait_ge(lo_ready, n - 2)
                            nc.vector.scalar_tensor_tensor(out=full[:, n % 3, :], in0=ps[:, 3 + n % 3, :],
                                                           scalar=s2[:, n % NB:n % NB + 1], in1=gate[:, n % 3, :],
                                                           op0=ALU.mult, op1=ALU.mult).then_inc(full_ready, 1)
                            if n >= 1:
                                lower(n - 1)
                        lower(NB * NC - 1)
                        if has_tail:
                            late_z(dve, 1 - s)
                        for n in range(2 * NB * NC):
                            stage, c, o = 1 + n // (NB * NC), n // NB % NC, n % NB
                            buf = DST[c][stage]
                            dve.wait_ge(gelu_full, n + 1)
                            nc.vector.tensor_tensor(hid_lo[buf][:, o, :], full[:, n % 3, :], f32(hid_hi[buf][:, o, :]),
                                                    ALU.subtract).then_inc(gelu_lo, 1)
                            if has_tail:
                                if n == 4:
                                    dve.wait_ge(late_z_ready, 1)
                                for i in {4: (0,), 5: (1, 2), 7: (3,), 8: (4,), 9: (5,)}.get(n, ()):
                                    tail_step(dve, 1 - s, i)
                            if has_head:
                                for i in {0: (0,), 1: (1, 2), 3: (3,), 4: (4,)}.get(n, ()):
                                    head_step(dve, 1 - s, i)
                                if n in (6, 7):
                                    head_lower(dve, 1 - s, n - 6)
                        z_of(dve, s, 0, out_mm)

                    @block.tensor
                    def _(pe):
                        for n in range(NB * NC):
                            c, f = n // NB, n % NB
                            cols, blk = slice(c * CH, (c + 1) * CH), slice(f * P, (f + 1) * P)
                            if n >= 3:
                                pe.wait_ge(full_ready, n - 2)
                            pe.matmul(ps[:, n % 3, :], w1[:, blk], xt_hi[s][:, cols], start=True, stop=False)
                            pe.matmul(ps[:, n % 3, :], w1[:, blk], xt_lo[s][:, cols], start=False, stop=True)
                            pe.matmul(ps[:, 3 + n % 3, :], w2[:, blk], xt_hi[s][:, cols], start=True, stop=False)
                            pe.matmul(ps[:, 3 + n % 3, :], w2[:, blk], xt_lo[s][:, cols], start=False,
                                      stop=True).then_inc(up_mm, 1)
                            if n >= 4 and has_tail:
                                out_of(pe, 1, n - 4, late_out_mm)
                        for n in range(2 * NB * NC):
                            stage, c, o = 1 + n // (NB * NC), n // NB % NC, n % NB
                            w, src = (h1, h2)[stage - 1], SRC[c][stage]
                            if o == 0:
                                if stage == 1:
                                    pe.wait_ge(lo_ready, NB * (c + 1))
                                else:
                                    pe.wait_ge(gelu_lo, NB * (c + 1))
                            if n < 2:
                                if n == 1 and has_tail:
                                    pe.wait_ge(late_z_ready, 1)
                            elif n < 8:
                                pe.wait_ge(full_ready, LAST_UP[(n - 2) % 3] + 1)
                            else:
                                pe.wait_ge(gelu_full, n - 5)
                            for k_ in range(NB):
                                pe.matmul(ps[:, bank_of(n), :], w[:, k_, o * P:(o + 1) * P], hid_hi[src][:, k_, :],
                                          start=(k_ == 0), stop=False)
                                mm = pe.matmul(ps[:, bank_of(n), :], w[:, k_, o * P:(o + 1) * P], hid_lo[src][:, k_, :],
                                               start=False, stop=(k_ == NB - 1))
                            mm.then_inc(hid_mm, 1)
                            if has_head and n == 5:
                                head_pe(pe, 1 - s)
                        pe.wait_ge(gelu_lo, NB * NC + NB)
                        if has_head:
                            pe.wait_ge(xt_ready, 1)
                        for t in range(4):
                            out_of(pe, 0, t, out_mm)
            return set_up, turn, tail

        turns(nc, ctx, tag, program)


def window_attention(nc, x_in, x_out, WqkvT, bqkv, WgateT, bgate, WoutT, bout, pos_bias, offsets,
                     c_ident, c_dist, c_head_rows, c_turned, table):
    with ExitStack() as ctx:
        def sb(name, shape, dt=F32):
            return ctx.enter_context(nc.sbuf_tensor("wa_" + name, shape, dt))

        ps = ctx.enter_context(nc.psum_tensor("wa_ps", [P, 8, CH], F32))

        BY_VECTOR = (2, 2, 2, 4)
        vector_heads = [GH * g + i for g in range(NG) for i in range(BY_VECTOR[g])]
        tensor_heads = [h for h in range(H1) if h not in vector_heads]

        ident, ident_r = sb("ident", [P, P]), sb("ident_r", [P, P], F32R)
        wqk_hi, wqk_lo = sb("wqk_hi", [P, 2 * D], F32R), sb("wqk_lo", [P, 2 * D], F32R)
        wvg_hi, wvg_lo = sb("wvg_hi", [P, 2 * D], F32R), sb("wvg_lo", [P, 2 * D], F32R)
        wout = sb("wout", [P, D])
        bq, bk = sb("bq", [P, 1]), sb("bk", [P, 1])
        bvg_b, bout_b = sb("bvg_b", [P, 2 * D]), sb("bout_b", [P, D])
        minus_half = sb("minus_half", [P, NT])
        pos, off_i, off_f = sb("pos", [NOFF, H1]), sb("off_i", [NOFF, 1], I32), sb("off_f", [NOFF, 1])
        ones = sb("ones", [NOFF, H1])
        head_rows = sb("head_rows", [P, 2, GH])
        bias_qk = sb("bias_qk", [P, H1, WIN])
        bias_kq = sb("bias_kq", [P, len(vector_heads), WIN])
        bias_kq_hi = sb("bias_kq_hi", [P, len(tensor_heads), WIN], F32R)
        bias_kq_lo = sb("bias_kq_lo", [P, len(tensor_heads), WIN], F32R)

        x = [sb(f"x{i}", [P, NT, D]) for i in range(2)]
        gate = [sb(f"gate{i}", [P, NT, D]) for i in range(2)]
        xn = sb("xn", [P, NT, D])
        z = xn
        xt_hi, xt_lo = sb("xt_hi", [P, N], F32R), sb("xt_lo", [P, N], F32R)
        qk_hi, qk_lo = sb("qk_hi", [P, 2, N], F32R), sb("qk_lo", [P, 2, N], F32R)
        vp = sb("vp", [P, NT, H1, 32])
        qcat = sb("qcat", [P, NG, N], F32R)
        kz = sb("kz", [P, 3, GH, N], F32R)
        top = sb("top", [P, 2, NT, GH])
        negtop = sb("negtop", [P, NT, P])
        prob = sb("prob", [P, 3 * GH * WIN])
        prob_of = prob[:, :].rearrange("p (a i n) -> p a i n", a=3, i=GH)
        qk = prob[:, 0:2 * N].rearrange("p (a n) -> p a n", a=2)
        flat_t = prob[:, 2 * N:3 * N]
        k_parts = [qk[:, 0, :]] + [f32(xt_hi[:, :])] * (NG - 1)
        junk = f32(qk_lo[:, 0, 0:3 * WIN]).rearrange("p (a n) -> p a n", a=3)
        ot = sb("ot", [P, N])
        rden = sb("rden", [P, 4, GH, 1])
        flat = sb("flat", [P, NT, D])
        last_rows = f32(qk_lo[:, :, :]).rearrange("p a n -> p (a n)")[:, 0:GH * WIN].rearrange("p (a n) -> p a n", a=GH)
        raw = gate[1][:, :, :].rearrange("p t d -> p (t d)")[:, 4 * D:8 * D]
        dist = flat[:, :, :].rearrange("p t d -> p (t d)")[0:NOFF, 0:2 * TAB]
        hit = ot[0:NOFF, 0:2 * TAB]
        missing = x[1][:, :, :].rearrange("p t d -> p (t d)")[0:H1, 0:2 * TAB].rearrange("p (a n) -> p a n", a=2)
        bias_row = gate[0][:, :, :].rearrange("p t d -> p (t d)")[0:H1, 0:2 * TAB].rearrange("p (a n) -> p a n", a=2)
        turned = gate[1][:, 0, :]
        norm_in_bufs = norm_buffers(sb, "norm_in")
        norm_out_bufs = norm_buffers(sb, "norm_out")

        def program(sem, others):
            norm_in = Norm(nc, norm_in_bufs, sem, "norm_in")
            norm_out = Norm(nc, norm_out_bufs, sem, "norm_out")

            w_in = sem("w_in")
            w_ready = sem("w_ready")
            hit_ready = sem("hit_ready")
            table_mm = sem("table_mm")
            table_step = sem("table_step")
            table_out = sem("table_out")
            table_in = sem("table_in")
            flip_mm = sem("flip_mm")
            flip_copied = sem("flip_copied")
            x_loaded = sem("x_loaded")
            constants_ready = sem("constants_ready")
            xn_ready = sem("xn_ready")
            xt_mm = sem("xt_mm")
            xt_hi_ready = sem("xt_hi_ready")
            xt_ready = sem("xt_ready")
            qk_mm = sem("qk_mm")
            qk_biased = sem("qk_biased")
            qk_ready = sem("qk_ready")
            q_in = [sem(f"q_in{i}") for i in range(2)]
            q_lo_in = sem("q_lo_in")
            k_in = [sem(f"k_in{g}") for g in range(NG)]
            k_ready = sem("k_ready")
            rows_zero = sem("rows_zero")
            vg_mm = sem("vg_mm")
            v_ready = sem("v_ready")
            gate_ready = sem("gate_ready")
            s_mm = sem("s_mm")
            top_taken = sem("top_taken")
            bias_added = sem("bias_added")
            top_step = sem("top_step")
            top_mm = sem("top_mm")
            top_ready = sem("top_ready")
            prob_ready = sem("prob_ready")
            pv_mm = sem("pv_mm")
            ot_copied = sem("ot_copied")
            back_mm = sem("back_mm")
            rden_ready = sem("rden_ready")
            flat_ready = sem("flat_ready")
            last_back_mm = sem("last_back_mm")
            last_rden_ready = sem("last_rden_ready")
            last_flat_ready = sem("last_flat_ready")
            gated = sem("gated")
            flat_t_mm = sem("flat_t_mm")
            flat_t_ready = sem("flat_t_ready")
            out_mm = sem("out_mm")
            z_ready = sem("z_ready")
            z_normed = sem("z_normed")
            y_ready = sem("y_ready")
            stored = sem("stored")


            QP = (0, 0, 1)
            KP = (0, 1, 0)

            TOPS, PROBS = 0, 1
            steps = []
            for r in range(NG + 1):
                for u in range(NT + 1):
                    if r < NG and u < NT:
                        steps.append((TOPS, r, u))
                    if r >= 1 and u >= 1:
                        steps.append((PROBS, r - 1, u - 1))
            place = {step: m for m, step in enumerate(steps)}

            def early(r, u):
                return GH - BY_VECTOR[r - 1] if 1 <= r < NG and 1 <= u < NT - 1 else 0

            issued = []
            for r in range(NG + 1):
                for u in range(NT + 1):
                    if r < NG and u < NT:
                        issued += [(TOPS, r, u, i) for i in range(early(r, u - 1), GH)]
                    if r >= 1 and u >= 1:
                        issued += [(PROBS, r - 1, u - 1, i) for i in range(BY_VECTOR[r - 1])]
                        for i in range(BY_VECTOR[r - 1], GH):
                            issued.append((PROBS, r - 1, u - 1, i))
                            if early(r, u):
                                issued.append((TOPS, r, u + 1, i - BY_VECTOR[r - 1]))
            count = {scores: n + 1 for n, scores in enumerate(issued)}

            def scores_done(kind, g, t, i):
                return count[kind, g, t, i]

            def added_before(g, t):
                return NT * sum(BY_VECTOR[:g]) + BY_VECTOR[g] * t

            def keys_of(t):
                lo = max(0, P * t - REACH)
                return lo, lo - (P * t - REACH)

            def queries_of(j):
                return min(WIN, N - P * j)

            TAIL_AT, HEAD_AT = (1, 1), (3, 1)
            TR = 6
            VG_BANKS = (4, 5, 0, 1)

            def head_step(dve, s, i, stored_before):
                pair = range(2 * (i % 6), 2 * (i % 6) + 2)
                if 0 <= i < 4:
                    if i == 0:
                        dve.wait_ge(x_loaded, 16)
                    norm_in.statistics(x[s], pair)
                elif i == 4:
                    norm_in.moments(dve)
                elif 6 <= i < 10:
                    if i == 6 and stored_before:
                        dve.wait_ge(stored, 16)
                    norm_in.apply(dve, xn, x[s], xn_ready, pair)

            def head_pe(pe):
                for t in range(NT):
                    pe.wait_ge(xn_ready, t + 1)
                    pe.transpose(ps[:, TR + t // 4, (t % 4) * P:(t % 4 + 1) * P], xn[:, t, :],
                                 ident[:, :]).then_inc(xt_mm, 1)

            def head_act(act):
                for c in range(NC):
                    act.wait_ge(xt_mm, 4 * (c + 1))
                    nc.scalar.copy(xt_hi[:, c * CH:(c + 1) * CH], ps[:, TR + c, :]).then_inc(xt_hi_ready, 1)

            def head_lower(dve):
                for c in range(NC):
                    dve.wait_ge(xt_hi_ready, c + 1)
                    nc.vector.tensor_tensor(xt_lo[:, c * CH:(c + 1) * CH], ps[:, TR + c, :],
                                            f32(xt_hi[:, c * CH:(c + 1) * CH]), ALU.subtract).then_inc(xt_ready, 1)

            def back(pe, done):
                for t in range(NT):
                    pe.transpose(ps[:, TR + t // 4, (t % 4) * P:(t % 4 + 1) * P], ot[:, t * P:(t + 1) * P],
                                 ident[:, :]).then_inc(done, 1)

            def divide(dve, g, before, turned_back, inverse, divided):
                for c in range(NC):
                    dve.wait_ge(turned_back, NT * before + 4 * (c + 1))
                    if before + c >= 1:
                        dve.wait_ge(divided, NC * before + c)
                    bank = ps[:, TR + c, :].rearrange("p (t i e) -> p t i e", t=4, i=GH)
                    nc.vector.reciprocal(rden[:, :, :, :], bank[:, :, :, HD:HD + 1]).then_inc(inverse, 1)
                    dve.wait_ge(inverse, NC * before + c + 1)
                    nc.vector.tensor_tensor(
                        flat[:, 4 * c:4 * c + 4, 32 * g:32 * g + 32].rearrange("p t (i e) -> p t i e", i=GH),
                        bank[:, :, :, 0:HD], rden[:, :, :, :].broadcast_to([P, 4, GH, HD]),
                        ALU.mult).then_inc(divided, 1)

            def tail_gate(dve, s):
                divide(dve, NG - 1, 0, last_back_mm, last_rden_ready, last_flat_ready)
                dve.wait_ge(last_flat_ready, NC)
                nc.vector.tensor_tensor(flat[:, :, :], flat[:, :, :], gate[s][:, :, :], ALU.mult).then_inc(gated, 1)

            def tail_flat_t(pe):
                pe.wait_ge(gated, 1)
                for t in range(NT):
                    pe.transpose(ps[:, TR + t // 4, (t % 4) * P:(t % 4 + 1) * P], flat[:, t, :],
                                 ident[:, :]).then_inc(flat_t_mm, 1)

            def tail_act(act):
                for c in range(NC):
                    act.wait_ge(flat_t_mm, 4 * (c + 1))
                    nc.scalar.copy(flat_t[:, c * CH:(c + 1) * CH], ps[:, TR + c, :]).then_inc(flat_t_ready, 1)

            def tail_out(pe):
                for t in range(NT):
                    if t % 4 == 0:
                        pe.wait_ge(flat_t_ready, t // 4 + 1)
                    pe.matmul(ps[:, TR + t // 4, (t % 4) * D:(t % 4 + 1) * D], flat_t[:, t * P:(t + 1) * P],
                              wout[:, :], start=True, stop=True).then_inc(out_mm, 1)

            def tail_z(dve):
                for c in range(NC):
                    dve.wait_ge(out_mm, 4 * (c + 1))
                    nc.vector.tensor_tensor(z[:, 4 * c:4 * c + 4, :],
                                            ps[:, TR + c, :].rearrange("p (t d) -> p t d", t=4),
                                            bout_b[:, None, :].broadcast_to([P, 4, D]), ALU.add).then_inc(z_ready, 1)

            def tail_step(dve, s, i):
                pair = range(2 * (i % 6), 2 * (i % 6) + 2)
                if 0 <= i < 4:
                    if i == 0:
                        dve.wait_ge(z_ready, NC)
                    norm_out.statistics(z, pair)
                elif i == 4:
                    norm_out.moments(dve)
                elif 6 <= i < 10:
                    norm_out.apply(dve, z, z, z_normed, pair)

            def tail_pool(pool, s):
                norm_out.root(pool, minus_half[:, :])
                pool.wait_ge(z_normed, NT)
                nc.gpsimd.tensor_tensor(z[:, :, :], x[s][:, :, :], z[:, :, :], ALU.add).then_inc(y_ready, 1)

            def tail_store(sp, k):
                sp.wait_ge(y_ready, 1)
                sp.dma_start(rows(x_out, k), z[:, :, :]).then_inc(stored, 16)

            def set_up():
                with nc.Block() as block:
                    @block.sync
                    def _(sp):
                        sp.dma_start(x[0][:, :, :], rows(x_in, 0)).then_inc(x_loaded, 16)
                        sp.dma_start(raw[:, 0:3 * D], WqkvT).then_inc(w_in, 16)
                        sp.dma_start(raw[:, 3 * D:], WgateT).then_inc(w_in, 16)
                        sp.dma_start(wout[:, :], WoutT).then_inc(w_in, 16)
                        sp.dma_start(bq[:, :], bqkv[0:D].rearrange("(p a) -> p a", a=1)).then_inc(w_in, 16)
                        sp.dma_start(bk[:, :], bqkv[D:2 * D].rearrange("(p a) -> p a", a=1)).then_inc(w_in, 16)
                        sp.dma_start(bvg_b[:, 0:D], bqkv[2 * D:].rearrange("(a d) -> a d", a=1).broadcast_to([P, D])).then_inc(w_in, 16)
                        sp.dma_start(bvg_b[:, D:], bgate.rearrange("(a d) -> a d", a=1).broadcast_to([P, D])).then_inc(w_in, 16)
                        sp.dma_start(bout_b[:, :], bout.rearrange("(a d) -> a d", a=1).broadcast_to([P, D])).then_inc(w_in, 16)
                        sp.dma_start(pos[:, :], pos_bias).then_inc(w_in, 16)
                        sp.dma_start(off_i[:, :], offsets.rearrange("(p a) -> p a", a=1)).then_inc(w_in, 16)
                        sp.dma_start(dist, c_dist).then_inc(w_in, 16)
                        sp.dma_start(ident[:, :], c_ident).then_inc(w_in, 16)
                        sp.dma_start(head_rows[:, :, :], c_head_rows.rearrange("p (a i) -> p a i", a=2)).then_inc(w_in, 16)
                        sp.dma_start(turned, c_turned).then_inc(w_in, 16)
                        sp.wait_ge(table_step, 4)
                        sp.dma_start(table, bias_row).then_inc(table_out, 16)
                        sp.wait_ge(table_out, 16)
                        heads = 3 * GH
                        for dst, n, h, nh in ((bias_qk[:, :, :], 0, 0, H1),
                                              (prob[:, :].rearrange("p (h n) -> p h n", h=heads), 1, 0, heads),
                                              (last_rows, 1, heads, H1 - heads)):
                            src = bass.AP(table.tensor, (2 * h + n) * TAB + 1, [[1, P], [2 * TAB, nh], [1, WIN]])
                            sp.dma_start(dst, src).then_inc(table_in, 16)

                    @block.gpsimd
                    def _(pool):
                        nc.gpsimd.memset(minus_half[:, :], -0.5).then_inc(constants_ready, 1)
                        nc.gpsimd.memset(ones[:, :], 1.0).then_inc(w_ready, 1)
                        nc.gpsimd.memset(vp[:, :, :, :], 0.0).then_inc(w_ready, 1)
                        pool.wait_ge(w_ready, 2)
                        nc.gpsimd.memset(vp[:, :, :, HD:HD + 1], 1.0).then_inc(constants_ready, 1)
                        nc.gpsimd.memset(negtop[:, :, :], 0.0).then_inc(constants_ready, 1)
                        pool.wait_ge(constants_ready, 3)
                        norm_in.root(pool, minus_half[:, :])
                        pool.wait_ge(norm_in.rstd_ready, 1)
                        nc.gpsimd.memset(f32(kz[96:128, :, :, :]), 0.0).then_inc(constants_ready, 1)

                    @block.scalar
                    def _(act):
                        head_act(act)
                        act.wait_ge(constants_ready, 4)
                        for i in range(GH):
                            nc.scalar.activation(kz[96:128, :, i, :], f32(kz[96:128, :, i, :]), ACT.Identity,
                                                 bias=head_rows[96:128, 1, i:i + 1])

                    @block.vector
                    def _(dve):
                        dve.wait_ge(w_in, 14 * 16)
                        nc.vector.tensor_copy(off_f[:, :], off_i[:, :]).then_inc(hit_ready, 1)
                        dve.wait_ge(hit_ready, 1)
                        nc.vector.tensor_scalar(hit, dist, off_f[:, 0:1], None, ALU.is_equal).then_inc(hit_ready, 1)
                        split(nc, dve, wqk_hi[:, :], wqk_lo[:, :], raw[:, 0:2 * D], hit_ready, 2)
                        split(nc, dve, wvg_hi[:, :], wvg_lo[:, :], raw[:, 2 * D:], hit_ready, 4)
                        nc.vector.tensor_scalar(bq[:, :], bq[:, :], float(HD) ** -0.5, None, ALU.mult)
                        nc.vector.tensor_copy(ident_r[:, :], ident[:, :])
                        for n in range(2):
                            dve.wait_ge(table_mm, n + 1)
                            nc.vector.tensor_scalar(missing[:, n, :], ps[0:H1, 2 + n, 0:TAB], -1.0, FAR, ALU.add,
                                                    ALU.mult).then_inc(table_step, 1)
                            dve.wait_ge(table_step, 2 * n + 1)
                            nc.vector.tensor_tensor(bias_row[:, n, :], ps[0:H1, n, 0:TAB], missing[:, n, :],
                                                    ALU.add).then_inc(table_step, 1)
                        for i in range(10):
                            head_step(dve, 0, i, False)
                        head_lower(dve)
                        for n in range(2 * H1):
                            dve.wait_ge(flip_mm, n + 1)
                            h, rows_ = n % H1, ps[:, n % 4, 0:WIN]
                            if n >= H1:
                                nc.vector.tensor_copy(bias_qk[:, h, :], rows_).then_inc(flip_copied, 2)
                            elif h in vector_heads:
                                nc.vector.tensor_copy(bias_kq[:, vector_heads.index(h), :], rows_).then_inc(flip_copied, 2)
                            else:
                                m = tensor_heads.index(h)
                                split(nc, dve, bias_kq_hi[:, m, :], bias_kq_lo[:, m, :], rows_, flip_copied, 2 * n)

                    @block.tensor
                    def _(pe):
                        pe.wait_ge(w_ready, 1)
                        pe.wait_ge(hit_ready, 2)
                        for n in range(2):
                            cols = slice(n * TAB, (n + 1) * TAB)
                            pe.matmul(ps[0:H1, n, 0:TAB], pos[:, :], hit[:, cols], start=True, stop=True)
                            pe.matmul(ps[0:H1, 2 + n, 0:TAB], ones[:, :], hit[:, cols], start=True, stop=True).then_inc(table_mm, 1)
                        pe.wait_ge(w_in, 14 * 16)
                        head_pe(pe)
                        pe.wait_ge(table_in, 3 * 16)
                        for n in range(2 * H1):
                            h = n % H1
                            if n < H1:
                                src = bias_qk[:, h, :]
                            elif h < 3 * GH:
                                src = prob[:, h * WIN:(h + 1) * WIN]
                            else:
                                src = last_rows[:, h - 3 * GH, :]
                            if n >= 4:
                                pe.wait_ge(flip_copied, 2 * (n - 3))
                            pe.matmul(ps[:, n % 4, 0:WIN], turned, src, start=True, stop=True).then_inc(flip_mm, 1)

            def tail():
                with nc.Block() as block:
                    @block.sync
                    def _(sp):
                        tail_store(sp, B - 1)
                        sp.wait_ge(stored, 16)

                    @block.gpsimd
                    def _(pool):
                        tail_pool(pool, 1)

                    @block.scalar
                    def _(act):
                        tail_act(act)

                    @block.vector
                    def _(dve):
                        tail_gate(dve, 1)
                        tail_z(dve)
                        for i in range(10):
                            tail_step(dve, 1, i)

                    @block.tensor
                    def _(pe):
                        back(pe, last_back_mm)
                        tail_flat_t(pe)
                        tail_out(pe)

            def turn(k, s, has_head=True, has_tail=True):
                with nc.Block() as block:
                    @block.sync
                    def _(sp):
                        clear(sp, others)
                        def move(dst, part_of, a, g, done, those=range(3)):
                            for r in those:
                                src = (qk_hi, qk_lo)[part_of[r]]
                                sp.dma_start(dst[32 * r:32 * r + 32], f32(src[32 * g:32 * g + 32, a, :])).then_inc(done, 16)

                        sp.wait_ge(qk_ready, 4)
                        move(f32(qcat[:, 0, :]), QP, 0, 0, q_in[0])
                        sp.wait_ge(qk_ready, 8)
                        move(k_parts[0], KP, 1, 0, k_in[0])
                        for g in range(1, NG):
                            move(f32(qcat[:, g, :]), QP, 0, g, q_lo_in, (2,))
                        for g in range(1, NG):
                            move(f32(qcat[:, g, :]), QP, 0, g, q_in[1], (0, 1))
                        for g in range(1, NG):
                            sp.wait_ge(vg_mm, NT)
                            if g >= 2:
                                sp.wait_ge(k_ready, GH * g)
                            move(k_parts[g], KP, 1, g, k_in[g])
                        if has_tail:
                            tail_store(sp, k - 1)
                        if has_head:
                            sp.dma_start(x[1 - s][:, :, :], rows(x_in, k + 1)).then_inc(x_loaded, 16)
                        if has_tail:
                            sp.wait_ge(stored, 16)

                    @block.gpsimd
                    def _(pool):
                        nc.gpsimd.memset(f32(qcat[96:128, :, :]), 0.0).then_inc(rows_zero, 1)
                        pool.wait_ge(rows_zero, 1)
                        if has_tail:
                            tail_pool(pool, 1 - s)
                        if has_head:
                            norm_in.root(pool, minus_half[:, :])

                    @block.scalar
                    def _(act):
                        for a, (scale, bias) in enumerate(((float(HD) ** -0.5, bq), (1.0, bk))):
                            for c in range(NC):
                                act.wait_ge(qk_mm, 2 * a + c + 1)
                                nc.scalar.activation(qk[:, a, c * CH:(c + 1) * CH], ps[:, 2 * a + c, :], ACT.Identity,
                                                     bias=bias[:, 0:1], scale=scale).then_inc(qk_biased, 1)
                        if has_tail:
                            tail_act(act)

                        def keys_apart(g, heads=range(GH)):
                            act.wait_ge(k_in[g], 3 * 16)
                            if g == 3:
                                act.wait_ge(s_mm, scores_done(PROBS, 0, NT - 1, GH - 1))
                            for i in heads:
                                nc.scalar.activation(kz[0:96, g % 3, i, :], k_parts[g][0:96, :], ACT.Identity,
                                                     scale=head_rows[0:96, 0, i:i + 1]).then_inc(k_ready, 1)

                        keys_apart(0)
                        act.wait_ge(v_ready, 2 * NT)
                        nc.scalar.activation(gate[s][:, :, :], gate[s][:, :, :], ACT.Sigmoid).then_inc(gate_ready, 1)
                        def place_tops(g):
                            for c in range(NC):
                                act.wait_ge(top_mm, NT * g + 4 * (c + 1))
                                nc.scalar.copy(qcat[96:128, g, c * CH:(c + 1) * CH],
                                               ps[96:128, TR + c, :]).then_inc(top_ready, 1)

                        keys_apart(1)
                        keys_apart(2)
                        place_tops(0)
                        for g in range(NG):
                            for j in range(NT):
                                n = g * NT + j
                                cols, nv = queries_of(j), BY_VECTOR[g]
                                if g == 1 and 1 <= j <= GH:
                                    keys_apart(3, (j - 1,))
                                if n >= 3:
                                    act.wait_ge(pv_mm, n - 2)
                                for i in range(nv, GH):
                                    act.wait_ge(s_mm, scores_done(PROBS, g, j, i))
                                    nc.scalar.activation(prob_of[:, n % 3, i, 0:cols], ps[:, i, 0:cols],
                                                         ACT.Exp).then_inc(prob_ready, 1)
                                act.wait_ge(bias_added, added_before(g, j) + nv)
                                nc.scalar.activation(prob_of[:, n % 3, 0:nv, 0:cols], prob_of[:, n % 3, 0:nv, 0:cols],
                                                     ACT.Exp).then_inc(prob_ready, nv)
                                if g == NG - 1 and j == 2 and has_head:
                                    head_act(act)
                            if g < NG - 1:
                                place_tops(g + 1)
                            for c in range(NC):
                                act.wait_ge(pv_mm, NT * (g + 1))
                                if g >= 1 and c == 0:
                                    act.wait_ge(back_mm, NT * g)
                                nc.scalar.copy(ot[:, c * CH:(c + 1) * CH], ps[:, 4 + c, :]).then_inc(ot_copied, 1)

                    @block.vector
                    def _(dve):
                        for n in range(2 * NC):
                            a, cols = n // NC, slice((n % NC) * CH, (n % NC + 1) * CH)
                            dve.wait_ge(qk_biased, n + 1)
                            split(nc, dve, qk_hi[:, a, cols], qk_lo[:, a, cols], qk[:, a, cols], qk_ready, 2 * n)
                        if has_tail:
                            tail_gate(dve, 1 - s)
                        for t in range(NT):
                            dve.wait_ge(vg_mm, t + 1)
                            bank = ps[:, VG_BANKS[t % 4], :]
                            nc.vector.tensor_tensor(vp[:, t, :, 0:HD], bank[:, 0:D].rearrange("p (h d) -> p h d", h=H1),
                                                    bvg_b[:, 0:D].rearrange("p (h d) -> p h d", h=H1),
                                                    ALU.add).then_inc(v_ready, 1)
                            nc.vector.tensor_tensor(gate[s][:, t, :], bank[:, D:2 * D], bvg_b[:, D:], ALU.add).then_inc(v_ready, 1)
                        if has_tail:
                            tail_z(dve)

                        def tops(g, t):
                            lo, skip = keys_of(t)
                            cols = P * (t + 1) - lo
                            for i in range(GH):
                                used = GH * (NT * g + t) + i
                                dve.wait_ge(s_mm, scores_done(TOPS, g, t, i))
                                if used >= 3:
                                    dve.wait_ge(top_taken, used - 2)
                                nc.vector.tensor_tensor_reduce(
                                    out=junk[:, used % 3, 0:cols], in0=ps[:, i, 0:cols], in1=bias_qk[:, GH * g + i, skip:WIN],
                                    scale=1.0, scalar=-FAR, op0=ALU.add, op1=ALU.max,
                                    accum_out=top[:, g % 2, t, i:i + 1]).then_inc(top_taken, 1)

                        def minus_tops(g):
                            pair = negtop[:, :, 96:96 + 2 * GH].rearrange("p t (i a) -> p t i a", a=2)
                            dve.wait_ge(top_taken, NT * GH * (g + 1))
                            if g >= 1:
                                dve.wait_ge(top_mm, NT * g)
                            nc.vector.tensor_scalar(pair[:, :, :, 0].bitcast(F32R), top[:, g % 2, :, :], -1.0, None,
                                                    ALU.mult).then_inc(top_step, 1)
                            dve.wait_ge(top_step, 2 * g + 1)
                            nc.vector.scalar_tensor_tensor(out=pair[:, :, :, 1].bitcast(F32R), in0=top[:, g % 2, :, :],
                                                           scalar=-1.0, in1=pair[:, :, :, 0], op0=ALU.mult,
                                                           op1=ALU.subtract).then_inc(top_step, 1)

                        def biases(g, j):
                            n, cols = g * NT + j, queries_of(j)
                            if n >= 3:
                                dve.wait_ge(pv_mm, n - 2)
                            for i in range(BY_VECTOR[g]):
                                dve.wait_ge(s_mm, scores_done(PROBS, g, j, i))
                                nc.vector.tensor_tensor(prob_of[:, n % 3, i, 0:cols], ps[:, i, 0:cols],
                                                        bias_kq[:, vector_heads.index(GH * g + i), 0:cols],
                                                        ALU.add).then_inc(bias_added, 1)

                        dve.wait_ge(q_in[0], 3 * 16)
                        dve.wait_ge(q_lo_in, 16 * (NG - 1))
                        for r in range(NG + 1):
                            for u in range(NT + 1):
                                if r < NG and u < NT:
                                    tops(r, u)
                                if r < NG and u == NT - 1:
                                    minus_tops(r)
                                if r >= 1 and u >= 1:
                                    biases(r - 1, u - 1)
                                if r >= 2 and u == (6 if r == NG else 4):
                                    divide(dve, r - 2, r - 2, back_mm, rden_ready, flat_ready)
                                if has_tail:
                                    tail_step(dve, 1 - s, (r - TAIL_AT[0]) * (NT + 1) + u - TAIL_AT[1])
                                if has_head:
                                    head_step(dve, 1 - s, (r - HEAD_AT[0]) * (NT + 1) + u - HEAD_AT[1], has_tail)
                                    if (r, u) == (4, 4):
                                        head_lower(dve)

                    @block.tensor
                    def _(pe):
                        def three(out, lhs, rhs):
                            pe.matmul(out, lhs[0], rhs[0], start=True, stop=False)
                            pe.matmul(out, lhs[0], rhs[1], start=False, stop=False)
                            return pe.matmul(out, lhs[1], rhs[0], start=False, stop=True)

                        for a in range(2):
                            for c in range(NC):
                                cols = slice(c * CH, (c + 1) * CH)
                                three(ps[:, 2 * a + c, :], (wqk_hi[:, a * D:(a + 1) * D], wqk_lo[:, a * D:(a + 1) * D]),
                                      (xt_hi[:, cols], xt_lo[:, cols])).then_inc(qk_mm, 1)
                        if has_tail:
                            back(pe, last_back_mm)
                        for t in range(NT):
                            toks = slice(t * P, (t + 1) * P)
                            if t >= 4:
                                pe.wait_ge(v_ready, 2 * (t - 3))
                            elif t == 2:
                                pe.wait_ge(qk_biased, 2)
                            three(ps[:, VG_BANKS[t % 4], 0:2 * D], (xt_hi[:, toks], xt_lo[:, toks]),
                                  (wvg_hi[:, :], wvg_lo[:, :])).then_inc(vg_mm, 1)
                            if t == 3 and has_tail:
                                tail_flat_t(pe)
                        if has_tail:
                            tail_out(pe)
                        pe.wait_ge(qk_biased, 2 * NC)
                        pe.wait_ge(v_ready, 2 * NT)
                        pe.wait_ge(q_in[0], 3 * 16)
                        pe.wait_ge(rows_zero, 1)

                        def bank_free(m, i):
                            kind, g, t = steps[m - 1]
                            if kind == TOPS:
                                pe.wait_ge(top_taken, GH * (NT * g + t) + i + 1)
                            elif i < BY_VECTOR[g]:
                                pe.wait_ge(bias_added, added_before(g, t) + i + 1)
                            else:
                                pe.wait_ge(prob_ready, GH * (NT * g + t) + i - BY_VECTOR[g] + 1)

                        def scores_for_tops(g, t, heads):
                            lo, _ = keys_of(t)
                            for i in heads:
                                if t == 0:
                                    pe.wait_ge(k_ready, GH * g + i + 1)
                                if place[TOPS, g, t] >= 1:
                                    bank_free(place[TOPS, g, t], i)
                                pe.matmul(ps[:, i, 0:P * (t + 1) - lo], qcat[:, g, t * P:(t + 1) * P],
                                          kz[:, g % 3, i, lo:P * (t + 1)], start=True, stop=True).then_inc(s_mm, 1)

                        def scores_for_probs(g, j, heads):
                            cols = queries_of(j)
                            for i in heads:
                                bank_free(place[PROBS, g, j], i)
                                out = ps[:, i, 0:cols]
                                by_vector = i < BY_VECTOR[g]
                                mm = pe.matmul(out, kz[:, g % 3, i, j * P:(j + 1) * P], qcat[:, g, j * P:j * P + cols],
                                               start=True, stop=by_vector)
                                if not by_vector:
                                    m = tensor_heads.index(GH * g + i)
                                    pe.matmul(out, ident_r[:, :], bias_kq_hi[:, m, 0:cols], start=False, stop=False)
                                    mm = pe.matmul(out, ident_r[:, :], bias_kq_lo[:, m, 0:cols], start=False, stop=True)
                                mm.then_inc(s_mm, 1)

                        def weighted(g, j):
                            n = g * NT + j
                            pe.wait_ge(prob_ready, GH * (n + 1))
                            if g >= 1 and j == 0:
                                pe.wait_ge(ot_copied, NC * g)
                            first, last = P * j, min(N, P * j + WIN)
                            for c in range(NC):
                                a, z_ = max(first, c * CH), min(last, (c + 1) * CH)
                                if a >= z_:
                                    continue
                                opens = j == (0 if c == 0 else (CH - WIN) // P + 1)
                                for i in range(GH):
                                    mm = pe.matmul(ps[32 * i:32 * i + 32, 4 + c, a - c * CH:z_ - c * CH],
                                                   vp[:, j, GH * g + i, :], prob_of[:, n % 3, i, a - first:z_ - first],
                                                   start=opens, stop=(j == NT - 1), skip_group_check=True)
                            mm.then_inc(pv_mm, 1)

                        for r in range(NG + 1):
                            if r == 1:
                                pe.wait_ge(q_lo_in, 16 * (NG - 1))
                                pe.wait_ge(q_in[1], 2 * 16 * (NG - 1))
                            for u in range(NT + 1):
                                if r < NG and u < NT:
                                    scores_for_tops(r, u, range(early(r, u - 1), GH))
                                if r >= 2 and u == 0:
                                    weighted(r - 2, NT - 1)
                                if r >= 1 and u == 1:
                                    pe.wait_ge(top_ready, NC * r)
                                if r >= 1 and u >= 1:
                                    scores_for_probs(r - 1, u - 1, range(BY_VECTOR[r - 1]))
                                if 1 <= r < NG and u >= 2:
                                    weighted(r - 1, u - 2)
                                if r >= 1 and u >= 1:
                                    for i in range(BY_VECTOR[r - 1], GH):
                                        scores_for_probs(r - 1, u - 1, (i,))
                                        if early(r, u):
                                            scores_for_tops(r, u + 1, (i - BY_VECTOR[r - 1],))
                                if r < NG and u == NT:
                                    pe.wait_ge(top_step, 2 * (r + 1))
                                    if r >= 2:
                                        pe.wait_ge(flat_ready, NC * (r - 1))
                                    elif r == 0 and has_tail:
                                        pe.wait_ge(z_ready, NC)
                                    for t in range(NT):
                                        pe.transpose(ps[:, TR + t // 4, (t % 4) * P:(t % 4 + 1) * P], negtop[:, t, :],
                                                     ident[:, :]).then_inc(top_mm, 1)
                                if r == NG and u >= 3:
                                    weighted(r - 1, u - 3)
                                if r == NG and u == 2 and has_head:
                                    head_pe(pe)
                                if r >= 2 and u == (5 if r == NG else 3):
                                    if r == NG and has_head:
                                        pe.wait_ge(xt_ready, NC)
                                    pe.wait_ge(ot_copied, NC * (r - 1))
                                    back(pe, back_mm)
                        weighted(NG - 1, NT - 2)
                        weighted(NG - 1, NT - 1)
            return set_up, turn, tail

        turns(nc, ctx, "wa_", program)


def build(nc, a, out):
    mid = [nc.dram_tensor(f"x_after_{i}", (B, N, D), F32).ap() for i in range(3)]
    table = nc.dram_tensor("bias_by_distance", (H1, 2, TAB), F32).ap()
    linear_attention(nc, a["x"], mid[0], a["L0_WQ"], a["L0_WK"], a["L0_WVT"], a["L0_Wfc"], a["gamma"], a["beta"],
                     a["ident"], a["headcol"], a["headsel"])
    for layer, x_in, x_out in ((0, mid[0], mid[1]), (1, mid[2], out)):
        if layer == 1:
            window_attention(nc, mid[1], mid[2], a["WqkvT"], a["bqkv"], a["WgateT"], a["bgate"], a["WoutT"], a["bout"],
                             a["pos_bias"], a["offsets"], a["ident"], a["dist"], a["head_rows"], a["turned"], table)
        w = {k: a[f"L{layer}_{k}"] for k in ("w1t", "w1s", "w2t", "w2s", "h1t", "h1s", "h2t", "h2s", "w3t", "w3s")}
        feed_forward(nc, f"ff{layer}_", x_in, x_out, c_ident=a["ident"], **w)


def constants():
    part, col = np.arange(P)[:, None], np.arange(P)[None, :]
    headcol = np.zeros((P, NF, 32), np.float32)
    headsel = np.zeros((P, NF, P), np.float32)
    for f in range(NF):
        headcol[:, f, :] = np.arange(32)[None, :] == 2 * f + part // DK
        headsel[:, f, :] = part % 32 == 2 * f + col // DK
    e = np.arange(TAB, dtype=np.float32) - P
    dist = np.concatenate([e, REACH - e])[None, :].repeat(NOFF, 0)
    head = np.arange(GH)[None, :]
    own, takes_max = (part < 96) & (part % 32 // HD == head), part // 2 == 48 + head
    head_rows = np.concatenate([own, takes_max], 1).astype(np.float32)
    return {"ident": np.eye(P, dtype=np.float32), "turned": np.eye(P, dtype=np.float32)[::-1].copy(),
            "headcol": headcol.reshape(P, -1), "headsel": headsel.reshape(P, -1),
            "dist": np.ascontiguousarray(dist), "head_rows": head_rows}


def kernel(**inputs):
    import concourse.bacc as bacc
    from concourse.bass_utils import run_bass_kernel_spmd as run

    def take(name):
        return np.ascontiguousarray(inputs[name])

    def flip(name):
        return np.ascontiguousarray(np.asarray(inputs[name]).T)

    arrays = {"x": take("L0_attn_inputs"), "L0_WQ": take("L0_attn_W_Q"), "L0_WK": take("L0_attn_W_K"),
              "L0_WVT": flip("L0_attn_W_V"), "L0_Wfc": take("L0_attn_W_fc"), "gamma": take("L0_attn_gamma"),
              "beta": take("L0_attn_beta"), "WqkvT": flip("L1_attn_Wqkv"), "bqkv": take("L1_attn_bqkv"),
              "WgateT": flip("L1_attn_Wgate"), "bgate": take("L1_attn_bgate"), "WoutT": flip("L1_attn_Wout"),
              "bout": take("L1_attn_bout"), "pos_bias": take("L1_attn_pos_bias"), "offsets": take("L1_attn_offsets")}
    for layer in (0, 1):
        for w in ("w1", "w2", "h1", "h2", "w3"):
            arrays[f"L{layer}_{w}t"] = flip(f"L{layer}_ffn_{w}_w")
            scale = take(f"L{layer}_ffn_{w}_s")
            arrays[f"L{layer}_{w}s"] = scale if w == "w3" else np.ascontiguousarray(scale.reshape(NB, P).T)
    arrays.update(constants())

    nc = bacc.Bacc("TRN2", target_bir_lowering=False, num_devices=1)
    aps = {k: nc.dram_tensor(f"in_{k}", v.shape, mybir.dt.from_np(v.dtype), kind="ExternalInput").ap()
           for k, v in arrays.items()}
    out = nc.dram_tensor("out_x", (B, N, D), F32, kind="ExternalOutput").ap()
    build(nc, aps, out)
    r = run(nc, [{f"in_{k}": v for k, v in arrays.items()}], core_ids=[0])
    return r.results[0]["out_x"]
```
